# Optimizing a Trainium2 kernel written in Bass

```python
import numpy as np
import jax
import jax.numpy as jnp

def _softmax(x, axis=-1):
    return jax.nn.softmax(x, axis=axis)

def _gelu(x):
    return jax.nn.gelu(x, approximate=True)

def _silu(x):
    return jax.nn.silu(x)

def _sigmoid(x):
    return jax.nn.sigmoid(x)

def _layernorm(x, axis=-1, eps=1e-05):
    m = jnp.mean(x, axis=axis, keepdims=True)
    v = jnp.var(x, axis=axis, keepdims=True)
    return (x - m) / jnp.sqrt(v + eps)

def _scatter_add(tgt, idx, src, axis=0):
    return tgt.at[idx].add(src)

def _segment_sum(src, seg, n):
    return jax.ops.segment_sum(src, seg, n)
kernel_name = 'mk_seq_postln_d1_jaxref_r8_73ab13'

def setup_inputs(seed: int=0):
    np.random.seed(seed)
    _w = jnp.asarray

    def _L0_attn_setup():
        import jax, jax.numpy as jnp
        import numpy as np
        HIDDEN = 256
        KEY = 256
        EPS = 1e-05
        key = jax.random.key(seed)
        k1, k2, k3 = jax.random.split(key, 3)
        B, S = (4, 256)
        x = jax.random.normal(k1, (B, S, HIDDEN), dtype=jnp.float32)
        bq = 1.0 / np.sqrt(HIDDEN)
        qkv = jax.random.uniform(k2, (HIDDEN, KEY * 3), minval=-bq, maxval=bq, dtype=jnp.float32)
        bo = 1.0 / np.sqrt(KEY)
        o_proj = jax.random.uniform(k3, (KEY, HIDDEN), minval=-bo, maxval=bo, dtype=jnp.float32)
        gamma = jnp.ones((HIDDEN,), dtype=jnp.float32)
        beta = jnp.zeros((HIDDEN,), dtype=jnp.float32)
        return {'x': x, 'qkv': qkv, 'o_proj': o_proj, 'gamma': gamma, 'beta': beta}
    _L0_attn_in = _L0_attn_setup()

    def _L0_ffn_setup():
        import jax, jax.numpy as jnp
        import numpy as np
        import math
        B, S, D = (2, 256, 256)
        H, HD = (16, 128)
        E, I = (4, 256)
        TOP_K = 2
        ROPE_THETA = 10000.0

        def _layernorm(x, w, b):
            mu = jnp.mean(x, axis=-1, keepdims=True)
            var = jnp.mean(jnp.square(x - mu), axis=-1, keepdims=True)
            return (x - mu) * jax.lax.rsqrt(var + 1e-05) * w + b

        def _rotate_half(x):
            x1, x2 = jnp.split(x, 2, axis=-1)
            return jnp.concatenate((-x2, x1), axis=-1)

        def _attention(h, wq, bq, wk, bk, wv, bv, wo, bo):
            b, s, _ = h.shape
            q = (h @ wq + bq).reshape(b, s, H, HD).transpose(0, 2, 1, 3)
            k = (h @ wk + bk).reshape(b, s, H, HD).transpose(0, 2, 1, 3)
            v = (h @ wv + bv).reshape(b, s, H, HD).transpose(0, 2, 1, 3)
            inv_freq = 1.0 / ROPE_THETA ** (jnp.arange(0, HD, 2, dtype=jnp.float32) / HD)
            freqs = jnp.arange(s, dtype=jnp.float32)[:, None] * inv_freq[None, :]
            emb = jnp.concatenate((freqs, freqs), axis=-1)
            cos = jnp.cos(emb)[None, None]
            sin = jnp.sin(emb)[None, None]
            q = q * cos + _rotate_half(q) * sin
            k = k * cos + _rotate_half(k) * sin
            scores = jnp.einsum('bhqd,bhkd->bhqk', q, k) / math.sqrt(HD)
            causal = jnp.tril(jnp.ones((s, s), bool))
            scores = jnp.where(causal[None, None], scores, jnp.finfo(jnp.float32).min)
            probs = jax.nn.softmax(scores.astype(jnp.float32), axis=-1).astype(q.dtype)
            out = jnp.einsum('bhqk,bhkd->bhqd', probs, v)
            out = out.transpose(0, 2, 1, 3).reshape(b, s, H * HD)
            return out @ wo + bo

        def _moe(h, w_gate, we1, be1, we2, be2):
            b, s, d = h.shape
            x = h.reshape(-1, d)
            t = x.shape[0]
            raw = jax.nn.softmax(x @ w_gate, axis=-1)
            top_vals, top_idx = jax.lax.top_k(raw, TOP_K)
            w = jax.nn.softmax(top_vals, axis=-1)
            comb = jnp.zeros((t, E), x.dtype).at[jnp.arange(t)[:, None], top_idx].add(w)
            hmid = jax.nn.gelu(jnp.einsum('td,edi->tei', x, we1) + be1[None], approximate=False)
            eout = jnp.einsum('tei,eid->ted', hmid, we2) + be2[None]
            out = jnp.einsum('te,ted->td', comb, eout)
            return out.reshape(b, s, d)
        key = jax.random.key(seed)
        ks = jax.random.split(key, 20)
        s = 0.02
        p = {'hidden_states': jax.random.normal(ks[0], (B, S, D), jnp.float32), 'wq': jax.random.normal(ks[1], (D, H * HD), jnp.float32) * s, 'bq': jnp.zeros((H * HD,), jnp.float32), 'wk': jax.random.normal(ks[2], (D, H * HD), jnp.float32) * s, 'bk': jnp.zeros((H * HD,), jnp.float32), 'wv': jax.random.normal(ks[3], (D, H * HD), jnp.float32) * s, 'bv': jnp.zeros((H * HD,), jnp.float32), 'wo': jax.random.normal(ks[4], (H * HD, D), jnp.float32) * s, 'bo': jnp.zeros((D,), jnp.float32), 'ln1_w': jnp.ones((D,), jnp.float32), 'ln1_b': jnp.zeros((D,), jnp.float32), 'ln2_w': jnp.ones((D,), jnp.float32), 'ln2_b': jnp.zeros((D,), jnp.float32), 'w_gate': jax.random.normal(ks[5], (D, E), jnp.float32) * s, 'we1': jax.random.normal(ks[6], (E, D, I), jnp.float32) * s, 'be1': jnp.zeros((E, I), jnp.float32), 'we2': jax.random.normal(ks[7], (E, I, D), jnp.float32) * s, 'be2': jnp.zeros((E, D), jnp.float32)}
        return p
    _L0_ffn_in = _L0_ffn_setup()
    _d = {'L0_attn_x': _L0_attn_in['x'], 'L0_attn_qkv': _L0_attn_in['qkv'], 'L0_attn_o_proj': _L0_attn_in['o_proj'], 'L0_attn_gamma': _L0_attn_in['gamma'], 'L0_attn_beta': _L0_attn_in['beta'], 'L0_ffn_wq': _L0_ffn_in['wq'], 'L0_ffn_bq': _L0_ffn_in['bq'], 'L0_ffn_wk': _L0_ffn_in['wk'], 'L0_ffn_bk': _L0_ffn_in['bk'], 'L0_ffn_wv': _L0_ffn_in['wv'], 'L0_ffn_bv': _L0_ffn_in['bv'], 'L0_ffn_wo': _L0_ffn_in['wo'], 'L0_ffn_bo': _L0_ffn_in['bo'], 'L0_ffn_ln1_w': _L0_ffn_in['ln1_w'], 'L0_ffn_ln1_b': _L0_ffn_in['ln1_b'], 'L0_ffn_ln2_w': _L0_ffn_in['ln2_w'], 'L0_ffn_ln2_b': _L0_ffn_in['ln2_b'], 'L0_ffn_w_gate': _L0_ffn_in['w_gate'], 'L0_ffn_we1': _L0_ffn_in['we1'], 'L0_ffn_be1': _L0_ffn_in['be1'], 'L0_ffn_we2': _L0_ffn_in['we2'], 'L0_ffn_be2': _L0_ffn_in['be2']}
    _x0 = _d['L0_attn_x']
    _d['L0_attn_x'] = jax.random.normal(jax.random.fold_in(jax.random.key(seed), 1), (2, 1024, 256), dtype=_x0.dtype)
    del _x0
    return _d

def reference(L0_attn_x, L0_attn_qkv, L0_attn_o_proj, L0_attn_gamma, L0_attn_beta, L0_ffn_wq, L0_ffn_bq, L0_ffn_wk, L0_ffn_bk, L0_ffn_wv, L0_ffn_bv, L0_ffn_wo, L0_ffn_bo, L0_ffn_ln1_w, L0_ffn_ln1_b, L0_ffn_ln2_w, L0_ffn_ln2_b, L0_ffn_w_gate, L0_ffn_we1, L0_ffn_be1, L0_ffn_we2, L0_ffn_be2):

    def _L0_attn_ref(x, qkv, o_proj, gamma, beta):
        import jax, jax.numpy as jnp
        import numpy as np
        HIDDEN = 256
        KEY = 256
        EPS = 1e-05
        residual = x
        mu = jnp.mean(x, axis=-1, keepdims=True)
        var = jnp.mean((x - mu) ** 2, axis=-1, keepdims=True)
        x_norm = (x - mu) / jnp.sqrt(var + EPS) * gamma + beta
        q = x_norm @ qkv[:, :KEY]
        k = x_norm @ qkv[:, KEY:2 * KEY]
        v = x_norm @ qkv[:, 2 * KEY:]
        scale = 1.0 / jnp.sqrt(jnp.float32(KEY))
        scores = jnp.einsum('bsk,btk->bst', q, k) * scale
        S_len = x.shape[1]
        causal = jnp.tril(jnp.ones((S_len, S_len), dtype=bool))
        scores = jnp.where(causal[None], scores, -jnp.inf)
        attn = jax.nn.softmax(scores, axis=-1)
        out = attn @ v
        out = out @ o_proj
        return out + residual

    def _L0_ffn_ref(hidden_states, wq, bq, wk, bk, wv, bv, wo, bo, ln1_w, ln1_b, ln2_w, ln2_b, w_gate, we1, be1, we2, be2):
        import jax, jax.numpy as jnp
        import numpy as np
        import math
        B, S, D = (2, 256, 256)
        H, HD = (16, 128)
        E, I = (4, 256)
        TOP_K = 2
        ROPE_THETA = 10000.0

        def _layernorm(x, w, b):
            mu = jnp.mean(x, axis=-1, keepdims=True)
            var = jnp.mean(jnp.square(x - mu), axis=-1, keepdims=True)
            return (x - mu) * jax.lax.rsqrt(var + 1e-05) * w + b

        def _rotate_half(x):
            x1, x2 = jnp.split(x, 2, axis=-1)
            return jnp.concatenate((-x2, x1), axis=-1)

        def _attention(h, wq, bq, wk, bk, wv, bv, wo, bo):
            b, s, _ = h.shape
            q = (h @ wq + bq).reshape(b, s, H, HD).transpose(0, 2, 1, 3)
            k = (h @ wk + bk).reshape(b, s, H, HD).transpose(0, 2, 1, 3)
            v = (h @ wv + bv).reshape(b, s, H, HD).transpose(0, 2, 1, 3)
            inv_freq = 1.0 / ROPE_THETA ** (jnp.arange(0, HD, 2, dtype=jnp.float32) / HD)
            freqs = jnp.arange(s, dtype=jnp.float32)[:, None] * inv_freq[None, :]
            emb = jnp.concatenate((freqs, freqs), axis=-1)
            cos = jnp.cos(emb)[None, None]
            sin = jnp.sin(emb)[None, None]
            q = q * cos + _rotate_half(q) * sin
            k = k * cos + _rotate_half(k) * sin
            scores = jnp.einsum('bhqd,bhkd->bhqk', q, k) / math.sqrt(HD)
            causal = jnp.tril(jnp.ones((s, s), bool))
            scores = jnp.where(causal[None, None], scores, jnp.finfo(jnp.float32).min)
            probs = jax.nn.softmax(scores.astype(jnp.float32), axis=-1).astype(q.dtype)
            out = jnp.einsum('bhqk,bhkd->bhqd', probs, v)
            out = out.transpose(0, 2, 1, 3).reshape(b, s, H * HD)
            return out @ wo + bo

        def _moe(h, w_gate, we1, be1, we2, be2):
            b, s, d = h.shape
            x = h.reshape(-1, d)
            t = x.shape[0]
            raw = jax.nn.softmax(x @ w_gate, axis=-1)
            top_vals, top_idx = jax.lax.top_k(raw, TOP_K)
            w = jax.nn.softmax(top_vals, axis=-1)
            comb = jnp.zeros((t, E), x.dtype).at[jnp.arange(t)[:, None], top_idx].add(w)
            hmid = jax.nn.gelu(jnp.einsum('td,edi->tei', x, we1) + be1[None], approximate=False)
            eout = jnp.einsum('tei,eid->ted', hmid, we2) + be2[None]
            out = jnp.einsum('te,ted->td', comb, eout)
            return out.reshape(b, s, d)
        a = _attention(_layernorm(hidden_states, ln1_w, ln1_b), wq, bq, wk, bk, wv, bv, wo, bo)
        h = hidden_states + a
        m = _moe(_layernorm(h, ln2_w, ln2_b), w_gate, we1, be1, we2, be2)
        return h + m
    x = L0_attn_x
    x = _layernorm(x + _L0_attn_ref(x, L0_attn_qkv, L0_attn_o_proj, L0_attn_gamma, L0_attn_beta), axis=-1)
    x = _layernorm(x + _L0_ffn_ref(x, L0_ffn_wq, L0_ffn_bq, L0_ffn_wk, L0_ffn_bk, L0_ffn_wv, L0_ffn_bv, L0_ffn_wo, L0_ffn_bo, L0_ffn_ln1_w, L0_ffn_ln1_b, L0_ffn_ln2_w, L0_ffn_ln2_b, L0_ffn_w_gate, L0_ffn_we1, L0_ffn_be1, L0_ffn_we2, L0_ffn_be2), axis=-1)
    return x

_drawn_inputs = setup_inputs


def setup_inputs(seed=0):
    import zlib

    import numpy as np

    out = dict(_drawn_inputs(seed))
    spreads = {'L0_attn_gamma': (1.0, 0.6),
     'L0_attn_beta': (0.0, 0.542),
     'L0_ffn_bq': (0.0, 0.8),
     'L0_ffn_bk': (0.0, 0.8),
     'L0_ffn_bv': (0.0, 0.1),
     'L0_ffn_bo': (0.0, 0.1),
     'L0_ffn_ln1_w': (1.0, 0.6),
     'L0_ffn_ln1_b': (0.0, 0.531),
     'L0_ffn_ln2_w': (1.0, 0.6),
     'L0_ffn_ln2_b': (0.0, 0.8),
     'L0_ffn_be1': (0.0, 0.8),
     'L0_ffn_be2': (0.0, 0.284)}
    factors = {'L0_ffn_wq': 8.0, 'L0_ffn_wk': 8.0, 'L0_ffn_wv': 2.768, 'L0_ffn_we1': 2.771}
    for name, (base, spread) in spreads.items():
        noise = np.random.default_rng([zlib.crc32(name.encode()), seed]).standard_normal(out[name].shape)
        drawn = base * np.exp(spread * noise) if base else spread * noise
        out[name] = jnp.asarray(drawn.astype(out[name].dtype))
    for name, factor in factors.items():
        out[name] = (out[name] * factor).astype(out[name].dtype)
    return out
```

```python
from contextlib import ExitStack

import numpy as np

import concourse.bass as bass
from concourse import mybir

F32 = mybir.dt.float32
F32R = mybir.dt.float32r
BF16 = mybir.dt.bfloat16
ALU = mybir.AluOpType
ACT = mybir.ActivationFunctionType
AX = mybir.AxisListType

P = 128
BATCH, T, D = 2, 1024, 256
NT = T // P
KD = D // P
HEADS, HD = 16, 128
PAIRS = HEADS // 2
EXPERTS, INNER = 4, 256
EPS = 1e-5
CH = 512
NC = T // CH
TC = CH // P
MASKED = -1e30
S1_SCALE = 1.0 / 16.0
HEAD_SCALE = float(1.0 / np.sqrt(HD))
THETA = 10000.0

SECTIONS = ("S1", "PRO", "BODY", "LAST", "POST")

TG0 = [0, 1, 2, 3, 4, 6, 8, 10]
TG = [[i + 1] if i < 4 else [4, i - 3] for i in range(NT)]
NTG = 12
KEYS = [[(0, 256)], [(0, 256)], [(0, 384)], [(0, 512)],
        [(0, 512), (512, 256)], [(0, 512), (512, 256)], [(0, 512), (512, 384)], [(0, 512), (512, 512)]]

QK = [("qk", h, n) for h in range(2) for n in range(4)]
def _att(h, v):
    pv = lambda c: [("pv", x, c) for x in ((0, 1) if h is None else (h,))]
    wo = lambda c: [("wo", h, c, g) for g in range(2)]
    return pv(0) + wo(0) + [("v", x) for x in v[:1]] + pv(1) + [("v", x) for x in v[1:]] + wo(1)
SHARED = {
    "S1": QK + [("v", g) for g in range(4)] + _att(None, []),
    "PRO": QK[:4] + [("v", g) for g in range(4)],
    "BODY": QK[4:] + _att(0, [0, 1]) + QK[:4] + _att(1, [2, 3]),
    "LAST": QK[4:] + _att(0, []) + _att(1, []),
    "POST": [("mid", n) for n in range(2 * 2 * EXPERTS)],
}


class Count:

    def __init__(self, sem, s1=0, pro=0, body=0, last=0, post=0, step=1, lead=0):
        self.sem, self.body, self.step, self.lead = sem, body, step, lead
        n = dict(zip(SECTIONS, (s1, pro, body * (PAIRS - 1), last, post)))
        self.first = {s: sum(n[x] for x in SECTIONS[:k]) for k, s in enumerate(SECTIONS)}
        self.batch = sum(n.values())

    def at(self, w, n):
        passed = self.lead + self.first[w.section] + n + 1
        assert passed > 0
        return w.base(self.batch * self.step, self.body * self.step) + passed * self.step


class Where:

    def __init__(self, eng, b, section, it=0):
        self.eng, self.b, self.section, self.it, self.known = eng, b, section, it, {}

    def base(self, batch, turn):
        if (batch, turn) not in self.known:
            turns = self.it * turn if self.section == "BODY" else 0
            self.known[batch, turn] = self.eng.snap(self.b * batch + turns)
        return self.known[batch, turn]

    def place(self, use):
        return SHARED[self.section].index(use)


def build(nc, A):
    with ExitStack() as ctx:
        def sb(name, shape, dt=F32):
            return ctx.enter_context(nc.sbuf_tensor(name, shape, dt))

        def counted(name, **n):
            return Count(ctx.enter_context(nc.semaphore(name)), **n)

        def sem(name):
            return ctx.enter_context(nc.semaphore(name))

        ps_s = ctx.enter_context(nc.psum_tensor("ps_s", [P, 4, 512], F32))
        ps_t = ctx.enter_context(nc.psum_tensor("ps_t", [P, 2, 512], F32))
        ps_m = ctx.enter_context(nc.psum_tensor("ps_m", [P, 2, 512], F32))

        ident = sb("ident", [P, P])
        ident_bf = sb("ident_bf", [P, P], BF16)
        mask = sb("mask", [P, P])
        mask_bf = sb("mask_bf", [P, P], BF16)
        minus_half = sb("minus_half", [P, NT])
        ones = sb("ones", [P, 1, 1])
        bias_scale = sb("bias_scale", [P, 2])
        held = sb("held", [P, 1])
        cos_t = sb("cos_t", [P, T])
        sin_t = sb("sin_t", [P, T])
        ln_w = sb("ln_w", [P, 3, KD])
        ln_b = sb("ln_b", [P, 3, KD])
        be1 = sb("be1", [P, EXPERTS, 2])
        w_gate = sb("w_gate", [P, KD, EXPERTS])
        bo = sb("bo", [P, 1, D])

        stage = sb("stage", [P, NT, D])
        rows = sb("rows", [P, NT, D])
        acc = sb("acc", [P, NT, D])
        x1 = sb("x1", [P, NT, D])
        hT_hi = sb("hT_hi", [P, KD, T], F32R)
        hT_lo = sb("hT_lo", [P, KD, T], F32R)
        q_hi = sb("q_hi", [P, 2, T], F32R)
        q_lo = sb("q_lo", [P, 2, T], F32R)
        k_hi = sb("k_hi", [P, 2, T], F32R)
        k_lo = sb("k_lo", [P, 2, T], F32R)
        v_hi = sb("v_hi", [P, NT, D], F32R)
        v_lo = sb("v_lo", [P, NT, D], F32R)
        pT_hi = sb("pT_hi", [P, NT, CH], F32R)
        pT_lo = sb("pT_lo", [P, NT, CH], F32R)
        oT_hi = sb("oT_hi", [P, 2, CH], F32R)
        oT_lo = sb("oT_lo", [P, 2, CH], F32R)
        work = sb("work", [P, 8, CH])
        qb, qs, rot, roped = (work[:, 2 * k:2 * k + 2, :] for k in range(4))
        hf = work[:, 0:4, :].rearrange("p (k c) n -> p k c n", k=KD)
        be2 = work[:, 4:6, :].rearrange("p a (e n) -> p (a e) n", n=D)
        gelu = work[:, 6:8, :]
        prob = rows[:, :, :].rearrange("p (r a) n -> p r (a n)", r=2)

        wqk_st = sb("wqk_st", [P, 2, 2, KD, HD])
        wqk_hi = sb("wqk_hi", [P, 2, 2, KD, HD], F32R)
        wqk_lo = sb("wqk_lo", [P, 2, 2, KD, HD], F32R)
        wv_st = sb("wv_st", [P, KD, 2 * HD])
        wv_hi = sb("wv_hi", [P, KD, 2 * HD], F32R)
        wv_lo = sb("wv_lo", [P, KD, 2 * HD], F32R)
        wo_st = sb("wo_st", [P, 2, D])
        wo_hi = sb("wo_hi", [P, 2, D], F32R)
        wo_lo = sb("wo_lo", [P, 2, D], F32R)
        bqk_st = sb("bqk_st", [P, 2, 2])
        bqk = sb("bqk", [P, 2, 2])
        bv = sb("bv", [P, 1, 2 * HD])

        stats = sb("stats", [P, NT, 6])
        mv = sb("mv", [P, NT, 2])
        var = sb("var", [P, NT])
        rstd = sb("rstd", [P, NT])
        nmax = sb("nmax", [P, 2, NT])
        rsum = sb("rsum", [P, 2, NT])
        rinv = sb("rinv", [P, 2, NT])
        logit = sb("logit", [P, NT, EXPERTS])
        prob4 = sb("prob4", [P, NT, EXPERTS])
        beats = sb("beats", [P, NT, EXPERTS, EXPERTS])
        rank = sb("rank", [P, NT, EXPERTS])
        is1 = sb("is1", [P, NT, EXPERTS])
        is2 = sb("is2", [P, NT, EXPERTS])
        g1 = sb("g1", [P, NT, 1])
        g2 = sb("g2", [P, NT, 1])
        g3 = sb("g3", [P, NT, 1])
        g4 = sb("g4", [P, NT, 1])
        e21 = sb("e21", [P, NT, 1])
        comb = sb("comb", [P, NT, EXPERTS])

        const_ld = sem("const_ld")
        const_done = sem("const_done")
        x_ld = counted("x_ld", s1=2, step=16)
        norm_step = counted("norm_step", s1=3, pro=6, post=6)
        norm_rstd = counted("norm_rstd", s1=1, pro=2, post=2)
        norm_rows = counted("norm_rows", s1=8, pro=16, post=16)
        norm_T = counted("norm_T", s1=4, pro=4, post=4)
        norm_f = counted("norm_f", s1=4, pro=4, post=4)
        norm_hi = counted("norm_hi", s1=4, pro=4, post=4)
        norm_lo = counted("norm_lo", s1=4, pro=4, post=4)
        added = counted("added", pro=2, post=1)
        qk_ld = [counted("qkA_ld", s1=2, pro=4, body=4, step=16),
                 counted("qkB_ld", s1=2, pro=4, body=4, step=16)]
        v_ld = counted("v_ld", s1=1, pro=2, body=2, step=16)
        wo_ld = [counted("woA_ld", s1=1, pro=1, body=1, step=16),
                 counted("woB_ld", s1=1, body=1, last=1, step=16)]
        qk_w = [counted("qkA_w", lead=1, s1=2, pro=2, body=2), counted("qkB_w", lead=1, s1=2, pro=2, body=2)]
        v_w = counted("v_w", lead=1, s1=2, pro=2, body=2)
        wo_w = [counted("woA_w", lead=1, s1=2, pro=2, body=2), counted("woB_w", lead=1, s1=2, body=2, last=2)]
        qk_mm = counted("qk_mm", lead=1, s1=8, pro=4, body=8, last=4)
        s1_hi = counted("s1_hi", s1=8)
        s1_lo = counted("s1_lo", s1=8)
        qb_done = counted("qb_done", pro=4, body=8, last=4)
        swapped = [counted("swap_even", pro=4, body=8, last=4, step=16),
                   counted("swap_odd", pro=4, body=8, last=4, step=16)]
        rot_done = counted("rot_done", pro=4, body=8, last=4)
        cos_done = counted("cos_done", pro=4, body=8, last=4)
        rope_done = counted("rope_done", pro=4, body=8, last=4)
        qk_hi_done = counted("qk_hi_done", pro=4, body=8, last=4)
        qk_lo_done = counted("qk_lo_done", pro=4, body=8, last=4)
        v_mm = counted("v_mm", lead=1, s1=4, pro=4, body=4)
        v_staged = counted("v_staged", s1=4, pro=4, body=4)
        v_split = [counted("vA_split", s1=8, pro=8, body=8), counted("vB_split", s1=8, body=8, last=8)]
        s_mm = counted("s_mm", s1=8, body=16, last=16)
        max_done = counted("max_done", s1=8, body=16, last=16)
        exp_done = counted("exp_done", s1=8, body=16, last=16)
        t_mm = counted("t_mm", s1=12, body=24, last=24)
        t_hi = counted("t_hi", s1=12, body=24, last=24)
        t_lo = counted("t_lo", s1=12, body=24, last=24)
        pv_mm = counted("pv_mm", s1=4, body=4, last=4)
        o_hi = counted("o_hi", s1=4, body=4, last=4)
        o_lo = counted("o_lo", s1=4, body=4, last=4)
        rinv_done = counted("rinv_done", s1=2, body=4, last=4)
        wo_mm = counted("wo_mm", lead=1, s1=4, body=8, last=8)
        acc_done = counted("acc_done", s1=4, body=8, last=8)
        we_ld = counted("we_ld", last=1, post=1, step=16)
        we_hi = counted("we_hi", last=1, post=1)
        we_lo = counted("we_lo", lead=1, last=1, post=1)
        be2_ld = counted("be2_ld", post=1, step=16)
        gate_mm = counted("gate_mm", post=1)
        gate_in = counted("gate_in", post=2)
        gate_exp = counted("gate_exp", post=2)
        GATE_LINKS = 23
        gate_link = counted("gate_link", post=GATE_LINKS)
        mid_mm = counted("mid_mm", post=16)
        gelu_done = counted("gelu_done", post=16)
        mid_hi = counted("mid_hi", post=16)
        mid_lo = counted("mid_lo", post=16)
        out_mm = counted("out_mm", post=16)
        mixed = counted("mixed", post=16)
        bias2 = counted("bias2", post=8)
        stored = counted("stored", lead=1, post=1, step=16)

        block = ctx.enter_context(nc.Block())
        SETUP_DMAS = 11

        @block.sync
        def _(sp):
            w_attn = A["L0_attn_qkv"]

            def first_loads():
                for dst, src in ((cos_t[:, :], A["rope_cos"]), (sin_t[:, :], A["rope_sin"])):
                    sp.dma_start(dst, src).then_inc(const_ld, 16)
                with nc.allow_non_contiguous_dma(reason="a few short vectors, once"):
                    for m, name in enumerate(("attn_gamma", "ffn_ln1_w", "ffn_ln2_w")):
                        sp.dma_start(ln_w[:, m, :], A["L0_" + name].rearrange("(k p) -> p k", p=P)).then_inc(const_ld, 16)
                    for m, name in enumerate(("attn_beta", "ffn_ln1_b", "ffn_ln2_b")):
                        sp.dma_start(ln_b[:, m, :], A["L0_" + name].rearrange("(k p) -> p k", p=P)).then_inc(const_ld, 16)
                    sp.dma_start(be1[:, :, :].rearrange("p e i -> p (e i)"),
                                 A["L0_ffn_be1"].rearrange("e (i p) -> p (e i)", p=P)).then_inc(const_ld, 16)
                    sp.dma_start(w_gate[:, :, :], A["L0_ffn_w_gate"].rearrange("(k p) e -> p k e", p=P)).then_inc(const_ld, 16)
                    sp.dma_start(bo[:, 0, :], A["L0_ffn_bo"].partition_broadcast(P)).then_inc(const_ld, 16)

            def at(offset):
                return offset if isinstance(offset, int) else sp.snap(offset)

            def load_qk(w, h, head):
                cols = bass.ds(at(head * HD), HD)
                sp.wait_ge(qk_w[h].sem, qk_w[h].at(w, -1))
                sp.dma_start(wqk_st[:, h, 0], A["L0_ffn_wq"][:, cols].rearrange("(k p) n -> p k n", p=P)).then_inc(qk_ld[h].sem, 16)
                sp.dma_start(wqk_st[:, h, 1], A["L0_ffn_wk"][:, cols].rearrange("(k p) n -> p k n", p=P)).then_inc(qk_ld[h].sem, 16)
                sp.dma_start(bqk_st[:, h, 0:1], A["L0_ffn_bq"][cols].unsqueeze(1)).then_inc(qk_ld[h].sem, 16)
                sp.dma_start(bqk_st[:, h, 1:2], A["L0_ffn_bk"][cols].unsqueeze(1)).then_inc(qk_ld[h].sem, 16)

            def load_v(w, pair):
                cols = bass.ds(at(pair * 2 * HD), 2 * HD)
                sp.wait_ge(v_staged.sem, v_staged.at(w, -1))
                sp.dma_start(wv_st[:, :, :], A["L0_ffn_wv"][:, cols].rearrange("(k p) n -> p k n", p=P)).then_inc(v_ld.sem, 16)
                sp.dma_start(bv[:, 0, :], A["L0_ffn_bv"][cols].partition_broadcast(P)).then_inc(v_ld.sem, 16)

            def load_wo(w, h, head):
                rows_ = bass.ds(at(head * HD), HD)
                sp.wait_ge(wo_w[h].sem, wo_w[h].at(w, -1))
                sp.dma_start(wo_st[:, h, :], A["L0_ffn_wo"][rows_, :]).then_inc(wo_ld[h].sem, 16)

            def swap(w, g):
                sp.wait_ge(qb_done.sem, qb_done.at(w, g))
                r = g % 2
                half = HD // 2
                sp.dma_start(qs[0:half, r, :], qb[half:HD, r, :]).then_inc(swapped[r].sem, 16)
                sp.dma_start(qs[half:HD, r, :], qb[0:half, r, :]).then_inc(swapped[r].sem, 16)

            first_loads()
            sp.sem_inc(stored.sem, 16)
            with sp.Fori(0, BATCH) as b:
                w = Where(sp, b, "S1")
                b = sp.snap(b)
                x_rows = A["L0_attn_x"][bass.ds(b, 1)].rearrange("o (t p) d -> p (o t) d", p=P)
                sp.wait_ge(we_lo.sem, we_lo.at(w, -1))
                sp.dma_start(stage[:, :, :], x_rows).then_inc(x_ld.sem, 16)
                for h in range(2):
                    sp.wait_ge(qk_w[h].sem, qk_w[h].at(w, -1))
                    for j in range(2):
                        cols = slice(j * D + h * HD, j * D + (h + 1) * HD)
                        sp.dma_start(wqk_st[:, h, j], w_attn[:, cols].rearrange("(k p) n -> p k n", p=P)).then_inc(qk_ld[h].sem, 16)
                sp.wait_ge(v_w.sem, v_w.at(w, -1))
                sp.dma_start(wv_st[:, :, :], w_attn[:, 2 * D:3 * D].rearrange("(k p) n -> p k n", p=P)).then_inc(v_ld.sem, 16)
                for h in range(2):
                    sp.wait_ge(wo_w[h].sem, wo_w[h].at(w, -1))
                    sp.dma_start(wo_st[:, h, :], A["L0_attn_o_proj"][h * P:(h + 1) * P, :]).then_inc(wo_ld[h].sem, 16)
                sp.wait_ge(v_split[1].sem, v_split[1].at(w, 7))
                sp.dma_start(stage[:, :, :], x_rows).then_inc(x_ld.sem, 16)

                w = Where(sp, b, "PRO")
                load_qk(w, 0, 0)
                load_v(w, 0)
                load_wo(w, 0, 0)
                load_qk(w, 1, 1)
                for g in range(4):
                    swap(w, g)

                with sp.Fori(0, PAIRS - 1) as it:
                    w = Where(sp, b, "BODY", it)
                    swap(w, 0)
                    swap(w, 1)
                    load_v(w, it + 1)
                    load_wo(w, 1, it * 2 + 1)
                    load_qk(w, 0, it * 2 + 2)
                    swap(w, 2)
                    swap(w, 3)
                    swap(w, 4)
                    swap(w, 5)
                    load_wo(w, 0, it * 2 + 2)
                    load_qk(w, 1, it * 2 + 3)
                    swap(w, 6)
                    swap(w, 7)

                w = Where(sp, b, "LAST")
                swap(w, 0)
                swap(w, 1)
                load_wo(w, 1, HEADS - 1)
                swap(w, 2)
                swap(w, 3)
                sp.wait_ge(v_split[1].sem, v_split[1].at(w, 7))
                sp.dma_start(stage[:, :, :].rearrange("p (e k) n -> p e k n", k=KD),
                             A["L0_ffn_we1"].rearrange("e (k p) n -> p e k n", p=P)).then_inc(we_ld.sem, 16)

                w = Where(sp, b, "POST")
                sp.wait_ge(we_lo.sem, we_lo.at(w, -1))
                sp.dma_start(stage[:, :, :].rearrange("p (e k) n -> p e k n", k=KD),
                             A["L0_ffn_we2"].rearrange("e (k p) n -> p e k n", p=P)).then_inc(we_ld.sem, 16)
                sp.wait_ge(rope_done.sem, rope_done.at(w, -1))
                sp.dma_start(be2[:, :, :], A["L0_ffn_be2"].partition_broadcast(P)).then_inc(be2_ld.sem, 16)
                out_rows = A["out"][bass.ds(b, 1)].rearrange("o (t p) d -> p (o t) d", p=P)
                sp.wait_ge(norm_rows.sem, norm_rows.at(w, 15))
                sp.dma_start(out_rows, rows[:, :, :]).then_inc(stored.sem, 16)
            sp.wait_ge(stored.sem, 16 * (stored.lead + BATCH))

        @block.gpsimd
        def _(pool):
            pool.memset(ident[:, :], 0.0)
            pool.memset(mask[:, :], 0.0)
            pool.memset(minus_half[:, :], -0.5)
            pool.memset(ones[:, :, :], 1.0)
            pool.memset(bias_scale[:, 0:1], HEAD_SCALE)
            pool.memset(bias_scale[:, 1:2], 1.0)
            pool.memset(beats[:, :, :, :], 0.0)
            pool.memset(pT_hi[:, NT - 1, 2 * P:3 * P].bitcast(F32), 0.0)
            pool.memset(pT_lo[:, NT - 1, 2 * P:3 * P].bitcast(F32), 0.0).then_inc(const_done, 1)
            pool.wait_ge(const_done, 1)
            pool.affine_select(out=ident[:, :], in_=ident[:, :], compare_op=ALU.not_equal, fill=1.0,
                               base=0, pattern=[[-1, P]], channel_multiplier=1)
            pool.affine_select(out=mask[:, :], in_=mask[:, :], compare_op=ALU.is_ge, fill=MASKED,
                               base=0, pattern=[[-1, P]], channel_multiplier=1).then_inc(const_done, 1)
            pool.wait_ge(const_done, 2)
            pool.tensor_copy(ident_bf[:, :], ident[:, :])
            pool.tensor_copy(mask_bf[:, :], mask[:, :]).then_inc(const_done, 1)

            def norm_power(w, n):
                pool.wait_ge(norm_step.sem, norm_step.at(w, 3 * n + 2))
                pool.tensor_tensor(rstd[:, :], var[:, :], minus_half[:, :], ALU.pow).then_inc(norm_rstd.sem, 1)

            def split(w, hi, lo, src, count, n):
                one = ones[:, :, :] if len(src.shape) == 3 else ones[:, :, 0]
                pool.tensor_tensor(hi, src, one.to_broadcast(src.shape), ALU.mult).then_inc(count.sem, 1)
                pool.wait_ge(count.sem, count.at(w, n))
                pool.tensor_tensor(lo, src, hi.bitcast(F32), ALU.subtract).then_inc(count.sem, 1)

            def split_qk(w, h, k, last_dma, use):
                pool.wait_ge(qk_ld[h].sem, qk_ld[h].at(w, last_dma))
                pool.wait_ge(qk_mm.sem, qk_mm.at(w, use))
                if w.section != "S1":
                    pool.tensor_tensor(bqk[:, h, :], bqk_st[:, h, :], bias_scale[:, :], ALU.mult)
                flat = "p j k n -> p (j k n)"
                split(w, wqk_hi[:, h].rearrange(flat), wqk_lo[:, h].rearrange(flat),
                      wqk_st[:, h].rearrange(flat), qk_w[h], 2 * k)

            def split_v_weights(w, last_dma, use):
                pool.wait_ge(v_ld.sem, v_ld.at(w, last_dma))
                pool.wait_ge(v_mm.sem, v_mm.at(w, use))
                flat = "p k n -> p (k n)"
                split(w, wv_hi[:, :, :].rearrange(flat), wv_lo[:, :, :].rearrange(flat),
                      wv_st[:, :, :].rearrange(flat), v_w, 0)

            def split_wo(w, h, use):
                pool.wait_ge(wo_ld[h].sem, wo_ld[h].at(w, 0))
                pool.wait_ge(wo_mm.sem, wo_mm.at(w, use))
                split(w, wo_hi[:, h], wo_lo[:, h], wo_st[:, h], wo_w[h], 0)

            def split_values(w, h, g, k):
                pool.wait_ge(v_staged.sem, v_staged.at(w, g))
                tiles, cols = slice(2 * k, 2 * k + 2), slice(h * HD, (h + 1) * HD)
                split(w, v_hi[:, tiles, cols], v_lo[:, tiles, cols], stage[:, tiles, cols], v_split[h], 2 * k)

            def rotate(w, g, c):
                pool.wait_ge(swapped[g % 2].sem, swapped[g % 2].at(w, g // 2 * 2 + 1))
                if w.section != "PRO" or g >= 2:
                    pool.wait_ge(rope_done.sem, rope_done.at(w, g - 2))
                pool.tensor_tensor(rot[:, g % 2, :], qs[:, g % 2, :], sin_t[:, c * CH:(c + 1) * CH],
                                   ALU.mult).then_inc(rot_done.sem, 1)

            def low_qk(w, g, h):
                pool.wait_ge(qk_hi_done.sem, qk_hi_done.at(w, g))
                hi, lo = ((q_hi, q_lo), (k_hi, k_lo))[g % 4 // 2]
                cols = slice(g % 2 * CH, (g % 2 + 1) * CH)
                pool.tensor_tensor(lo[:, h, cols], roped[:, g % 2, :], hi[:, h, cols].bitcast(F32),
                                   ALU.subtract).then_inc(qk_lo_done.sem, 1)

            def rope(w, g, h):
                for k in range(5):
                    if k < 4:
                        rotate(w, g + k, k % 2)
                    if k:
                        low_qk(w, g + k - 1, h)

            def low_expert(w, n):
                pool.wait_ge(we_hi.sem, we_hi.at(w, 0))
                lo = (q_lo, k_lo)[n]
                hi = (q_hi, k_hi)[n]
                pool.tensor_tensor(lo[:, :, :].rearrange("p h n -> p (h n)"), stage[:, :, :].rearrange("p t n -> p (t n)"),
                                   hi[:, :, :].rearrange("p h n -> p (h n)").bitcast(F32),
                                   ALU.subtract).then_inc(we_lo.sem, 1)

            for count in (*qk_w, v_w, *wo_w, we_lo):
                pool.sem_inc(count.sem, count.lead)
            with pool.Fori(0, BATCH) as b:
                w = Where(pool, b, "S1")
                norm_power(w, 0)
                split_qk(w, 0, 0, 1, -1)
                split_qk(w, 1, 0, 1, -1)
                split_v_weights(w, 0, -1)
                split_wo(w, 0, -1)
                split_wo(w, 1, -1)
                for k in range(4):
                    for h in range(2):
                        split_values(w, h, k, k)

                w = Where(pool, b, "PRO")
                split_qk(w, 0, 0, 3, -1)
                split_v_weights(w, 1, -1)
                norm_power(w, 0)
                norm_power(w, 1)
                split_wo(w, 0, -1)
                rope(w, 0, 0)
                for k in range(4):
                    if k == 0:
                        pool.wait_ge(pv_mm.sem, pv_mm.at(w, -1))
                    split_values(w, 0, k, k)
                split_qk(w, 1, 0, 3, -1)

                with pool.Fori(0, PAIRS - 1) as it:
                    w = Where(pool, b, "BODY", it)
                    rope(w, 0, 1)
                    pool.wait_ge(pv_mm.sem, pv_mm.at(w, -1))
                    for k in range(4):
                        split_values(w, 1, -1, k)
                    split_v_weights(w, 1, -1)
                    split_wo(w, 1, -1)
                    split_qk(w, 0, 0, 3, -1)
                    rope(w, 4, 0)
                    pool.wait_ge(pv_mm.sem, pv_mm.at(w, 1))
                    split_values(w, 0, 0, 0)
                    split_values(w, 0, 1, 1)
                    split_wo(w, 0, 3)
                    split_qk(w, 1, 0, 3, 3)
                    split_values(w, 0, 2, 2)
                    split_values(w, 0, 3, 3)

                w = Where(pool, b, "LAST")
                rope(w, 0, 1)
                pool.wait_ge(pv_mm.sem, pv_mm.at(w, -1))
                for k in range(4):
                    split_values(w, 1, -1, k)
                split_wo(w, 1, -1)
                low_expert(w, 0)

                w = Where(pool, b, "POST")
                norm_power(w, 0)
                low_expert(w, 1)
                for n in range(16):
                    pool.wait_ge(mid_hi.sem, mid_hi.at(w, n))
                    pool.tensor_tensor(pT_lo[:, n % 4, :], gelu[:, n % 2, :], pT_hi[:, n % 4, :].bitcast(F32),
                                       ALU.subtract).then_inc(mid_lo.sem, 1)
                norm_power(w, 1)

        @block.scalar
        def _(act):
            act.wait_ge(const_ld, 16 * SETUP_DMAS)

            def norm_affine(w, m):
                for u in range(4):
                    act.wait_ge(norm_T.sem, norm_T.at(w, u))
                    c, k = u // 2, u % 2
                    act.activation(hf[:, k, c, :], ps_s[:, u, :], ACT.Identity, bias=ln_b[:, m, k:k + 1],
                                   scale=ln_w[:, m, k:k + 1]).then_inc(norm_f.sem, 1)

            def high_qk_s1(w, n):
                act.wait_ge(qk_mm.sem, qk_mm.at(w, n))
                hi = (q_hi, k_hi)[n % 4 // 2]
                act.activation(hi[:, n // 4, n % 2 * CH:(n % 2 + 1) * CH], ps_m[:, n % 2, :], ACT.Identity,
                               scale=S1_SCALE if n % 4 < 2 else 1.0).then_inc(s1_hi.sem, 1)

            def add_bias(w, g, h):
                act.wait_ge(qk_mm.sem, qk_mm.at(w, g))
                if w.section != "PRO" or g >= 2:
                    act.wait_ge(rope_done.sem, rope_done.at(w, g - 2))
                j = g % 4 // 2
                act.activation(qb[:, g % 2, :], ps_m[:, w.place(("qk", h, g % 4)) % 2, :], ACT.Identity,
                               bias=bqk[:, h, j:j + 1], scale=(HEAD_SCALE, 1.0)[j]).then_inc(qb_done.sem, 1)

            def high_qk(w, g, h):
                act.wait_ge(rope_done.sem, rope_done.at(w, g))
                hi = (q_hi, k_hi)[g % 4 // 2]
                act.activation(hi[:, h, g % 2 * CH:(g % 2 + 1) * CH], roped[:, g % 2, :],
                               ACT.Copy).then_inc(qk_hi_done.sem, 1)

            def exponent(w, n, i, a):
                act.wait_ge(max_done.sem, max_done.at(w, n))
                if i >= 2:
                    act.wait_ge(t_mm.sem, t_mm.at(w, (n - i) // 8 * NTG + TG0[i - 1] - 1))
                elif w.section != "S1":
                    act.wait_ge(t_mm.sem, t_mm.at(w, (n - i) // 8 * NTG - (1 if i else 3)))
                k = (i + 1) * P
                act.activation(prob[:, i % 2, 0:k], ps_s[:, :, :].rearrange("p a n -> p (a n)")[:, i % 2 * T:i % 2 * T + k],
                               ACT.Exp, bias=nmax[:, a, i:i + 1], accum_out=rsum[:, a, i:i + 1]).then_inc(exp_done.sem, 1)

            def high_p(w, t0, i):
                for j, size in enumerate(TG[i]):
                    n = t0 + TG0[i] + j
                    act.wait_ge(t_mm.sem, t_mm.at(w, n))
                    first = 4 * j + (4 if i < 4 else 0)
                    act.activation(pT_hi[:, first:first + size, i % 4 * P:(i % 4 + 1) * P],
                                   ps_t[:, n % 2, 0:size * P].rearrange("p (j q) -> p j q", q=P),
                                   ACT.Copy).then_inc(t_hi.sem, 1)

            def high_o(w, n, h, use):
                act.wait_ge(pv_mm.sem, pv_mm.at(w, n))
                act.activation(oT_hi[:, h, :], ps_m[:, w.place(use) % 2, :], ACT.Copy).then_inc(o_hi.sem, 1)

            def attention(w, a, n0, t0, pv0, outs, rope_of, ahead):
                for i in range(NT):
                    if i + 1 < NT:
                        exponent(w, n0 + i + 1, i + 1, a)
                    elif ahead:
                        exponent(w, n0 + NT, 0, 1 - a)
                    if rope_of and i < 4:
                        add_bias(w, rope_of[0] + i, rope_of[1])
                    if rope_of and 2 <= i < 6:
                        high_qk(w, rope_of[0] + i - 2, rope_of[1])
                    if i == TC:
                        for j, (h, use) in enumerate(outs):
                            high_o(w, pv0 + j, h, ("pv", use, 0))
                    high_p(w, t0, i)
                for j, (h, use) in enumerate(outs):
                    high_o(w, pv0 + len(outs) + j, h, ("pv", use, 1))

            def high_expert(w, n):
                act.wait_ge(we_ld.sem, we_ld.at(w, 0))
                if n == 0:
                    act.wait_ge(s_mm.sem, s_mm.at(w, 15))
                hi = (q_hi, k_hi)[n]
                act.activation(hi[:, :, :].rearrange("p h n -> p (h n)"), stage[:, :, :].rearrange("p t n -> p (t n)"),
                               ACT.Copy).then_inc(we_hi.sem, 1)

            with act.Fori(0, BATCH) as b:
                w = Where(act, b, "S1")
                norm_affine(w, 0)
                for n in range(8):
                    high_qk_s1(w, n)
                exponent(w, 0, 0, 0)
                attention(w, 0, 0, 0, 0, [(0, 0), (1, 1)], None, False)

                w = Where(act, b, "PRO")
                norm_affine(w, 1)
                add_bias(w, 0, 0)
                for g in range(1, 5):
                    if g < 4:
                        add_bias(w, g, 0)
                    high_qk(w, g - 1, 0)
                exponent(w, 0, 0, 0)

                with act.Fori(0, PAIRS - 1) as it:
                    w = Where(act, b, "BODY", it)
                    attention(w, 0, 0, 0, 0, [(0, 0)], (0, 1), True)
                    attention(w, 1, 8, NTG, 2, [(1, 1)], (4, 0), True)

                w = Where(act, b, "LAST")
                attention(w, 0, 0, 0, 0, [(0, 0)], (0, 1), True)
                attention(w, 1, 8, NTG, 2, [(1, 1)], None, False)
                high_expert(w, 0)

                w = Where(act, b, "POST")
                norm_affine(w, 2)
                act.wait_ge(gate_in.sem, gate_in.at(w, 0))
                act.activation(prob4[:, :, :], logit[:, :, :], ACT.Exp).then_inc(gate_exp.sem, 1)
                act.wait_ge(gate_in.sem, gate_in.at(w, 1))
                act.activation(e21[:, :, :], g1[:, :, :], ACT.Exp).then_inc(gate_exp.sem, 1)
                high_expert(w, 1)
                for n in range(16):
                    act.wait_ge(mid_mm.sem, mid_mm.at(w, n))
                    if n >= 2:
                        act.wait_ge(mid_lo.sem, mid_lo.at(w, n - 2))
                    act.activation(gelu[:, n % 2, :], ps_m[:, n % 2, :], ACT.Gelu,
                                   bias=be1[:, n // 2 % EXPERTS, n % 2:n % 2 + 1]).then_inc(gelu_done.sem, 1)

        @block.vector
        def _(dve):
            dve.wait_ge(const_ld, 16 * SETUP_DMAS)
            dve.wait_ge(const_done, 3)

            def norm(w, n, src, dst):
                for t in range(NT):
                    last = dve.bn_stats(stats[:, t, :], src[:, t, :])
                last.then_inc(norm_step.sem, 1)
                dve.wait_ge(norm_step.sem, norm_step.at(w, 3 * n))
                dve.tensor_copy(held[:, 0:1], minus_half[:, 0:1])
                for t in range(NT):
                    last = dve.bn_aggr(mv[:, t, :], stats[:, t, :])
                last.then_inc(norm_step.sem, 1)
                dve.wait_ge(norm_step.sem, norm_step.at(w, 3 * n + 1))
                dve.tensor_scalar(var[:, :], mv[:, :, 1], EPS, None, ALU.add).then_inc(norm_step.sem, 1)
                dve.wait_ge(norm_rstd.sem, norm_rstd.at(w, n))
                for t in range(NT):
                    dve.tensor_scalar(dst[:, t, :], src[:, t, :], mv[:, t, 0:1], rstd[:, t:t + 1],
                                      ALU.subtract, ALU.mult).then_inc(norm_rows.sem, 1)

            def split_norm(w):
                for u in range(4):
                    c, k = u // 2, u % 2
                    dve.wait_ge(norm_f.sem, norm_f.at(w, u))
                    dve.tensor_copy(hT_hi[:, k, c * CH:(c + 1) * CH], hf[:, k, c, :]).then_inc(norm_hi.sem, 1)
                for u in range(4):
                    c, k = u // 2, u % 2
                    dve.wait_ge(norm_hi.sem, norm_hi.at(w, u))
                    dve.tensor_tensor(hT_lo[:, k, c * CH:(c + 1) * CH], hf[:, k, c, :],
                                      hT_hi[:, k, c * CH:(c + 1) * CH].bitcast(F32), ALU.subtract).then_inc(norm_lo.sem, 1)

            def low_qk_s1(w, n):
                dve.wait_ge(s1_hi.sem, s1_hi.at(w, n))
                hi, lo = ((q_hi, q_lo), (k_hi, k_lo))[n % 4 // 2]
                cols = slice(n % 2 * CH, (n % 2 + 1) * CH)
                dve.scalar_tensor_tensor(lo[:, n // 4, cols], ps_m[:, n % 2, :], S1_SCALE if n % 4 < 2 else 1.0,
                                         hi[:, n // 4, cols].bitcast(F32), ALU.mult,
                                         ALU.subtract).then_inc(s1_lo.sem, 1)

            def stage_values(w, g):
                dve.wait_ge(v_mm.sem, v_mm.at(w, g))
                src = ps_m[:, w.place(("v", g)) % 2, :].rearrange("p (t n) -> p t n", n=D)
                dst = stage[:, 2 * g:2 * g + 2, :]
                if w.section == "S1":
                    dve.tensor_copy(dst, src).then_inc(v_staged.sem, 1)
                else:
                    dve.tensor_tensor(dst, src, bv[:, :, :].to_broadcast([P, 2, D]), ALU.add).then_inc(v_staged.sem, 1)

            def rotate(w, g, c):
                dve.wait_ge(qb_done.sem, qb_done.at(w, g))
                if w.section != "PRO" or g >= 2:
                    dve.wait_ge(qk_lo_done.sem, qk_lo_done.at(w, g - 2))
                dve.tensor_tensor(roped[:, g % 2, :], qb[:, g % 2, :], cos_t[:, c * CH:(c + 1) * CH],
                                  ALU.mult).then_inc(cos_done.sem, 1)
                dve.wait_ge(rot_done.sem, rot_done.at(w, g))
                dve.wait_ge(cos_done.sem, cos_done.at(w, g))
                dve.tensor_tensor(roped[:, g % 2, :], roped[:, g % 2, :], rot[:, g % 2, :],
                                  ALU.add).then_inc(rope_done.sem, 1)

            def row_max(w, n, i, a):
                dve.wait_ge(s_mm.sem, s_mm.at(w, n))
                k = (i + 1) * P
                dve.tensor_reduce(nmax[:, a, i:i + 1], ps_s[:, :, :].rearrange("p a n -> p (a n)")[:, i % 2 * T:i % 2 * T + k],
                                  AX.X, ALU.max, negate=True).then_inc(max_done.sem, 1)

            def low_p(w, t0, i):
                for j, size in enumerate(TG[i]):
                    n = t0 + TG0[i] + j
                    dve.wait_ge(t_hi.sem, t_hi.at(w, n))
                    first = 4 * j + (4 if i < 4 else 0)
                    part = (slice(None), slice(first, first + size), slice(i % 4 * P, (i % 4 + 1) * P))
                    dve.tensor_tensor(pT_lo[part], ps_t[:, n % 2, 0:size * P].rearrange("p (j q) -> p j q", q=P),
                                      pT_hi[part].bitcast(F32), ALU.subtract).then_inc(t_lo.sem, 1)

            def low_o(w, n, h, use):
                dve.wait_ge(o_hi.sem, o_hi.at(w, n))
                dve.tensor_tensor(oT_lo[:, h, :], ps_m[:, w.place(use) % 2, :], oT_hi[:, h, :].bitcast(F32),
                                  ALU.subtract).then_inc(o_lo.sem, 1)

            def accumulate(w, a, c, wo0, r0, use, base):
                dve.wait_ge(exp_done.sem, exp_done.at(w, (r0 // 2) * NT + TC * c + TC - 1))
                dve.reciprocal(rinv[:, a, TC * c:TC * (c + 1)], rsum[:, a, TC * c:TC * (c + 1)]).then_inc(rinv_done.sem, 1)
                dve.wait_ge(rinv_done.sem, rinv_done.at(w, r0 + c))
                for g in range(2):
                    n = wo0 + 2 * c + g
                    dve.wait_ge(wo_mm.sem, wo_mm.at(w, n))
                    if w.section != "S1":
                        dve.wait_ge(acc_done.sem, acc_done.at(w, n - 4))
                    for t in range(2):
                        tile = TC * c + 2 * g + t
                        last = dve.scalar_tensor_tensor(
                            acc[:, tile, :], ps_m[:, w.place(("wo", use, c, g)) % 2, t * D:(t + 1) * D],
                            rinv[:, a, tile:tile + 1], base[:, tile, :], ALU.mult, ALU.add)
                    last.then_inc(acc_done.sem, 1)

            def attention(w, a, n0, t0, pv0, wo0, r0, outs, use, rope_of, values, base, ahead):
                for i in range(NT):
                    if i + 1 < NT:
                        row_max(w, n0 + i + 1, i + 1, a)
                    elif ahead:
                        row_max(w, n0 + NT, 0, 1 - a)
                    if rope_of is not None and 2 <= i < 6:
                        rotate(w, rope_of + i - 2, i % 2)
                    if i == TC:
                        for j, h in enumerate(outs):
                            low_o(w, pv0 + j, h, ("pv", h, 0))
                    if i == TC + 1:
                        accumulate(w, a, 0, wo0, r0, use, base)
                    low_p(w, t0, i)
                if values:
                    if values[0] == 0:
                        dve.wait_ge(v_split[1].sem, v_split[1].at(w, 7))
                    stage_values(w, values[0])
                for j, h in enumerate(outs):
                    low_o(w, pv0 + len(outs) + j, h, ("pv", h, 1))
                if values:
                    stage_values(w, values[1])
                accumulate(w, a, 1, wo0, r0, use, base)

            def gating(w):
                links = [0]

                def link(ins):
                    ins.then_inc(gate_link.sem, 1)
                    dve.wait_ge(gate_link.sem, gate_link.at(w, links[0]))
                    links[0] += 1

                wide = [P, NT, EXPERTS]
                link(dve.tensor_copy(logit[:, :, :], ps_t[:, 0, 0:NT * EXPERTS].rearrange("p (t e) -> p t e", e=EXPERTS)))
                link(dve.tensor_reduce(g1[:, :, :], logit[:, :, :], AX.X, ALU.max))
                dve.tensor_tensor(logit[:, :, :], logit[:, :, :], g1[:, :, :].to_broadcast(wide),
                                  ALU.subtract).then_inc(gate_in.sem, 1)
                dve.wait_ge(gate_exp.sem, gate_exp.at(w, 0))
                link(dve.tensor_reduce(g2[:, :, :], prob4[:, :, :], AX.X, ALU.add))
                link(dve.reciprocal(g3[:, :, :], g2[:, :, :]))
                link(dve.tensor_tensor(prob4[:, :, :], prob4[:, :, :], g3[:, :, :].to_broadcast(wide), ALU.mult))
                for a in range(EXPERTS):
                    if a:
                        link(dve.tensor_tensor(beats[:, :, 0:a, a], prob4[:, :, a:a + 1].to_broadcast([P, NT, a]),
                                               prob4[:, :, 0:a], ALU.is_gt))
                    if a + 1 < EXPERTS:
                        link(dve.tensor_tensor(beats[:, :, a + 1:, a], prob4[:, :, a:a + 1].to_broadcast([P, NT, EXPERTS - 1 - a]),
                                               prob4[:, :, a + 1:], ALU.is_ge))
                link(dve.tensor_reduce(rank[:, :, :], beats[:, :, :, :], AX.X, ALU.add))
                link(dve.tensor_scalar(is1[:, :, :], rank[:, :, :], 0.0, None, ALU.is_equal))
                link(dve.tensor_scalar(is2[:, :, :], rank[:, :, :], 1.0, None, ALU.is_equal))
                link(dve.tensor_tensor(rank[:, :, :], prob4[:, :, :], is2[:, :, :], ALU.mult))
                link(dve.tensor_reduce(g4[:, :, :], rank[:, :, :], AX.X, ALU.add))
                link(dve.tensor_reduce(g2[:, :, :], prob4[:, :, :], AX.X, ALU.max))
                dve.tensor_tensor(g1[:, :, :], g4[:, :, :], g2[:, :, :], ALU.subtract).then_inc(gate_in.sem, 1)
                dve.wait_ge(gate_exp.sem, gate_exp.at(w, 1))
                link(dve.tensor_scalar(g2[:, :, :], e21[:, :, :], 1.0, None, ALU.add))
                link(dve.reciprocal(g3[:, :, :], g2[:, :, :]))
                link(dve.tensor_tensor(g4[:, :, :], e21[:, :, :], g3[:, :, :], ALU.mult))
                link(dve.tensor_tensor(is1[:, :, :], is1[:, :, :], g3[:, :, :].to_broadcast(wide), ALU.mult))
                link(dve.tensor_tensor(is2[:, :, :], is2[:, :, :], g4[:, :, :].to_broadcast(wide), ALU.mult))
                link(dve.tensor_tensor(comb[:, :, :], is1[:, :, :], is2[:, :, :], ALU.add))
                assert links[0] == GATE_LINKS, links

            def high_mid(w, n):
                dve.wait_ge(gelu_done.sem, gelu_done.at(w, n))
                if n >= 4:
                    dve.wait_ge(out_mm.sem, out_mm.at(w, 2 * (n // 2 - 2) + 1))
                dve.tensor_copy(pT_hi[:, n % 4, :], gelu[:, n % 2, :]).then_inc(mid_hi.sem, 1)

            def mix(w, u):
                c, e = u // EXPERTS, u % EXPERTS
                for g in range(2):
                    n = 2 * u + g
                    dve.wait_ge(out_mm.sem, out_mm.at(w, n))
                    if u:
                        dve.wait_ge(bias2.sem, bias2.at(w, u - 1))
                    for t in range(2):
                        tile = TC * c + 2 * g + t
                        last = dve.scalar_tensor_tensor(acc[:, tile, :], ps_s[:, n % 4, t * D:(t + 1) * D],
                                                        comb[:, tile, e:e + 1], acc[:, tile, :], ALU.mult, ALU.add)
                    last.then_inc(mixed.sem, 1)
                dve.wait_ge(mixed.sem, mixed.at(w, 2 * u + 1))
                for t in range(TC):
                    tile = TC * c + t
                    last = dve.scalar_tensor_tensor(acc[:, tile, :], be2[:, e, :], comb[:, tile, e:e + 1],
                                                    acc[:, tile, :], ALU.mult, ALU.add)
                last.then_inc(bias2.sem, 1)

            with dve.Fori(0, BATCH) as b:
                w = Where(dve, b, "S1")
                dve.wait_ge(x_ld.sem, x_ld.at(w, 0))
                dve.wait_ge(stored.sem, stored.at(w, -1))
                norm(w, 0, stage, rows)
                split_norm(w)
                for n in range(8):
                    low_qk_s1(w, n)
                for g in range(4):
                    stage_values(w, g)
                row_max(w, 0, 0, 0)
                dve.wait_ge(x_ld.sem, x_ld.at(w, 1))
                attention(w, 0, 0, 0, 0, 0, 0, (0, 1), None, None, (), stage, False)

                w = Where(dve, b, "PRO")
                dve.wait_ge(acc_done.sem, acc_done.at(w, -1))
                dve.tensor_tensor(acc[:, :, :], acc[:, :, :], stage[:, :, :], ALU.add).then_inc(added.sem, 1)
                dve.wait_ge(added.sem, added.at(w, 0))
                norm(w, 0, acc, x1)
                dve.wait_ge(norm_rows.sem, norm_rows.at(w, 7))
                norm(w, 1, x1, rows)
                dve.tensor_tensor(acc[:, :, :], x1[:, :, :], bo[:, :, :].to_broadcast([P, NT, D]), ALU.add).then_inc(added.sem, 1)
                split_norm(w)
                for g in range(4):
                    rotate(w, g, g % 2)
                for g in range(4):
                    stage_values(w, g)
                dve.wait_ge(added.sem, added.at(w, 1))
                row_max(w, 0, 0, 0)

                with dve.Fori(0, PAIRS - 1) as it:
                    w = Where(dve, b, "BODY", it)
                    attention(w, 0, 0, 0, 0, 0, 0, (0,), 0, 0, (0, 1), acc, True)
                    attention(w, 1, 8, NTG, 2, 4, 2, (1,), 1, 4, (2, 3), acc, True)

                w = Where(dve, b, "LAST")
                attention(w, 0, 0, 0, 0, 0, 0, (0,), 0, 0, (), acc, True)
                attention(w, 1, 8, NTG, 2, 4, 2, (1,), 1, None, (), acc, False)

                w = Where(dve, b, "POST")
                dve.wait_ge(acc_done.sem, acc_done.at(w, -1))
                norm(w, 0, acc, rows)
                split_norm(w)
                dve.wait_ge(gate_mm.sem, gate_mm.at(w, 0))
                gating(w)
                dve.tensor_tensor(acc[:, :, :], acc[:, :, :], x1[:, :, :], ALU.add).then_inc(added.sem, 1)
                dve.wait_ge(added.sem, added.at(w, 0))
                dve.wait_ge(be2_ld.sem, be2_ld.at(w, 0))
                high_mid(w, 0)
                high_mid(w, 1)
                for u in range(8):
                    if u < 7:
                        high_mid(w, 2 * u + 2)
                        high_mid(w, 2 * u + 3)
                    mix(w, u)
                dve.wait_ge(bias2.sem, bias2.at(w, 7))
                norm(w, 1, acc, rows)

        @block.tensor
        def _(pe):
            pe.wait_ge(const_done, 3)
            pe.wait_ge(const_ld, 16 * SETUP_DMAS)

            def product(out, lhs, rhs, first, last):
                for k, (x, y) in enumerate(((0, 0), (0, 1), (1, 0))):
                    ins = pe.matmul(out, lhs[x], rhs[y], start=first and k == 0, stop=last and k == 2)
                return ins

            def norm_transpose(w, first_row):
                for u in range(4):
                    c, k = u // 2, u % 2
                    pe.wait_ge(norm_rows.sem, norm_rows.at(w, first_row + TC * (c + 1) - 1))
                    for t in range(TC):
                        last = pe.transpose(ps_s[:, u, t * P:(t + 1) * P], rows[:, TC * c + t, k * P:(k + 1) * P], ident[:, :])
                    last.then_inc(norm_T.sem, 1)

            def shared_bank(w, use):
                n = w.place(use)
                if n >= 2:
                    read, m = last_reader(w.section, n - 2)
                    pe.wait_ge(read.sem, read.at(w, m))
                elif w.section in ("BODY", "LAST"):
                    pe.wait_ge(acc_done.sem, acc_done.at(w, n - 2))
                return ps_m[:, n % 2, :]

            def last_reader(section, n):
                kind = SHARED[section][n][0]
                before = sum(u[0] == kind for u in SHARED[section][:n])
                if kind == "qk":
                    return (s1_lo if section == "S1" else qb_done), before
                return {"v": v_staged, "pv": o_lo, "wo": acc_done, "mid": gelu_done}[kind], before

            def project_qk(w, n, h, g):
                out = shared_bank(w, ("qk", h, g))
                j, c = g // 2, g % 2
                for k in range(KD):
                    last = product(out, (wqk_hi[:, h, j, k, :], wqk_lo[:, h, j, k, :]),
                                   (hT_hi[:, k, c * CH:(c + 1) * CH], hT_lo[:, k, c * CH:(c + 1) * CH]),
                                   k == 0, k == KD - 1)
                last.then_inc(qk_mm.sem, 1)

            def project_v(w, g):
                out = shared_bank(w, ("v", g))
                for t in range(2):
                    rows_ = slice((2 * g + t) * P, (2 * g + t + 1) * P)
                    for k in range(KD):
                        last = product(out[:, t * D:(t + 1) * D], (hT_hi[:, k, rows_], hT_lo[:, k, rows_]),
                                       (wv_hi[:, k, :], wv_lo[:, k, :]), k == 0, k == KD - 1)
                last.then_inc(v_mm.sem, 1)

            def scores(w, n, i, halves):
                if w.section != "S1" or i >= 2:
                    pe.wait_ge(exp_done.sem, exp_done.at(w, n - 2))
                tile = slice(i * P, (i + 1) * P)
                for piece, (k0, width) in enumerate(KEYS[i]):
                    bank = ps_s[:, i % 2 * 2 + piece, :]
                    diagonal = k0 <= i * P < k0 + width
                    for m, h in enumerate(halves):
                        last = product(bank[:, 0:width], (q_hi[:, h, tile], q_lo[:, h, tile]),
                                       (k_hi[:, h, k0:k0 + width], k_lo[:, h, k0:k0 + width]),
                                       m == 0, m == len(halves) - 1 and not diagonal)
                    if diagonal:
                        last = pe.matmul(bank[:, i * P - k0:(i + 1) * P - k0], ident_bf[:, :], mask_bf[:, :],
                                         start=False, stop=True)
                last.then_inc(s_mm.sem, 1)

            def transposes(w, n, t0, i):
                pe.wait_ge(exp_done.sem, exp_done.at(w, n))
                for j, size in enumerate(TG[i]):
                    m = t0 + TG0[i] + j
                    if w.section != "S1" or m >= 2:
                        pe.wait_ge(t_lo.sem, t_lo.at(w, m - 2))
                    for k in range(size):
                        block_ = 4 * j + k
                        last = pe.transpose(ps_t[:, m % 2, k * P:(k + 1) * P],
                                            prob[:, i % 2, block_ * P:(block_ + 1) * P], ident[:, :])
                    last.then_inc(t_mm.sem, 1)

            def outputs(w, c, h, t0):
                out = shared_bank(w, ("pv", h, c))
                pe.wait_ge(t_lo.sem, t_lo.at(w, t0 + (3, NTG - 1)[c]))
                tiles = TC * (c + 1)
                for j in range(tiles):
                    off = min(max(0, j - TC * c), 2) * P
                    slot = j + (4 if c == 0 else 0)
                    vals = slice(h * HD, (h + 1) * HD)
                    last = product(out[:, off:CH], (v_hi[:, j, vals], v_lo[:, j, vals]),
                                   (pT_hi[:, slot, off:CH], pT_lo[:, slot, off:CH]), j == 0, j == tiles - 1)
                last.then_inc(pv_mm.sem, 1)

            def out_project(w, c, halves, use, pv):
                for g in range(2):
                    out = shared_bank(w, ("wo", use, c, g))
                    if g == 0:
                        pe.wait_ge(o_lo.sem, o_lo.at(w, pv))
                    for t in range(2):
                        tile = slice((2 * g + t) * P, (2 * g + t + 1) * P)
                        for m, h in enumerate(halves):
                            last = product(out[:, t * D:(t + 1) * D], (oT_hi[:, h, tile], oT_lo[:, h, tile]),
                                           (wo_hi[:, h, :], wo_lo[:, h, :]), m == 0, m == len(halves) - 1)
                    last.then_inc(wo_mm.sem, 1)

            def attention(w, halves, use, n0, t0, pv0, fill, ends, ahead, v_ready, wo_ready):
                np_ = len(halves)
                for i in range(NT):
                    if i + 1 < NT:
                        scores(w, n0 + i + 1, i + 1, halves)
                    elif ahead:
                        ahead()
                    if fill and i < 4:
                        fill(i)
                    if i == TC:
                        v_ready(0)
                        for h in halves:
                            outputs(w, 0, h, t0)
                    if i == TC + 1:
                        wo_ready()
                        out_project(w, 0, halves, use, pv0 + np_ - 1)
                    transposes(w, n0 + i, t0, i)
                if ends:
                    pe.wait_ge(v_w.sem, v_w.at(w, 1))
                    project_v(w, ends[0])
                v_ready(1)
                for h in halves:
                    outputs(w, 1, h, t0)
                if ends:
                    project_v(w, ends[1])
                out_project(w, 1, halves, use, pv0 + 2 * np_ - 1)

            for count in (v_mm, qk_mm, wo_mm):
                pe.sem_inc(count.sem, count.lead)
            with pe.Fori(0, BATCH) as b:
                w = Where(pe, b, "S1")
                norm_transpose(w, 0)
                pe.wait_ge(norm_lo.sem, norm_lo.at(w, 3))
                for n in range(8):
                    if n % 4 == 0:
                        pe.wait_ge(qk_w[n // 4].sem, qk_w[n // 4].at(w, 1))
                    project_qk(w, n, n // 4, n % 4)
                pe.wait_ge(v_w.sem, v_w.at(w, 1))
                for g in range(4):
                    project_v(w, g)
                pe.wait_ge(s1_lo.sem, s1_lo.at(w, 7))
                scores(w, 0, 0, (0, 1))

                def s1_values(c):
                    for h in range(2):
                        pe.wait_ge(v_split[h].sem, v_split[h].at(w, 4 * c + 3))

                def s1_weights():
                    for h in range(2):
                        pe.wait_ge(wo_w[h].sem, wo_w[h].at(w, 1))

                attention(w, (0, 1), None, 0, 0, 0, None, (), None, s1_values, s1_weights)

                w = Where(pe, b, "PRO")
                norm_transpose(w, 8)
                pe.wait_ge(norm_lo.sem, norm_lo.at(w, 3))
                pe.wait_ge(qk_w[0].sem, qk_w[0].at(w, 1))
                for g in range(4):
                    project_qk(w, g, 0, g)
                pe.wait_ge(v_w.sem, v_w.at(w, 1))
                for g in range(4):
                    project_v(w, g)
                pe.wait_ge(qk_lo_done.sem, qk_lo_done.at(w, 3))
                scores(w, 0, 0, (0,))

                def pair(w, more):
                    def fill_b(i):
                        if i == 0:
                            pe.wait_ge(qk_w[1].sem, qk_w[1].at(w, -1))
                        project_qk(w, i, 1, i)

                    def fill_a(i):
                        if i == 0:
                            pe.wait_ge(qk_w[0].sem, qk_w[0].at(w, 1))
                        project_qk(w, 4 + i, 0, i)

                    def scores_b():
                        pe.wait_ge(qk_lo_done.sem, qk_lo_done.at(w, 3))
                        scores(w, 8, 0, (1,))

                    def scores_next():
                        pe.wait_ge(qk_lo_done.sem, qk_lo_done.at(w, 7))
                        scores(w, 16, 0, (0,))

                    def values_a(c):
                        pe.wait_ge(v_split[0].sem, v_split[0].at(w, -5 if c == 0 else -1))

                    attention(w, (0,), 0, 0, 0, 0, fill_b, (0, 1) if more else (), scores_b,
                              values_a, lambda: pe.wait_ge(wo_w[0].sem, wo_w[0].at(w, -1)))
                    attention(w, (1,), 1, 8, NTG, 2, fill_a if more else None, (2, 3) if more else (),
                              scores_next if more else None,
                              lambda c: pe.wait_ge(v_split[1].sem, v_split[1].at(w, 4 * c + 3)), lambda: pe.wait_ge(wo_w[1].sem, wo_w[1].at(w, 1)))

                with pe.Fori(0, PAIRS - 1) as it:
                    pair(Where(pe, b, "BODY", it), True)
                pair(Where(pe, b, "LAST"), False)

                w = Where(pe, b, "POST")
                norm_transpose(w, 0)
                pe.wait_ge(norm_lo.sem, norm_lo.at(w, 3))
                for t in range(NT):
                    for k in range(KD):
                        last = pe.matmul(ps_t[:, 0, t * EXPERTS:(t + 1) * EXPERTS],
                                         hf[:, k, t // TC, t % TC * P:(t % TC + 1) * P], w_gate[:, k, :],
                                         start=(k == 0), stop=(k == KD - 1))
                last.then_inc(gate_mm.sem, 1)
                we1 = [x[:, :, :].rearrange("p h (a n) -> p (h a) n", n=INNER) for x in (q_hi, q_lo)]
                we2 = [x[:, :, :].rearrange("p h (a n) -> p (h a) n", n=D) for x in (k_hi, k_lo)]

                def expert_in(u):
                    c, e = u // EXPERTS, u % EXPERTS
                    for i in range(2):
                        out = shared_bank(w, ("mid", 2 * u + i))
                        for k in range(KD):
                            last = product(out, [x[:, 2 * e + k, i * P:(i + 1) * P] for x in we1],
                                           (hT_hi[:, k, c * CH:(c + 1) * CH], hT_lo[:, k, c * CH:(c + 1) * CH]),
                                           k == 0, k == KD - 1)
                        last.then_inc(mid_mm.sem, 1)

                def expert_out(u):
                    e = u % EXPERTS
                    pe.wait_ge(mid_lo.sem, mid_lo.at(w, 2 * u + 1))
                    for g in range(2):
                        n = 2 * u + g
                        if n >= 4:
                            pe.wait_ge(mixed.sem, mixed.at(w, n - 4))
                        for t in range(2):
                            tile = slice((2 * g + t) * P, (2 * g + t + 1) * P)
                            for i in range(2):
                                slot = (2 * u + i) % 4
                                last = product(ps_s[:, n % 4, t * D:(t + 1) * D],
                                               (pT_hi[:, slot, tile], pT_lo[:, slot, tile]),
                                               [x[:, 2 * e + i, :] for x in we2], i == 0, i == 1)
                        last.then_inc(out_mm.sem, 1)

                pe.wait_ge(we_lo.sem, we_lo.at(w, -1))
                expert_in(0)
                for u in range(8):
                    if u < 7:
                        expert_in(u + 1)
                    if u == 0:
                        pe.wait_ge(we_lo.sem, we_lo.at(w, 0))
                    expert_out(u)


_INS = ["L0_attn_x", "L0_attn_qkv", "L0_attn_o_proj", "L0_attn_gamma", "L0_attn_beta", "L0_ffn_wq", "L0_ffn_bq",
        "L0_ffn_wk", "L0_ffn_bk", "L0_ffn_wv", "L0_ffn_bv", "L0_ffn_wo", "L0_ffn_bo", "L0_ffn_ln1_w", "L0_ffn_ln1_b",
        "L0_ffn_ln2_w", "L0_ffn_ln2_b", "L0_ffn_w_gate", "L0_ffn_we1", "L0_ffn_be1", "L0_ffn_we2", "L0_ffn_be2"]


def _rope_tables():
    inv = (np.float32(1.0) / np.float32(THETA) ** (np.arange(0, HD, 2, dtype=np.float32) / np.float32(HD))).astype(np.float32)
    angle = np.concatenate([inv, inv])[:, None] * np.arange(T, dtype=np.float32)[None, :]
    sign = np.where(np.arange(HD) < HD // 2, -1.0, 1.0).astype(np.float32)[:, None]
    return np.cos(angle).astype(np.float32), (np.sin(angle) * sign).astype(np.float32)


def kernel(**inputs):
    import concourse.bacc as bacc
    from concourse.bass_utils import run_bass_kernel_spmd

    nc = bacc.Bacc("TRN2", target_bir_lowering=False, num_devices=1, dynamic_dma_scratch_size=1024)
    arrays, dram = {}, {}
    cos, sin = _rope_tables()
    for name, a in [(n, inputs[n]) for n in _INS] + [("rope_cos", cos), ("rope_sin", sin)]:
        a = np.ascontiguousarray(a)
        arrays[f"in_{name}"] = a
        dram[name] = nc.dram_tensor(f"in_{name}", a.shape, mybir.dt.from_np(a.dtype), kind="ExternalInput").ap()
    dram["out"] = nc.dram_tensor("out_rows", (BATCH, T, D), F32, kind="ExternalOutput").ap()
    build(nc, dram)
    r = run_bass_kernel_spmd(nc, [arrays], core_ids=[0])
    return r.results[0]["out_rows"]
```

```python
from contextlib import ExitStack

import numpy as np

import concourse.bass as bass
from concourse import mybir

F32 = mybir.dt.float32
F32R = mybir.dt.float32r
BF16 = mybir.dt.bfloat16
ALU = mybir.AluOpType
ACT = mybir.ActivationFunctionType
AX = mybir.AxisListType

P = 128
BATCH, T, D = 2, 1024, 256
NT = T // P
KD = D // P
HEADS, HD = 16, 128
PAIRS = HEADS // 2
EXPERTS, INNER = 4, 256
EPS = 1e-5
CH = 512
NC = T // CH
TC = CH // P
MASKED = -1e30
S1_SCALE = 1.0 / 16.0
HEAD_SCALE = float(1.0 / np.sqrt(HD))
THETA = 10000.0

SECTIONS = ("S1", "PRO", "BODY", "LAST", "POST")

TG0 = [0, 1, 2, 3, 4, 6, 8, 10]
TG = [[i + 1] if i < 4 else [4, i - 3] for i in range(NT)]
NTG = 12
KEYS = [[(0, 256)], [(0, 256)], [(0, 384)], [(0, 512)],
        [(0, 512), (512, 256)], [(0, 512), (512, 256)], [(0, 512), (512, 384)], [(0, 512), (512, 512)]]

QK = {
    "S1": [(h, g) for h in range(2) for g in range(4)],
    "PRO": [(0, 0), (0, 2), (0, 1), (0, 3), (1, 0), (1, 2)],
    "BODY": [(1, 1), (1, 3), (0, 0), (0, 2), (0, 1), (0, 3), (1, 0), (1, 2)],
    "LAST": [(1, 1), (1, 3)],
}
QK_SLOTS = 4
QK_SLOT0 = {"PRO": 0, "BODY": len(QK["PRO"]) % QK_SLOTS, "LAST": len(QK["PRO"]) % QK_SLOTS}



def _attention_uses(h, fills, ends):
    pv = lambda c: [("pv", x, c) for x in ((0, 1) if h is None else (h,))]
    wo = lambda c: [("wo", h, c, g) for g in range(2)]
    uses = []
    for i in range(NT):
        if i == TC:
            uses += pv(0)
        if i == TC + 1:
            uses += wo(0)
        uses += fills.get(i, [])
    return uses + ends[:1] + pv(1) + ends[1:] + wo(1)


FILL_B = {0: [("qk", 1, 1)], 1: [("qk", 1, 3)]}
FILL_A = {0: [("qk", 0, 1)], 1: [("qk", 0, 3)]}
V_STEPS = {"A": (6, 7), "B": (3, 6)}
SHARED = {
    "S1": [("qk", *x) for x in QK["S1"]] + [("v", g) for g in range(4)] + _attention_uses(None, {}, []),
    "PRO": [("qk", *x) for x in QK["PRO"][:4]] + [("v", g) for g in range(4)] + [("qk", *x) for x in QK["PRO"][4:]],
    "BODY": _attention_uses(0, {**FILL_B, **{i: [("v", g)] for g, i in enumerate(V_STEPS["A"])}},
                            [("qk", 0, 0), ("qk", 0, 2)])
    + _attention_uses(1, {**FILL_A, **{i: [("v", 2 + g)] for g, i in enumerate(V_STEPS["B"])}},
                      [("qk", 1, 0), ("qk", 1, 2)]),
    "LAST": _attention_uses(0, FILL_B, []) + _attention_uses(1, {}, []),
    "POST": [("mid", n) for n in range(2 * 2 * EXPERTS)],
}


class Count:

    def __init__(self, sem, s1=0, pro=0, body=0, last=0, post=0, step=1, lead=0):
        self.sem, self.body, self.step, self.lead = sem, body, step, lead
        n = dict(zip(SECTIONS, (s1, pro, body * (PAIRS - 1), last, post)))
        self.first = {s: sum(n[x] for x in SECTIONS[:k]) for k, s in enumerate(SECTIONS)}
        self.batch = sum(n.values())

    def at(self, w, n):
        passed = self.lead + self.first[w.section] + n + 1
        assert passed > 0
        return w.base(self.batch * self.step, self.body * self.step) + passed * self.step


class Where:

    def __init__(self, eng, b, section, it=0):
        self.eng, self.b, self.section, self.it, self.known = eng, b, section, it, {}

    def base(self, batch, turn):
        if (batch, turn) not in self.known:
            turns = self.it * turn if self.section == "BODY" else 0
            self.known[batch, turn] = self.eng.snap(self.b * batch + turns)
        return self.known[batch, turn]

    def place(self, use):
        return SHARED[self.section].index(use)


def build(nc, A):
    with ExitStack() as ctx:
        def sb(name, shape, dt=F32):
            return ctx.enter_context(nc.sbuf_tensor(name, shape, dt))

        def counted(name, **n):
            return Count(ctx.enter_context(nc.semaphore(name)), **n)

        def sem(name):
            return ctx.enter_context(nc.semaphore(name))

        ps_s = ctx.enter_context(nc.psum_tensor("ps_s", [P, 4, 512], F32))
        ps_t = ctx.enter_context(nc.psum_tensor("ps_t", [P, 2, 512], F32))
        ps_m = ctx.enter_context(nc.psum_tensor("ps_m", [P, 2, 512], F32))

        ident = sb("ident", [P, P])
        ident_bf = sb("ident_bf", [P, P], BF16)
        mask = sb("mask", [P, P])
        mask_bf = sb("mask_bf", [P, P], BF16)
        minus_half = sb("minus_half", [P, NT])
        ones = sb("ones", [P, 1, 1])
        bias_scale = sb("bias_scale", [P, 2])
        held = sb("held", [P, 1])
        cos_t = sb("cos_t", [P, T])
        sin_t = sb("sin_t", [P, T])
        ln_w = sb("ln_w", [P, 3, KD])
        ln_b = sb("ln_b", [P, 3, KD])
        be1 = sb("be1", [P, EXPERTS, 2])
        w_gate = sb("w_gate", [P, KD, EXPERTS])
        bo = sb("bo", [P, 1, D])

        stage = sb("stage", [P, NT, D])
        rows = sb("rows", [P, NT, D])
        acc = sb("acc", [P, NT, D])
        x1 = sb("x1", [P, NT, D])
        hT_hi = sb("hT_hi", [P, KD, T], F32R)
        hT_lo = sb("hT_lo", [P, KD, T], F32R)
        q_hi = sb("q_hi", [P, 2, T], F32R)
        q_lo = sb("q_lo", [P, 2, T], F32R)
        k_hi = sb("k_hi", [P, 2, T], F32R)
        k_lo = sb("k_lo", [P, 2, T], F32R)
        v_hi = sb("v_hi", [P, NT, D], F32R)
        v_lo = sb("v_lo", [P, NT, D], F32R)
        pT_hi = sb("pT_hi", [P, NT, CH], F32R)
        pT_lo = sb("pT_lo", [P, NT, CH], F32R)
        oT_hi = sb("oT_hi", [P, 2, CH], F32R)
        oT_lo = sb("oT_lo", [P, 2, CH], F32R)
        work = sb("work", [P, 8, CH])
        qb, qs = work[:, 0:4, :], work[:, 4:8, :]
        hf = work[:, 0:4, :].rearrange("p (k c) n -> p k c n", k=KD)
        be2 = work[:, 4:6, :].rearrange("p a (e n) -> p (a e) n", n=D)
        gelu = work[:, 6:8, :]
        prob = rows[:, :, :].rearrange("p (r a) n -> p r (a n)", r=2)

        wqk_st = sb("wqk_st", [P, 2, 2, KD, HD])
        wqk_hi = sb("wqk_hi", [P, 2, 2, KD, HD], F32R)
        wqk_lo = sb("wqk_lo", [P, 2, 2, KD, HD], F32R)
        wv_st = sb("wv_st", [P, KD, 2 * HD])
        wv_hi = sb("wv_hi", [P, KD, 2 * HD], F32R)
        wv_lo = sb("wv_lo", [P, KD, 2 * HD], F32R)
        wo_st = sb("wo_st", [P, 2, D])
        wo_hi = sb("wo_hi", [P, 2, D], F32R)
        wo_lo = sb("wo_lo", [P, 2, D], F32R)
        bqk_st = sb("bqk_st", [P, 2, 2])
        bqk = sb("bqk", [P, 2, 2])
        bv = sb("bv", [P, 1, 2 * HD])

        stats = sb("stats", [P, NT, 6])
        mv = sb("mv", [P, NT, 2])
        var = sb("var", [P, NT])
        rstd = sb("rstd", [P, NT])
        nmax = sb("nmax", [P, 2, NT])
        rsum = sb("rsum", [P, 2, NT])
        rinv = sb("rinv", [P, 2, NT])
        logit = sb("logit", [P, NT, EXPERTS])
        prob4 = sb("prob4", [P, NT, EXPERTS])
        beats = sb("beats", [P, NT, EXPERTS, EXPERTS])
        rank = sb("rank", [P, NT, EXPERTS])
        is1 = sb("is1", [P, NT, EXPERTS])
        is2 = sb("is2", [P, NT, EXPERTS])
        g1 = sb("g1", [P, NT, 1])
        g2 = sb("g2", [P, NT, 1])
        g3 = sb("g3", [P, NT, 1])
        g4 = sb("g4", [P, NT, 1])
        e21 = sb("e21", [P, NT, 1])
        comb = sb("comb", [P, NT, EXPERTS])

        const_ld = sem("const_ld")
        const_done = sem("const_done")
        x_ld = counted("x_ld", s1=2, step=16)
        norm_step = counted("norm_step", s1=3, pro=6, post=6)
        norm_rstd = counted("norm_rstd", s1=1, pro=2, post=2)
        norm_rows = counted("norm_rows", s1=8, pro=16, post=16)
        norm_T = counted("norm_T", s1=4, pro=4, post=4)
        norm_f = counted("norm_f", s1=4, pro=4, post=4)
        norm_hi = counted("norm_hi", s1=4, pro=4, post=4)
        norm_lo = counted("norm_lo", s1=4, pro=4, post=4)
        added = counted("added", pro=2, post=1)
        qk_ld = [counted("qkA_ld", s1=2, pro=4, body=4, step=16),
                 counted("qkB_ld", s1=2, pro=4, body=4, step=16)]
        v_ld = counted("v_ld", s1=1, pro=2, body=2, step=16)
        wo_ld = [counted("woA_ld", s1=1, pro=1, body=1, step=16),
                 counted("woB_ld", s1=1, body=1, last=1, step=16)]
        qk_w_hi = [counted("qkA_w_hi", s1=1, pro=1, body=1), counted("qkB_w_hi", s1=1, pro=1, body=1)]
        qk_w = [counted("qkA_w", lead=1, s1=1, pro=1, body=1), counted("qkB_w", lead=1, s1=1, pro=1, body=1)]
        v_w_hi = counted("v_w_hi", s1=1, pro=1, body=1)
        v_w = counted("v_w", lead=1, s1=1, pro=1, body=1)
        wo_w_hi = [counted("woA_w_hi", s1=1, pro=1, body=1), counted("woB_w_hi", s1=1, body=1, last=1)]
        wo_w = [counted("woA_w", lead=1, s1=1, pro=1, body=1), counted("woB_w", lead=1, s1=1, body=1, last=1)]
        qk_mm = counted("qk_mm", lead=1, s1=8, pro=6, body=8, last=2)
        s1_hi = counted("s1_hi", s1=8)
        s1_lo = counted("s1_lo", s1=8)
        qb_done = counted("qb_done", pro=6, body=8, last=2)

        def slots(section):
            return [(QK_SLOT0[section] + n) % QK_SLOTS for n in range(len(QK[section]))]

        swapped = [counted(f"swapped_{x}", step=16, **{s.lower(): 2 * slots(s).count(x) for s in QK_SLOT0})
                   for x in range(QK_SLOTS)]
        rot_done = counted("rot_done", pro=6, body=8, last=2)
        cos_done = counted("cos_done", pro=6, body=8, last=2)
        rope_done = counted("rope_done", pro=6, body=8, last=2)
        qk_hi_done = counted("qk_hi_done", pro=6, body=8, last=2)
        qk_lo_done = counted("qk_lo_done", pro=6, body=8, last=2)

        def slot_of(w, n):
            return (QK_SLOT0[w.section] + n) % QK_SLOTS

        def group_of(w, n):
            return QK["BODY" if n < 0 else w.section][n]

        def swap_event(w, n):
            before = sum((QK_SLOT0[w.section] + m) % QK_SLOTS == slot_of(w, n) for m in range(max(n, 0)))
            return 2 * before + 1 if n >= 0 else -1

        v_mm = counted("v_mm", lead=1, s1=4, pro=4, body=4)
        v_staged = counted("v_staged", s1=4, pro=4, body=4)
        v_hi_done = [counted("vA_hi", s1=2, pro=2, body=2), counted("vB_hi", s1=2, body=2, last=2)]
        v_split = [counted("vA_split", s1=2, pro=2, body=2), counted("vB_split", s1=2, body=2, last=2)]
        s_mm = counted("s_mm", s1=8, body=16, last=16)
        max_done = counted("max_done", s1=8, body=16, last=16)
        exp_done = counted("exp_done", s1=8, body=16, last=16)
        t_mm = counted("t_mm", s1=12, body=24, last=24)
        t_hi = counted("t_hi", s1=12, body=24, last=24)
        t_lo = counted("t_lo", s1=12, body=24, last=24)
        pv_mm = counted("pv_mm", lead=1, s1=4, body=4, last=4)
        o_hi = counted("o_hi", s1=4, body=4, last=4)
        o_lo = counted("o_lo", s1=4, body=4, last=4)
        rinv_done = counted("rinv_done", s1=2, body=4, last=4)
        wo_mm = counted("wo_mm", lead=1, s1=4, body=8, last=8)
        acc_done = counted("acc_done", s1=4, body=8, last=8)
        we_ld = counted("we_ld", last=1, post=1, step=16)
        we_hi = counted("we_hi", last=1, post=1)
        we_lo = counted("we_lo", lead=1, last=1, post=1)
        be2_ld = counted("be2_ld", post=1, step=16)
        gate_mm = counted("gate_mm", post=1)
        gate_in = counted("gate_in", post=2)
        gate_exp = counted("gate_exp", post=2)
        GATE_LINKS = 23
        gate_link = counted("gate_link", post=GATE_LINKS)
        mid_mm = counted("mid_mm", post=16)
        gelu_done = counted("gelu_done", post=16)
        mid_hi = counted("mid_hi", post=16)
        mid_lo = counted("mid_lo", post=16)
        out_mm = counted("out_mm", post=16)
        mixed = counted("mixed", post=16)
        bias2 = counted("bias2", post=8)
        stored = counted("stored", lead=1, post=1, step=16)

        block = ctx.enter_context(nc.Block())
        SETUP_DMAS = 11

        @block.sync
        def _(sp):
            w_attn = A["L0_attn_qkv"]

            def first_loads():
                for dst, src in ((cos_t[:, :], A["rope_cos"]), (sin_t[:, :], A["rope_sin"])):
                    sp.dma_start(dst, src).then_inc(const_ld, 16)
                with nc.allow_non_contiguous_dma(reason="a few short vectors, once"):
                    for m, name in enumerate(("attn_gamma", "ffn_ln1_w", "ffn_ln2_w")):
                        sp.dma_start(ln_w[:, m, :], A["L0_" + name].rearrange("(k p) -> p k", p=P)).then_inc(const_ld, 16)
                    for m, name in enumerate(("attn_beta", "ffn_ln1_b", "ffn_ln2_b")):
                        sp.dma_start(ln_b[:, m, :], A["L0_" + name].rearrange("(k p) -> p k", p=P)).then_inc(const_ld, 16)
                    sp.dma_start(be1[:, :, :].rearrange("p e i -> p (e i)"),
                                 A["L0_ffn_be1"].rearrange("e (i p) -> p (e i)", p=P)).then_inc(const_ld, 16)
                    sp.dma_start(w_gate[:, :, :], A["L0_ffn_w_gate"].rearrange("(k p) e -> p k e", p=P)).then_inc(const_ld, 16)
                    sp.dma_start(bo[:, 0, :], A["L0_ffn_bo"].partition_broadcast(P)).then_inc(const_ld, 16)

            def at(offset):
                return offset if isinstance(offset, int) else sp.snap(offset)

            def load_qk(w, h, head):
                cols = bass.ds(at(head * HD), HD)
                sp.wait_ge(qk_w[h].sem, qk_w[h].at(w, -1))
                sp.dma_start(wqk_st[:, h, 0], A["L0_ffn_wq"][:, cols].rearrange("(k p) n -> p k n", p=P)).then_inc(qk_ld[h].sem, 16)
                sp.dma_start(wqk_st[:, h, 1], A["L0_ffn_wk"][:, cols].rearrange("(k p) n -> p k n", p=P)).then_inc(qk_ld[h].sem, 16)
                sp.dma_start(bqk_st[:, h, 0:1], A["L0_ffn_bq"][cols].unsqueeze(1)).then_inc(qk_ld[h].sem, 16)
                sp.dma_start(bqk_st[:, h, 1:2], A["L0_ffn_bk"][cols].unsqueeze(1)).then_inc(qk_ld[h].sem, 16)

            def load_v(w, pair):
                cols = bass.ds(at(pair * 2 * HD), 2 * HD)
                sp.wait_ge(v_staged.sem, v_staged.at(w, -1))
                sp.dma_start(wv_st[:, :, :], A["L0_ffn_wv"][:, cols].rearrange("(k p) n -> p k n", p=P)).then_inc(v_ld.sem, 16)
                sp.dma_start(bv[:, 0, :], A["L0_ffn_bv"][cols].partition_broadcast(P)).then_inc(v_ld.sem, 16)

            def load_wo(w, h, head):
                rows_ = bass.ds(at(head * HD), HD)
                sp.wait_ge(wo_w[h].sem, wo_w[h].at(w, -1))
                sp.dma_start(wo_st[:, h, :], A["L0_ffn_wo"][rows_, :]).then_inc(wo_ld[h].sem, 16)

            def swap(w, n):
                sp.wait_ge(qb_done.sem, qb_done.at(w, n))
                x = slot_of(w, n)
                half = HD // 2
                sp.dma_start(qs[0:half, x, :], qb[half:HD, x, :]).then_inc(swapped[x].sem, 16)
                sp.dma_start(qs[half:HD, x, :], qb[0:half, x, :]).then_inc(swapped[x].sem, 16)

            first_loads()
            sp.sem_inc(stored.sem, 16)
            with sp.Fori(0, BATCH) as b:
                w = Where(sp, b, "S1")
                b = sp.snap(b)
                x_rows = A["L0_attn_x"][bass.ds(b, 1)].rearrange("o (t p) d -> p (o t) d", p=P)
                sp.wait_ge(we_lo.sem, we_lo.at(w, -1))
                sp.dma_start(stage[:, :, :], x_rows).then_inc(x_ld.sem, 16)
                for h in range(2):
                    sp.wait_ge(qk_w[h].sem, qk_w[h].at(w, -1))
                    for j in range(2):
                        cols = slice(j * D + h * HD, j * D + (h + 1) * HD)
                        sp.dma_start(wqk_st[:, h, j], w_attn[:, cols].rearrange("(k p) n -> p k n", p=P)).then_inc(qk_ld[h].sem, 16)
                sp.wait_ge(v_w.sem, v_w.at(w, -1))
                sp.dma_start(wv_st[:, :, :], w_attn[:, 2 * D:3 * D].rearrange("(k p) n -> p k n", p=P)).then_inc(v_ld.sem, 16)
                for h in range(2):
                    sp.wait_ge(wo_w[h].sem, wo_w[h].at(w, -1))
                    sp.dma_start(wo_st[:, h, :], A["L0_attn_o_proj"][h * P:(h + 1) * P, :]).then_inc(wo_ld[h].sem, 16)
                sp.wait_ge(v_split[1].sem, v_split[1].at(w, 1))
                sp.dma_start(stage[:, :, :], x_rows).then_inc(x_ld.sem, 16)

                w = Where(sp, b, "PRO")
                load_qk(w, 0, 0)
                load_v(w, 0)
                load_wo(w, 0, 0)
                load_qk(w, 1, 1)
                for n in range(6):
                    swap(w, n)

                with sp.Fori(0, PAIRS - 1) as it:
                    w = Where(sp, b, "BODY", it)
                    load_v(w, it + 1)
                    load_qk(w, 0, it * 2 + 2)
                    load_wo(w, 1, it * 2 + 1)
                    for n in range(4):
                        swap(w, n)
                    load_qk(w, 1, it * 2 + 3)
                    load_wo(w, 0, it * 2 + 2)
                    for n in range(4, 8):
                        swap(w, n)

                w = Where(sp, b, "LAST")
                load_wo(w, 1, HEADS - 1)
                swap(w, 0)
                swap(w, 1)
                sp.wait_ge(v_split[1].sem, v_split[1].at(w, 1))
                sp.dma_start(stage[:, :, :].rearrange("p (e k) n -> p e k n", k=KD),
                             A["L0_ffn_we1"].rearrange("e (k p) n -> p e k n", p=P)).then_inc(we_ld.sem, 16)

                w = Where(sp, b, "POST")
                sp.wait_ge(we_lo.sem, we_lo.at(w, -1))
                sp.dma_start(stage[:, :, :].rearrange("p (e k) n -> p e k n", k=KD),
                             A["L0_ffn_we2"].rearrange("e (k p) n -> p e k n", p=P)).then_inc(we_ld.sem, 16)
                sp.wait_ge(rope_done.sem, rope_done.at(w, -1))
                sp.dma_start(be2[:, :, :], A["L0_ffn_be2"].partition_broadcast(P)).then_inc(be2_ld.sem, 16)
                out_rows = A["out"][bass.ds(b, 1)].rearrange("o (t p) d -> p (o t) d", p=P)
                sp.wait_ge(norm_rows.sem, norm_rows.at(w, 15))
                sp.dma_start(out_rows, rows[:, :, :]).then_inc(stored.sem, 16)
            sp.wait_ge(stored.sem, 16 * (stored.lead + BATCH))

        @block.gpsimd
        def _(pool):
            pool.memset(ident[:, :], 0.0)
            pool.memset(mask[:, :], 0.0)
            pool.memset(minus_half[:, :], -0.5)
            pool.memset(ones[:, :, :], 1.0)
            pool.memset(bias_scale[:, 0:1], HEAD_SCALE)
            pool.memset(bias_scale[:, 1:2], 1.0)
            pool.memset(beats[:, :, :, :], 0.0)
            pool.memset(pT_hi[:, NT - 1, 2 * P:3 * P].bitcast(F32), 0.0)
            pool.memset(pT_lo[:, NT - 1, 2 * P:3 * P].bitcast(F32), 0.0).then_inc(const_done, 1)
            pool.wait_ge(const_done, 1)
            pool.affine_select(out=ident[:, :], in_=ident[:, :], compare_op=ALU.not_equal, fill=1.0,
                               base=0, pattern=[[-1, P]], channel_multiplier=1)
            pool.affine_select(out=mask[:, :], in_=mask[:, :], compare_op=ALU.is_ge, fill=MASKED,
                               base=0, pattern=[[-1, P]], channel_multiplier=1).then_inc(const_done, 1)
            pool.wait_ge(const_done, 2)
            pool.tensor_copy(ident_bf[:, :], ident[:, :])
            pool.tensor_copy(mask_bf[:, :], mask[:, :]).then_inc(const_done, 1)

            def norm_power(w, n):
                pool.wait_ge(norm_step.sem, norm_step.at(w, 3 * n + 2))
                pool.tensor_tensor(rstd[:, :], var[:, :], minus_half[:, :], ALU.pow).then_inc(norm_rstd.sem, 1)

            def scale_biases(w, h, last_dma):
                pool.wait_ge(qk_ld[h].sem, qk_ld[h].at(w, last_dma))
                pool.tensor_tensor(bqk[:, h, :], bqk_st[:, h, :], bias_scale[:, :], ALU.mult)

            def low_qk_weights(w, h):
                pool.wait_ge(qk_w_hi[h].sem, qk_w_hi[h].at(w, 0))
                flat = "p j k n -> p (j k n)"
                pool.tensor_tensor(wqk_lo[:, h].rearrange(flat), wqk_st[:, h].rearrange(flat),
                                   wqk_hi[:, h].rearrange(flat).bitcast(F32), ALU.subtract).then_inc(qk_w[h].sem, 1)

            def low_v_weights(w):
                pool.wait_ge(v_w_hi.sem, v_w_hi.at(w, 0))
                flat = "p k n -> p (k n)"
                pool.tensor_tensor(wv_lo[:, :, :].rearrange(flat), wv_st[:, :, :].rearrange(flat),
                                   wv_hi[:, :, :].rearrange(flat).bitcast(F32), ALU.subtract).then_inc(v_w.sem, 1)

            def low_wo(w, h):
                pool.wait_ge(wo_w_hi[h].sem, wo_w_hi[h].at(w, 0))
                pool.tensor_tensor(wo_lo[:, h], wo_st[:, h], wo_hi[:, h].bitcast(F32), ALU.subtract).then_inc(wo_w[h].sem, 1)

            def low_values(w, h):
                for c in range(NC):
                    pool.wait_ge(v_hi_done[h].sem, v_hi_done[h].at(w, c))
                    tiles, cols = slice(TC * c, TC * (c + 1)), slice(h * HD, (h + 1) * HD)
                    pool.tensor_tensor(v_lo[:, tiles, cols], stage[:, tiles, cols], v_hi[:, tiles, cols].bitcast(F32),
                                       ALU.subtract).then_inc(v_split[h].sem, 1)

            def rotate(w, n):
                x = slot_of(w, n)
                pool.wait_ge(swapped[x].sem, swapped[x].at(w, swap_event(w, n)))
                c = group_of(w, n)[1] % 2
                pool.tensor_tensor(qs[:, x, :], qs[:, x, :], sin_t[:, c * CH:(c + 1) * CH],
                                   ALU.mult).then_inc(rot_done.sem, 1)

            def low_qk(w, n):
                h, g = group_of(w, n)
                pool.wait_ge(qk_hi_done.sem, qk_hi_done.at(w, n))
                hi, lo = ((q_hi, q_lo), (k_hi, k_lo))[g // 2]
                cols = slice(g % 2 * CH, (g % 2 + 1) * CH)
                pool.tensor_tensor(lo[:, h, cols], qb[:, slot_of(w, n), :], hi[:, h, cols].bitcast(F32),
                                   ALU.subtract).then_inc(qk_lo_done.sem, 1)

            def low_expert(w, n):
                pool.wait_ge(we_hi.sem, we_hi.at(w, 0))
                lo = (q_lo, k_lo)[n]
                hi = (q_hi, k_hi)[n]
                pool.tensor_tensor(lo[:, :, :].rearrange("p h n -> p (h n)"), stage[:, :, :].rearrange("p t n -> p (t n)"),
                                   hi[:, :, :].rearrange("p h n -> p (h n)").bitcast(F32),
                                   ALU.subtract).then_inc(we_lo.sem, 1)

            for count in (*qk_w, v_w, *wo_w, we_lo):
                pool.sem_inc(count.sem, count.lead)
            with pool.Fori(0, BATCH) as b:
                w = Where(pool, b, "S1")
                norm_power(w, 0)
                low_qk_weights(w, 0)
                low_qk_weights(w, 1)
                low_v_weights(w)
                low_wo(w, 0)
                low_wo(w, 1)
                low_values(w, 0)
                low_values(w, 1)

                w = Where(pool, b, "PRO")
                scale_biases(w, 0, 3)
                low_qk_weights(w, 0)
                low_v_weights(w)
                scale_biases(w, 1, 3)
                low_qk_weights(w, 1)
                norm_power(w, 0)
                norm_power(w, 1)
                low_wo(w, 0)
                rotate(w, 0)
                rotate(w, 1)
                low_qk(w, 0)
                rotate(w, 2)
                low_qk(w, 1)
                rotate(w, 3)
                low_qk(w, 2)
                low_values(w, 0)
                low_qk(w, 3)

                with pool.Fori(0, PAIRS - 1) as it:
                    w = Where(pool, b, "BODY", it)
                    rotate(w, -2)
                    rotate(w, -1)
                    low_values(w, 1)
                    rotate(w, 0)
                    low_qk(w, -2)
                    rotate(w, 1)
                    low_qk(w, -1)
                    low_v_weights(w)
                    low_qk(w, 0)
                    scale_biases(w, 0, 3)
                    low_qk_weights(w, 0)
                    low_wo(w, 1)
                    low_qk(w, 1)
                    rotate(w, 2)
                    rotate(w, 3)
                    rotate(w, 4)
                    low_qk(w, 2)
                    rotate(w, 5)
                    low_qk(w, 3)
                    low_qk(w, 4)
                    scale_biases(w, 1, 3)
                    low_qk_weights(w, 1)
                    low_values(w, 0)
                    low_wo(w, 0)
                    low_qk(w, 5)

                w = Where(pool, b, "LAST")
                rotate(w, -2)
                rotate(w, -1)
                low_values(w, 1)
                rotate(w, 0)
                low_qk(w, -2)
                rotate(w, 1)
                low_qk(w, -1)
                low_qk(w, 0)
                low_wo(w, 1)
                low_qk(w, 1)
                low_expert(w, 0)

                w = Where(pool, b, "POST")
                norm_power(w, 0)
                low_expert(w, 1)
                for n in range(16):
                    pool.wait_ge(mid_hi.sem, mid_hi.at(w, n))
                    pool.tensor_tensor(pT_lo[:, n % 4, :], gelu[:, n % 2, :], pT_hi[:, n % 4, :].bitcast(F32),
                                       ALU.subtract).then_inc(mid_lo.sem, 1)
                norm_power(w, 1)

        @block.scalar
        def _(act):
            act.wait_ge(const_ld, 16 * SETUP_DMAS)

            def norm_affine(w, m):
                for u in range(4):
                    act.wait_ge(norm_T.sem, norm_T.at(w, u))
                    c, k = u // 2, u % 2
                    act.activation(hf[:, k, c, :], ps_s[:, u, :], ACT.Identity, bias=ln_b[:, m, k:k + 1],
                                   scale=ln_w[:, m, k:k + 1]).then_inc(norm_f.sem, 1)

            def high_qk_s1(w, n):
                act.wait_ge(qk_mm.sem, qk_mm.at(w, n))
                hi = (q_hi, k_hi)[n % 4 // 2]
                act.activation(hi[:, n // 4, n % 2 * CH:(n % 2 + 1) * CH], ps_m[:, n % 2, :], ACT.Identity,
                               scale=S1_SCALE if n % 4 < 2 else 1.0).then_inc(s1_hi.sem, 1)

            def add_bias(w, n):
                h, g = group_of(w, n)
                act.wait_ge(qk_mm.sem, qk_mm.at(w, n))
                if w.section != "PRO" or n >= QK_SLOTS:
                    act.wait_ge(qk_lo_done.sem, qk_lo_done.at(w, n - QK_SLOTS))
                j = g // 2
                act.activation(qb[:, slot_of(w, n), :], ps_m[:, w.place(("qk", h, g)) % 2, :], ACT.Identity,
                               bias=bqk[:, h, j:j + 1], scale=(HEAD_SCALE, 1.0)[j]).then_inc(qb_done.sem, 1)

            def high_qk(w, n):
                h, g = group_of(w, n)
                act.wait_ge(rope_done.sem, rope_done.at(w, n))
                hi = (q_hi, k_hi)[g // 2]
                act.activation(hi[:, h, g % 2 * CH:(g % 2 + 1) * CH], qb[:, slot_of(w, n), :],
                               ACT.Copy).then_inc(qk_hi_done.sem, 1)

            def high_qk_weights(w, h, last_dma, use):
                act.wait_ge(qk_ld[h].sem, qk_ld[h].at(w, last_dma))
                act.wait_ge(qk_mm.sem, qk_mm.at(w, use))
                flat = "p j k n -> p (j k n)"
                act.activation(wqk_hi[:, h].rearrange(flat), wqk_st[:, h].rearrange(flat),
                               ACT.Copy).then_inc(qk_w_hi[h].sem, 1)

            def high_v_weights(w, last_dma):
                act.wait_ge(v_ld.sem, v_ld.at(w, last_dma))
                act.wait_ge(v_mm.sem, v_mm.at(w, -1))
                flat = "p k n -> p (k n)"
                act.activation(wv_hi[:, :, :].rearrange(flat), wv_st[:, :, :].rearrange(flat),
                               ACT.Copy).then_inc(v_w_hi.sem, 1)

            def high_wo(w, h, use):
                act.wait_ge(wo_ld[h].sem, wo_ld[h].at(w, 0))
                act.wait_ge(wo_mm.sem, wo_mm.at(w, use))
                act.activation(wo_hi[:, h], wo_st[:, h], ACT.Copy).then_inc(wo_w_hi[h].sem, 1)

            def high_values(w, h, c, staged, used):
                act.wait_ge(pv_mm.sem, pv_mm.at(w, used))
                act.wait_ge(v_staged.sem, v_staged.at(w, staged))
                tiles, cols = slice(TC * c, TC * (c + 1)), slice(h * HD, (h + 1) * HD)
                act.activation(v_hi[:, tiles, cols], stage[:, tiles, cols], ACT.Copy).then_inc(v_hi_done[h].sem, 1)

            def exponent(w, n, i, a):
                act.wait_ge(max_done.sem, max_done.at(w, n))
                if i >= 2:
                    act.wait_ge(t_mm.sem, t_mm.at(w, (n - i) // 8 * NTG + TG0[i - 1] - 1))
                elif w.section != "S1":
                    act.wait_ge(t_mm.sem, t_mm.at(w, (n - i) // 8 * NTG - (1 if i else 3)))
                k = (i + 1) * P
                act.activation(prob[:, i % 2, 0:k], ps_s[:, :, :].rearrange("p a n -> p (a n)")[:, i % 2 * T:i % 2 * T + k],
                               ACT.Exp, bias=nmax[:, a, i:i + 1], accum_out=rsum[:, a, i:i + 1]).then_inc(exp_done.sem, 1)

            def high_p(w, t0, i):
                for j, size in enumerate(TG[i]):
                    n = t0 + TG0[i] + j
                    act.wait_ge(t_mm.sem, t_mm.at(w, n))
                    first = 4 * j + (4 if i < 4 else 0)
                    act.activation(pT_hi[:, first:first + size, i % 4 * P:(i % 4 + 1) * P],
                                   ps_t[:, n % 2, 0:size * P].rearrange("p (j q) -> p j q", q=P),
                                   ACT.Copy).then_inc(t_hi.sem, 1)

            def high_o(w, n, h, use):
                act.wait_ge(pv_mm.sem, pv_mm.at(w, n))
                act.activation(oT_hi[:, h, :], ps_m[:, w.place(use) % 2, :], ACT.Copy).then_inc(o_hi.sem, 1)

            def attention(w, a, n0, t0, pv0, outs, others, ends, late, ahead):
                for i in range(NT):
                    if i + 1 < NT:
                        exponent(w, n0 + i + 1, i + 1, a)
                    elif ahead:
                        exponent(w, n0 + NT, 0, 1 - a)
                    if i == TC:
                        for j, (h, use) in enumerate(outs):
                            high_o(w, pv0 + j, h, ("pv", use, 0))
                    high_p(w, t0, i)
                    for other in others.get(i, ()):
                        other()
                for n in ends[:1]:
                    add_bias(w, n)
                if late is not None:
                    high_qk(w, late)
                for j, (h, use) in enumerate(outs):
                    high_o(w, pv0 + len(outs) + j, h, ("pv", use, 1))
                for n in ends[1:]:
                    add_bias(w, n)

            def high_expert(w, n):
                act.wait_ge(we_ld.sem, we_ld.at(w, 0))
                if n == 0:
                    act.wait_ge(s_mm.sem, s_mm.at(w, 15))
                hi = (q_hi, k_hi)[n]
                act.activation(hi[:, :, :].rearrange("p h n -> p (h n)"), stage[:, :, :].rearrange("p t n -> p (t n)"),
                               ACT.Copy).then_inc(we_hi.sem, 1)

            with act.Fori(0, BATCH) as b:
                w = Where(act, b, "S1")
                high_qk_weights(w, 0, 1, -1)
                high_qk_weights(w, 1, 1, -1)
                high_v_weights(w, 0)
                high_wo(w, 0, -1)
                high_wo(w, 1, -1)
                norm_affine(w, 0)
                for n in range(8):
                    high_qk_s1(w, n)
                exponent(w, 0, 0, 0)
                values = {c: [lambda h=h, c=c: high_values(w, h, c, 2 * c + 1, -1) for h in range(2)] for c in range(NC)}
                attention(w, 0, 0, 0, 0, [(0, 0), (1, 1)], values, (), None, False)

                w = Where(act, b, "PRO")
                high_qk_weights(w, 0, 3, -1)
                high_v_weights(w, 1)
                high_qk_weights(w, 1, 3, -1)
                high_wo(w, 0, -1)
                norm_affine(w, 1)
                add_bias(w, 0)
                for n in range(3):
                    add_bias(w, n + 1)
                    high_qk(w, n)
                high_values(w, 0, 0, 1, -1)
                high_values(w, 0, 1, 3, -1)
                high_qk(w, 3)
                exponent(w, 0, 0, 0)
                add_bias(w, 4)
                add_bias(w, 5)

                def beside_a(w, more):
                    steps = {
                        0: [lambda: add_bias(w, 0), lambda: high_values(w, 1, 0, -1, -1)],
                        1: [lambda: add_bias(w, 1), lambda: high_values(w, 1, 1, -1, -1)],
                        2: [lambda: high_qk(w, -2)],
                        3: [lambda: high_qk(w, -1)],
                        4: [lambda: high_qk(w, 0)],
                        6: [lambda: high_wo(w, 1, -1)],
                    }
                    if more:
                        steps[3].append(lambda: high_v_weights(w, 1))
                        steps[5] = [lambda: high_qk_weights(w, 0, 3, -1)]
                    return steps

                def beside_b(w):
                    return {
                        0: [lambda: add_bias(w, 4)],
                        1: [lambda: add_bias(w, 5)],
                        2: [lambda: high_qk(w, 2)],
                        3: [lambda: high_qk(w, 3)],
                        4: [lambda: high_qk(w, 4)],
                        5: [lambda: high_qk_weights(w, 1, 3, 1)],
                        6: [lambda: high_values(w, 0, 0, 1, 1)],
                        7: [lambda: high_values(w, 0, 1, 3, 1), lambda: high_wo(w, 0, 3)],
                    }

                with act.Fori(0, PAIRS - 1) as it:
                    w = Where(act, b, "BODY", it)
                    attention(w, 0, 0, 0, 0, [(0, 0)], beside_a(w, True), (2, 3), 1, True)
                    attention(w, 1, 8, NTG, 2, [(1, 1)], beside_b(w), (6, 7), 5, True)

                w = Where(act, b, "LAST")
                attention(w, 0, 0, 0, 0, [(0, 0)], beside_a(w, False), (), 1, True)
                attention(w, 1, 8, NTG, 2, [(1, 1)], {}, (), None, False)
                high_expert(w, 0)

                w = Where(act, b, "POST")
                norm_affine(w, 2)
                act.wait_ge(gate_in.sem, gate_in.at(w, 0))
                act.activation(prob4[:, :, :], logit[:, :, :], ACT.Exp).then_inc(gate_exp.sem, 1)
                act.wait_ge(gate_in.sem, gate_in.at(w, 1))
                act.activation(e21[:, :, :], g1[:, :, :], ACT.Exp).then_inc(gate_exp.sem, 1)
                high_expert(w, 1)
                for n in range(16):
                    act.wait_ge(mid_mm.sem, mid_mm.at(w, n))
                    if n >= 2:
                        act.wait_ge(mid_lo.sem, mid_lo.at(w, n - 2))
                    act.activation(gelu[:, n % 2, :], ps_m[:, n % 2, :], ACT.Gelu,
                                   bias=be1[:, n // 2 % EXPERTS, n % 2:n % 2 + 1]).then_inc(gelu_done.sem, 1)

        @block.vector
        def _(dve):
            dve.wait_ge(const_ld, 16 * SETUP_DMAS)
            dve.wait_ge(const_done, 3)

            def norm(w, n, src, dst):
                for t in range(NT):
                    last = dve.bn_stats(stats[:, t, :], src[:, t, :])
                last.then_inc(norm_step.sem, 1)
                dve.wait_ge(norm_step.sem, norm_step.at(w, 3 * n))
                dve.tensor_copy(held[:, 0:1], minus_half[:, 0:1])
                for t in range(NT):
                    last = dve.bn_aggr(mv[:, t, :], stats[:, t, :])
                last.then_inc(norm_step.sem, 1)
                dve.wait_ge(norm_step.sem, norm_step.at(w, 3 * n + 1))
                dve.tensor_scalar(var[:, :], mv[:, :, 1], EPS, None, ALU.add).then_inc(norm_step.sem, 1)
                dve.wait_ge(norm_rstd.sem, norm_rstd.at(w, n))
                for t in range(NT):
                    dve.tensor_scalar(dst[:, t, :], src[:, t, :], mv[:, t, 0:1], rstd[:, t:t + 1],
                                      ALU.subtract, ALU.mult).then_inc(norm_rows.sem, 1)

            def split_norm(w):
                for u in range(4):
                    c, k = u // 2, u % 2
                    dve.wait_ge(norm_f.sem, norm_f.at(w, u))
                    dve.tensor_copy(hT_hi[:, k, c * CH:(c + 1) * CH], hf[:, k, c, :]).then_inc(norm_hi.sem, 1)
                for u in range(4):
                    c, k = u // 2, u % 2
                    dve.wait_ge(norm_hi.sem, norm_hi.at(w, u))
                    dve.tensor_tensor(hT_lo[:, k, c * CH:(c + 1) * CH], hf[:, k, c, :],
                                      hT_hi[:, k, c * CH:(c + 1) * CH].bitcast(F32), ALU.subtract).then_inc(norm_lo.sem, 1)

            def low_qk_s1(w, n):
                dve.wait_ge(s1_hi.sem, s1_hi.at(w, n))
                hi, lo = ((q_hi, q_lo), (k_hi, k_lo))[n % 4 // 2]
                cols = slice(n % 2 * CH, (n % 2 + 1) * CH)
                dve.scalar_tensor_tensor(lo[:, n // 4, cols], ps_m[:, n % 2, :], S1_SCALE if n % 4 < 2 else 1.0,
                                         hi[:, n // 4, cols].bitcast(F32), ALU.mult,
                                         ALU.subtract).then_inc(s1_lo.sem, 1)

            def stage_values(w, g):
                dve.wait_ge(v_mm.sem, v_mm.at(w, g))
                src = ps_m[:, w.place(("v", g)) % 2, :].rearrange("p (t n) -> p t n", n=D)
                dst = stage[:, 2 * g:2 * g + 2, :]
                if w.section == "S1":
                    dve.tensor_copy(dst, src).then_inc(v_staged.sem, 1)
                else:
                    dve.tensor_tensor(dst, src, bv[:, :, :].to_broadcast([P, 2, D]), ALU.add).then_inc(v_staged.sem, 1)

            def rotate(w, n):
                x, c = slot_of(w, n), group_of(w, n)[1] % 2
                dve.wait_ge(rot_done.sem, rot_done.at(w, n))
                dve.tensor_tensor(qb[:, x, :], qb[:, x, :], cos_t[:, c * CH:(c + 1) * CH],
                                  ALU.mult).then_inc(cos_done.sem, 1)
                dve.wait_ge(cos_done.sem, cos_done.at(w, n))
                dve.tensor_tensor(qb[:, x, :], qb[:, x, :], qs[:, x, :], ALU.add).then_inc(rope_done.sem, 1)

            def row_max(w, n, i, a):
                dve.wait_ge(s_mm.sem, s_mm.at(w, n))
                k = (i + 1) * P
                dve.tensor_reduce(nmax[:, a, i:i + 1], ps_s[:, :, :].rearrange("p a n -> p (a n)")[:, i % 2 * T:i % 2 * T + k],
                                  AX.X, ALU.max, negate=True).then_inc(max_done.sem, 1)

            def low_p(w, t0, i):
                for j, size in enumerate(TG[i]):
                    n = t0 + TG0[i] + j
                    dve.wait_ge(t_hi.sem, t_hi.at(w, n))
                    first = 4 * j + (4 if i < 4 else 0)
                    part = (slice(None), slice(first, first + size), slice(i % 4 * P, (i % 4 + 1) * P))
                    dve.tensor_tensor(pT_lo[part], ps_t[:, n % 2, 0:size * P].rearrange("p (j q) -> p j q", q=P),
                                      pT_hi[part].bitcast(F32), ALU.subtract).then_inc(t_lo.sem, 1)

            def low_o(w, n, h, use):
                dve.wait_ge(o_hi.sem, o_hi.at(w, n))
                dve.tensor_tensor(oT_lo[:, h, :], ps_m[:, w.place(use) % 2, :], oT_hi[:, h, :].bitcast(F32),
                                  ALU.subtract).then_inc(o_lo.sem, 1)

            def accumulate(w, a, c, wo0, r0, use, base):
                dve.wait_ge(exp_done.sem, exp_done.at(w, (r0 // 2) * NT + TC * c + TC - 1))
                dve.reciprocal(rinv[:, a, TC * c:TC * (c + 1)], rsum[:, a, TC * c:TC * (c + 1)]).then_inc(rinv_done.sem, 1)
                dve.wait_ge(rinv_done.sem, rinv_done.at(w, r0 + c))
                if w.section == "S1":
                    dve.wait_ge(x_ld.sem, x_ld.at(w, 1))
                for g in range(2):
                    n = wo0 + 2 * c + g
                    dve.wait_ge(wo_mm.sem, wo_mm.at(w, n))
                    if w.section != "S1":
                        dve.wait_ge(acc_done.sem, acc_done.at(w, n - 4))
                    for t in range(2):
                        tile = TC * c + 2 * g + t
                        last = dve.scalar_tensor_tensor(
                            acc[:, tile, :], ps_m[:, w.place(("wo", use, c, g)) % 2, t * D:(t + 1) * D],
                            rinv[:, a, tile:tile + 1], base[:, tile, :], ALU.mult, ALU.add)
                    last.then_inc(acc_done.sem, 1)

            def attention(w, a, n0, t0, pv0, wo0, r0, outs, use, ropes, values, base, ahead):
                for i in range(NT):
                    if i + 2 < NT:
                        row_max(w, n0 + i + 2, i + 2, a)
                    elif ahead:
                        row_max(w, n0 + i + 2, i + 2 - NT, 1 - a)
                    if i == TC:
                        for j, h in enumerate(outs):
                            low_o(w, pv0 + j, h, ("pv", h, 0))
                    if i == TC + 1:
                        accumulate(w, a, 0, wo0, r0, use, base)
                    low_p(w, t0, i)
                    if i in ropes:
                        rotate(w, ropes[i])
                    if i in values:
                        if values[i] == 0:
                            dve.wait_ge(v_split[1].sem, v_split[1].at(w, 1))
                        stage_values(w, values[i])
                for j, h in enumerate(outs):
                    low_o(w, pv0 + len(outs) + j, h, ("pv", h, 1))
                accumulate(w, a, 1, wo0, r0, use, base)

            def gating(w):
                links = [0]

                def link(ins):
                    ins.then_inc(gate_link.sem, 1)
                    dve.wait_ge(gate_link.sem, gate_link.at(w, links[0]))
                    links[0] += 1

                wide = [P, NT, EXPERTS]
                link(dve.tensor_copy(logit[:, :, :], ps_t[:, 0, 0:NT * EXPERTS].rearrange("p (t e) -> p t e", e=EXPERTS)))
                link(dve.tensor_reduce(g1[:, :, :], logit[:, :, :], AX.X, ALU.max))
                dve.tensor_tensor(logit[:, :, :], logit[:, :, :], g1[:, :, :].to_broadcast(wide),
                                  ALU.subtract).then_inc(gate_in.sem, 1)
                dve.wait_ge(gate_exp.sem, gate_exp.at(w, 0))
                link(dve.tensor_reduce(g2[:, :, :], prob4[:, :, :], AX.X, ALU.add))
                link(dve.reciprocal(g3[:, :, :], g2[:, :, :]))
                link(dve.tensor_tensor(prob4[:, :, :], prob4[:, :, :], g3[:, :, :].to_broadcast(wide), ALU.mult))
                for a in range(EXPERTS):
                    if a:
                        link(dve.tensor_tensor(beats[:, :, 0:a, a], prob4[:, :, a:a + 1].to_broadcast([P, NT, a]),
                                               prob4[:, :, 0:a], ALU.is_gt))
                    if a + 1 < EXPERTS:
                        link(dve.tensor_tensor(beats[:, :, a + 1:, a], prob4[:, :, a:a + 1].to_broadcast([P, NT, EXPERTS - 1 - a]),
                                               prob4[:, :, a + 1:], ALU.is_ge))
                link(dve.tensor_reduce(rank[:, :, :], beats[:, :, :, :], AX.X, ALU.add))
                link(dve.tensor_scalar(is1[:, :, :], rank[:, :, :], 0.0, None, ALU.is_equal))
                link(dve.tensor_scalar(is2[:, :, :], rank[:, :, :], 1.0, None, ALU.is_equal))
                link(dve.tensor_tensor(rank[:, :, :], prob4[:, :, :], is2[:, :, :], ALU.mult))
                link(dve.tensor_reduce(g4[:, :, :], rank[:, :, :], AX.X, ALU.add))
                link(dve.tensor_reduce(g2[:, :, :], prob4[:, :, :], AX.X, ALU.max))
                dve.tensor_tensor(g1[:, :, :], g4[:, :, :], g2[:, :, :], ALU.subtract).then_inc(gate_in.sem, 1)
                dve.wait_ge(gate_exp.sem, gate_exp.at(w, 1))
                link(dve.tensor_scalar(g2[:, :, :], e21[:, :, :], 1.0, None, ALU.add))
                link(dve.reciprocal(g3[:, :, :], g2[:, :, :]))
                link(dve.tensor_tensor(g4[:, :, :], e21[:, :, :], g3[:, :, :], ALU.mult))
                link(dve.tensor_tensor(is1[:, :, :], is1[:, :, :], g3[:, :, :].to_broadcast(wide), ALU.mult))
                link(dve.tensor_tensor(is2[:, :, :], is2[:, :, :], g4[:, :, :].to_broadcast(wide), ALU.mult))
                link(dve.tensor_tensor(comb[:, :, :], is1[:, :, :], is2[:, :, :], ALU.add))
                assert links[0] == GATE_LINKS, links

            def high_mid(w, n):
                dve.wait_ge(gelu_done.sem, gelu_done.at(w, n))
                if n >= 4:
                    dve.wait_ge(out_mm.sem, out_mm.at(w, 2 * (n // 2 - 2) + 1))
                dve.tensor_copy(pT_hi[:, n % 4, :], gelu[:, n % 2, :]).then_inc(mid_hi.sem, 1)

            def mix(w, u):
                c, e = u // EXPERTS, u % EXPERTS
                for g in range(2):
                    n = 2 * u + g
                    dve.wait_ge(out_mm.sem, out_mm.at(w, n))
                    if u:
                        dve.wait_ge(bias2.sem, bias2.at(w, u - 1))
                    for t in range(2):
                        tile = TC * c + 2 * g + t
                        last = dve.scalar_tensor_tensor(acc[:, tile, :], ps_s[:, n % 4, t * D:(t + 1) * D],
                                                        comb[:, tile, e:e + 1], acc[:, tile, :], ALU.mult, ALU.add)
                    last.then_inc(mixed.sem, 1)
                dve.wait_ge(mixed.sem, mixed.at(w, 2 * u + 1))
                for t in range(TC):
                    tile = TC * c + t
                    last = dve.scalar_tensor_tensor(acc[:, tile, :], be2[:, e, :], comb[:, tile, e:e + 1],
                                                    acc[:, tile, :], ALU.mult, ALU.add)
                last.then_inc(bias2.sem, 1)

            with dve.Fori(0, BATCH) as b:
                w = Where(dve, b, "S1")
                dve.wait_ge(x_ld.sem, x_ld.at(w, 0))
                dve.wait_ge(stored.sem, stored.at(w, -1))
                norm(w, 0, stage, rows)
                split_norm(w)
                for n in range(8):
                    low_qk_s1(w, n)
                row_max(w, 0, 0, 0)
                row_max(w, 1, 1, 0)
                for g in range(4):
                    stage_values(w, g)
                attention(w, 0, 0, 0, 0, 0, 0, (0, 1), None, {}, {}, stage, False)

                w = Where(dve, b, "PRO")
                dve.wait_ge(acc_done.sem, acc_done.at(w, -1))
                dve.tensor_tensor(acc[:, :, :], acc[:, :, :], stage[:, :, :], ALU.add).then_inc(added.sem, 1)
                dve.wait_ge(added.sem, added.at(w, 0))
                norm(w, 0, acc, x1)
                dve.wait_ge(norm_rows.sem, norm_rows.at(w, 7))
                norm(w, 1, x1, rows)
                dve.tensor_tensor(acc[:, :, :], x1[:, :, :], bo[:, :, :].to_broadcast([P, NT, D]), ALU.add).then_inc(added.sem, 1)
                split_norm(w)
                rotate(w, 0)
                rotate(w, 1)
                stage_values(w, 0)
                stage_values(w, 1)
                rotate(w, 2)
                stage_values(w, 2)
                stage_values(w, 3)
                rotate(w, 3)
                dve.wait_ge(added.sem, added.at(w, 1))
                row_max(w, 0, 0, 0)
                row_max(w, 1, 1, 0)

                with dve.Fori(0, PAIRS - 1) as it:
                    w = Where(dve, b, "BODY", it)
                    attention(w, 0, 0, 0, 0, 0, 0, (0,), 0, {1: -2, 2: -1, 3: 0, 7: 1},
                              {i: g for g, i in enumerate(V_STEPS["A"])}, acc, True)
                    attention(w, 1, 8, NTG, 2, 4, 2, (1,), 1, {1: 2, 2: 3, 3: 4, 7: 5},
                              {i: 2 + g for g, i in enumerate(V_STEPS["B"])}, acc, True)

                w = Where(dve, b, "LAST")
                attention(w, 0, 0, 0, 0, 0, 0, (0,), 0, {1: -2, 2: -1, 3: 0, 7: 1}, {}, acc, True)
                attention(w, 1, 8, NTG, 2, 4, 2, (1,), 1, {}, {}, acc, False)

                w = Where(dve, b, "POST")
                dve.wait_ge(acc_done.sem, acc_done.at(w, -1))
                norm(w, 0, acc, rows)
                split_norm(w)
                dve.wait_ge(gate_mm.sem, gate_mm.at(w, 0))
                gating(w)
                dve.tensor_tensor(acc[:, :, :], acc[:, :, :], x1[:, :, :], ALU.add).then_inc(added.sem, 1)
                dve.wait_ge(added.sem, added.at(w, 0))
                dve.wait_ge(be2_ld.sem, be2_ld.at(w, 0))
                high_mid(w, 0)
                high_mid(w, 1)
                for u in range(8):
                    if u < 7:
                        high_mid(w, 2 * u + 2)
                        high_mid(w, 2 * u + 3)
                    mix(w, u)
                dve.wait_ge(bias2.sem, bias2.at(w, 7))
                norm(w, 1, acc, rows)

        @block.tensor
        def _(pe):
            pe.wait_ge(const_done, 3)
            pe.wait_ge(const_ld, 16 * SETUP_DMAS)

            def product(out, lhs, rhs, first, last):
                for k, (x, y) in enumerate(((0, 0), (0, 1), (1, 0))):
                    ins = pe.matmul(out, lhs[x], rhs[y], start=first and k == 0, stop=last and k == 2)
                return ins

            def norm_transpose(w, first_row):
                for u in range(4):
                    c, k = u // 2, u % 2
                    pe.wait_ge(norm_rows.sem, norm_rows.at(w, first_row + TC * (c + 1) - 1))
                    for t in range(TC):
                        last = pe.transpose(ps_s[:, u, t * P:(t + 1) * P], rows[:, TC * c + t, k * P:(k + 1) * P], ident[:, :])
                    last.then_inc(norm_T.sem, 1)

            def shared_bank(w, use):
                n = w.place(use)
                if n >= 2:
                    read, m = last_reader(w.section, n - 2)
                    pe.wait_ge(read.sem, read.at(w, m))
                elif w.section in ("BODY", "LAST"):
                    pe.wait_ge(qb_done.sem, qb_done.at(w, n - 2))
                    pe.wait_ge(acc_done.sem, acc_done.at(w, n - 2))
                return ps_m[:, n % 2, :]

            def last_reader(section, n):
                kind = SHARED[section][n][0]
                before = sum(u[0] == kind for u in SHARED[section][:n])
                if kind == "qk":
                    return (s1_lo if section == "S1" else qb_done), before
                return {"v": v_staged, "pv": o_lo, "wo": acc_done, "mid": gelu_done}[kind], before

            def project_qk(w, n):
                h, g = group_of(w, n)
                out = shared_bank(w, ("qk", h, g))
                j, c = g // 2, g % 2
                for k in range(KD):
                    last = product(out, (wqk_hi[:, h, j, k, :], wqk_lo[:, h, j, k, :]),
                                   (hT_hi[:, k, c * CH:(c + 1) * CH], hT_lo[:, k, c * CH:(c + 1) * CH]),
                                   k == 0, k == KD - 1)
                last.then_inc(qk_mm.sem, 1)

            def project_v(w, g):
                out = shared_bank(w, ("v", g))
                for t in range(2):
                    rows_ = slice((2 * g + t) * P, (2 * g + t + 1) * P)
                    for k in range(KD):
                        last = product(out[:, t * D:(t + 1) * D], (hT_hi[:, k, rows_], hT_lo[:, k, rows_]),
                                       (wv_hi[:, k, :], wv_lo[:, k, :]), k == 0, k == KD - 1)
                last.then_inc(v_mm.sem, 1)

            def scores(w, n, i, halves):
                if w.section != "S1" or i >= 2:
                    pe.wait_ge(exp_done.sem, exp_done.at(w, n - 2))
                tile = slice(i * P, (i + 1) * P)
                for piece, (k0, width) in enumerate(KEYS[i]):
                    bank = ps_s[:, i % 2 * 2 + piece, :]
                    diagonal = k0 <= i * P < k0 + width
                    for m, h in enumerate(halves):
                        last = product(bank[:, 0:width], (q_hi[:, h, tile], q_lo[:, h, tile]),
                                       (k_hi[:, h, k0:k0 + width], k_lo[:, h, k0:k0 + width]),
                                       m == 0, m == len(halves) - 1 and not diagonal)
                    if diagonal:
                        last = pe.matmul(bank[:, i * P - k0:(i + 1) * P - k0], ident_bf[:, :], mask_bf[:, :],
                                         start=False, stop=True)
                last.then_inc(s_mm.sem, 1)

            def transposes(w, n, t0, i):
                pe.wait_ge(exp_done.sem, exp_done.at(w, n))
                for j, size in enumerate(TG[i]):
                    m = t0 + TG0[i] + j
                    if w.section != "S1" or m >= 2:
                        pe.wait_ge(t_lo.sem, t_lo.at(w, m - 2))
                    for k in range(size):
                        block_ = 4 * j + k
                        last = pe.transpose(ps_t[:, m % 2, k * P:(k + 1) * P],
                                            prob[:, i % 2, block_ * P:(block_ + 1) * P], ident[:, :])
                    last.then_inc(t_mm.sem, 1)

            def outputs(w, c, h, t0):
                out = shared_bank(w, ("pv", h, c))
                pe.wait_ge(t_lo.sem, t_lo.at(w, t0 + (3, NTG - 1)[c]))
                tiles = TC * (c + 1)
                for j in range(tiles):
                    off = min(max(0, j - TC * c), 2) * P
                    slot = j + (4 if c == 0 else 0)
                    vals = slice(h * HD, (h + 1) * HD)
                    last = product(out[:, off:CH], (v_hi[:, j, vals], v_lo[:, j, vals]),
                                   (pT_hi[:, slot, off:CH], pT_lo[:, slot, off:CH]), j == 0, j == tiles - 1)
                last.then_inc(pv_mm.sem, 1)

            def out_project(w, c, halves, use, pv):
                for g in range(2):
                    out = shared_bank(w, ("wo", use, c, g))
                    if g == 0:
                        pe.wait_ge(o_lo.sem, o_lo.at(w, pv))
                    for t in range(2):
                        tile = slice((2 * g + t) * P, (2 * g + t + 1) * P)
                        for m, h in enumerate(halves):
                            last = product(out[:, t * D:(t + 1) * D], (oT_hi[:, h, tile], oT_lo[:, h, tile]),
                                           (wo_hi[:, h, :], wo_lo[:, h, :]), m == 0, m == len(halves) - 1)
                    last.then_inc(wo_mm.sem, 1)

            def attention(w, halves, use, n0, t0, pv0, fill, ends, ahead, rest, v_ready, wo_ready):
                np_ = len(halves)
                for i in range(NT):
                    if i + 2 == TC and rest is not None:
                        pe.wait_ge(qk_lo_done.sem, qk_lo_done.at(w, rest))
                    if i + 2 < NT:
                        scores(w, n0 + i + 2, i + 2, halves)
                    elif ahead:
                        ahead(i + 2 - NT)
                    if i == TC:
                        v_ready(0)
                        for h in halves:
                            outputs(w, 0, h, t0)
                    if i == TC + 1:
                        wo_ready()
                        out_project(w, 0, halves, use, pv0 + np_ - 1)
                    transposes(w, n0 + i, t0, i)
                    for other in fill.get(i, ()):
                        other()
                for other in ends[:1]:
                    other()
                v_ready(1)
                for h in halves:
                    outputs(w, 1, h, t0)
                for other in ends[1:]:
                    other()
                out_project(w, 1, halves, use, pv0 + 2 * np_ - 1)

            for count in (v_mm, qk_mm, pv_mm, wo_mm):
                pe.sem_inc(count.sem, count.lead)
            with pe.Fori(0, BATCH) as b:
                w = Where(pe, b, "S1")
                norm_transpose(w, 0)
                pe.wait_ge(norm_lo.sem, norm_lo.at(w, 3))
                for n in range(8):
                    if n % 4 == 0:
                        pe.wait_ge(qk_w[n // 4].sem, qk_w[n // 4].at(w, 0))
                    project_qk(w, n)
                pe.wait_ge(s1_lo.sem, s1_lo.at(w, 7))
                scores(w, 0, 0, (0, 1))
                scores(w, 1, 1, (0, 1))
                pe.wait_ge(v_w.sem, v_w.at(w, 0))
                for g in range(4):
                    project_v(w, g)

                def s1_values(c):
                    for h in range(2):
                        pe.wait_ge(v_split[h].sem, v_split[h].at(w, c))

                def s1_weights():
                    for h in range(2):
                        pe.wait_ge(wo_w[h].sem, wo_w[h].at(w, 0))

                attention(w, (0, 1), None, 0, 0, 0, {}, (), None, None, s1_values, s1_weights)

                w = Where(pe, b, "PRO")
                norm_transpose(w, 8)
                pe.wait_ge(norm_lo.sem, norm_lo.at(w, 3))
                pe.wait_ge(qk_w[0].sem, qk_w[0].at(w, 0))
                for n in range(4):
                    project_qk(w, n)
                pe.wait_ge(v_w.sem, v_w.at(w, 0))
                for g in range(4):
                    project_v(w, g)
                pe.wait_ge(qk_lo_done.sem, qk_lo_done.at(w, 1))
                scores(w, 0, 0, (0,))
                scores(w, 1, 1, (0,))
                pe.wait_ge(qk_w[1].sem, qk_w[1].at(w, 0))
                for n in range(4, 6):
                    project_qk(w, n)

                def pair(w, more):
                    def project(n, ready=None):
                        if ready:
                            pe.wait_ge(ready.sem, ready.at(w, 0))
                        project_qk(w, n)

                    def values(g, ready=None):
                        if ready:
                            pe.wait_ge(ready.sem, ready.at(w, 0))
                        project_v(w, g)

                    fill_a = {0: [lambda: project(0)], 1: [lambda: project(1)]}
                    fill_b, ends_a, ends_b = {}, (), ()
                    if more:
                        for g, i in enumerate(V_STEPS["A"]):
                            fill_a[i] = [lambda g=g: values(g, None if g else v_w)]
                        ends_a = (lambda: project(2, qk_w[0]), lambda: project(3))
                        fill_b = {0: [lambda: project(4)], 1: [lambda: project(5)]}
                        for g, i in enumerate(V_STEPS["B"]):
                            fill_b[i] = [lambda g=g: values(2 + g)]
                        ends_b = (lambda: project(6, qk_w[1]), lambda: project(7))

                    def scores_b(i):
                        pe.wait_ge(qk_lo_done.sem, qk_lo_done.at(w, -1))
                        scores(w, 8 + i, i, (1,))

                    def scores_next(i):
                        pe.wait_ge(qk_lo_done.sem, qk_lo_done.at(w, 3))
                        scores(w, 16 + i, i, (0,))

                    attention(w, (0,), 0, 0, 0, 0, fill_a, ends_a, scores_b, -3,
                              lambda c: pe.wait_ge(v_split[0].sem, v_split[0].at(w, c - 2)),
                              lambda: pe.wait_ge(wo_w[0].sem, wo_w[0].at(w, -1)))
                    attention(w, (1,), 1, 8, NTG, 2, fill_b, ends_b, scores_next if more else None, 1,
                              lambda c: pe.wait_ge(v_split[1].sem, v_split[1].at(w, c)),
                              lambda: pe.wait_ge(wo_w[1].sem, wo_w[1].at(w, 0)))

                with pe.Fori(0, PAIRS - 1) as it:
                    pair(Where(pe, b, "BODY", it), True)
                pair(Where(pe, b, "LAST"), False)

                w = Where(pe, b, "POST")
                norm_transpose(w, 0)
                pe.wait_ge(norm_lo.sem, norm_lo.at(w, 3))
                for t in range(NT):
                    for k in range(KD):
                        last = pe.matmul(ps_t[:, 0, t * EXPERTS:(t + 1) * EXPERTS],
                                         hf[:, k, t // TC, t % TC * P:(t % TC + 1) * P], w_gate[:, k, :],
                                         start=(k == 0), stop=(k == KD - 1))
                last.then_inc(gate_mm.sem, 1)
                we1 = [x[:, :, :].rearrange("p h (a n) -> p (h a) n", n=INNER) for x in (q_hi, q_lo)]
                we2 = [x[:, :, :].rearrange("p h (a n) -> p (h a) n", n=D) for x in (k_hi, k_lo)]

                def expert_in(u):
                    c, e = u // EXPERTS, u % EXPERTS
                    for i in range(2):
                        out = shared_bank(w, ("mid", 2 * u + i))
                        for k in range(KD):
                            last = product(out, [x[:, 2 * e + k, i * P:(i + 1) * P] for x in we1],
                                           (hT_hi[:, k, c * CH:(c + 1) * CH], hT_lo[:, k, c * CH:(c + 1) * CH]),
                                           k == 0, k == KD - 1)
                        last.then_inc(mid_mm.sem, 1)

                def expert_out(u):
                    e = u % EXPERTS
                    pe.wait_ge(mid_lo.sem, mid_lo.at(w, 2 * u + 1))
                    for g in range(2):
                        n = 2 * u + g
                        if n >= 4:
                            pe.wait_ge(mixed.sem, mixed.at(w, n - 4))
                        for t in range(2):
                            tile = slice((2 * g + t) * P, (2 * g + t + 1) * P)
                            for i in range(2):
                                slot = (2 * u + i) % 4
                                last = product(ps_s[:, n % 4, t * D:(t + 1) * D],
                                               (pT_hi[:, slot, tile], pT_lo[:, slot, tile]),
                                               [x[:, 2 * e + i, :] for x in we2], i == 0, i == 1)
                        last.then_inc(out_mm.sem, 1)

                pe.wait_ge(we_lo.sem, we_lo.at(w, -1))
                expert_in(0)
                for u in range(8):
                    if u < 7:
                        expert_in(u + 1)
                    if u == 0:
                        pe.wait_ge(we_lo.sem, we_lo.at(w, 0))
                    expert_out(u)


_INS = ["L0_attn_x", "L0_attn_qkv", "L0_attn_o_proj", "L0_attn_gamma", "L0_attn_beta", "L0_ffn_wq", "L0_ffn_bq",
        "L0_ffn_wk", "L0_ffn_bk", "L0_ffn_wv", "L0_ffn_bv", "L0_ffn_wo", "L0_ffn_bo", "L0_ffn_ln1_w", "L0_ffn_ln1_b",
        "L0_ffn_ln2_w", "L0_ffn_ln2_b", "L0_ffn_w_gate", "L0_ffn_we1", "L0_ffn_be1", "L0_ffn_we2", "L0_ffn_be2"]


def _rope_tables():
    inv = (np.float32(1.0) / np.float32(THETA) ** (np.arange(0, HD, 2, dtype=np.float32) / np.float32(HD))).astype(np.float32)
    angle = np.concatenate([inv, inv])[:, None] * np.arange(T, dtype=np.float32)[None, :]
    sign = np.where(np.arange(HD) < HD // 2, -1.0, 1.0).astype(np.float32)[:, None]
    return np.cos(angle).astype(np.float32), (np.sin(angle) * sign).astype(np.float32)


def kernel(**inputs):
    import concourse.bacc as bacc
    from concourse.bass_utils import run_bass_kernel_spmd

    nc = bacc.Bacc("TRN2", target_bir_lowering=False, num_devices=1, dynamic_dma_scratch_size=1024)
    arrays, dram = {}, {}
    cos, sin = _rope_tables()
    for name, a in [(n, inputs[n]) for n in _INS] + [("rope_cos", cos), ("rope_sin", sin)]:
        a = np.ascontiguousarray(a)
        arrays[f"in_{name}"] = a
        dram[name] = nc.dram_tensor(f"in_{name}", a.shape, mybir.dt.from_np(a.dtype), kind="ExternalInput").ap()
    dram["out"] = nc.dram_tensor("out_rows", (BATCH, T, D), F32, kind="ExternalOutput").ap()
    build(nc, dram)
    r = run_bass_kernel_spmd(nc, [arrays], core_ids=[0])
    return r.results[0]["out_rows"]
```

```python
from contextlib import ExitStack

import numpy as np

import concourse.bass as bass
from concourse import mybir

F32 = mybir.dt.float32
F32R = mybir.dt.float32r
BF16 = mybir.dt.bfloat16
ALU = mybir.AluOpType
ACT = mybir.ActivationFunctionType
AX = mybir.AxisListType

P = 128
BATCH, T, D = 2, 1024, 256
NT = T // P
KD = D // P
HEADS, HD = 16, 128
PAIRS = HEADS // 2
EXPERTS, INNER = 4, 256
EPS = 1e-5
CH = 512
NC = T // CH
TC = CH // P
MASKED = -1e30
S1_SCALE = 1.0 / 16.0
HEAD_SCALE = float(1.0 / np.sqrt(HD))
THETA = 10000.0

SECTIONS = ("S1", "PRO", "BODY", "LAST", "POST")

NORM_CHUNKS = {"PRO": (0, 0, 1, 1), "POST": (0, 1, 0, 1)}

TG0 = [0, 1, 2, 3, 4, 6, 8, 10]
TG = [[i + 1] if i < 4 else [4, i - 3] for i in range(NT)]
NTG = 12
KEYS = [[(0, 256)], [(0, 256)], [(0, 384)], [(0, 512)],
        [(0, 512), (512, 256)], [(0, 512), (512, 256)], [(0, 512), (512, 384)], [(0, 512), (512, 512)]]

QK = {
    "S1": [(0, 0), (0, 2), (1, 0), (1, 2), (0, 1), (0, 3), (1, 1), (1, 3)],
    "PRO": [(0, 0), (0, 2), (0, 1), (0, 3), (1, 0), (1, 2)],
    "BODY": [(1, 1), (1, 3), (0, 0), (0, 2), (0, 1), (0, 3), (1, 0), (1, 2)],
    "LAST": [(1, 1), (1, 3)],
}
QK_SLOTS = 4
QK_SLOT0 = {"PRO": 0, "BODY": len(QK["PRO"]) % QK_SLOTS, "LAST": len(QK["PRO"]) % QK_SLOTS}



def _attention_uses(h, fills, ends):
    pv = lambda c: [("pv", x, c) for x in ((0, 1) if h is None else (h,))]
    wo = lambda c: [("wo", h, c, g) for g in range(2)]
    uses = []
    for i in range(NT):
        if i == TC:
            uses += pv(0)
        if i == TC + 1:
            uses += wo(0)
        uses += fills.get(i, [])
    return uses + ends[:1] + pv(1) + ends[1:] + wo(1)


FILL_B = {0: [("qk", 1, 1)], 1: [("qk", 1, 3)]}
FILL_A = {0: [("qk", 0, 1)], 1: [("qk", 0, 3)]}
V_STEPS = {"A": (6, 7), "B": (3, 6)}
SHARED = {
    "S1": [("qk", *x) for x in QK["S1"]] + [("v", g) for g in range(4)] + _attention_uses(None, {}, []),
    "PRO": ([("qk", *x) for x in QK["PRO"][:2]] + [("v", 0), ("v", 1)] + [("qk", *x) for x in QK["PRO"][2:4]]
            + [("v", 2), ("v", 3)] + [("qk", *x) for x in QK["PRO"][4:]]),
    "BODY": _attention_uses(0, {**FILL_B, **{i: [("v", g)] for g, i in enumerate(V_STEPS["A"])}},
                            [("qk", 0, 0), ("qk", 0, 2)])
    + _attention_uses(1, {**FILL_A, **{i: [("v", 2 + g)] for g, i in enumerate(V_STEPS["B"])}},
                      [("qk", 1, 0), ("qk", 1, 2)]),
    "LAST": _attention_uses(0, FILL_B, []) + _attention_uses(1, {}, []),
    "POST": [("mid", n) for n in range(2 * 2 * EXPERTS)],
}


class Count:

    def __init__(self, sem, s1=0, pro=0, body=0, last=0, post=0, step=1, lead=0):
        self.sem, self.body, self.step, self.lead = sem, body, step, lead
        n = dict(zip(SECTIONS, (s1, pro, body * (PAIRS - 1), last, post)))
        self.first = {s: sum(n[x] for x in SECTIONS[:k]) for k, s in enumerate(SECTIONS)}
        self.batch = sum(n.values())

    def at(self, w, n):
        passed = self.lead + self.first[w.section] + n + 1
        assert passed > 0
        return w.base(self.batch * self.step, self.body * self.step) + passed * self.step


class Where:

    def __init__(self, eng, b, section, it=0):
        self.eng, self.b, self.section, self.it, self.known = eng, b, section, it, {}

    def base(self, batch, turn):
        if isinstance(self.b, int):
            return self.b * batch
        if (batch, turn) not in self.known:
            turns = self.it * turn if self.section == "BODY" else 0
            self.known[batch, turn] = self.eng.snap(self.b * batch + turns)
        return self.known[batch, turn]

    def place(self, use):
        return SHARED[self.section].index(use)


def build(nc, A):
    with ExitStack() as ctx:
        def sb(name, shape, dt=F32):
            return ctx.enter_context(nc.sbuf_tensor(name, shape, dt))

        def counted(name, **n):
            return Count(ctx.enter_context(nc.semaphore(name)), **n)

        def sem(name):
            return ctx.enter_context(nc.semaphore(name))

        ps_s = ctx.enter_context(nc.psum_tensor("ps_s", [P, 4, 512], F32))
        ps_t = ctx.enter_context(nc.psum_tensor("ps_t", [P, 2, 512], F32))
        ps_m = ctx.enter_context(nc.psum_tensor("ps_m", [P, 2, 512], F32))

        ident = sb("ident", [P, P])
        ident_bf = sb("ident_bf", [P, P], BF16)
        mask = sb("mask", [P, P])
        mask_bf = sb("mask_bf", [P, P], BF16)
        minus_half = sb("minus_half", [P, NT])
        ones = sb("ones", [P, 1, 1])
        bias_scale = sb("bias_scale", [P, 2])
        held = sb("held", [P, 1])
        cos_t = sb("cos_t", [P, T])
        sin_t = sb("sin_t", [P, T])
        ln_w = sb("ln_w", [P, 3, KD])
        ln_b = sb("ln_b", [P, 3, KD])
        be1 = sb("be1", [P, EXPERTS, 2])
        w_gate = sb("w_gate", [P, KD, EXPERTS])
        bo = sb("bo", [P, 1, D])

        stage = sb("stage", [P, NT, D])
        rows = sb("rows", [P, NT, D])
        acc = sb("acc", [P, NT, D])
        x1 = sb("x1", [P, NT, D])
        hT_hi = sb("hT_hi", [P, KD, T], F32R)
        hT_lo = sb("hT_lo", [P, KD, T], F32R)
        q_hi = sb("q_hi", [P, 2, T], F32R)
        q_lo = sb("q_lo", [P, 2, T], F32R)
        k_hi = sb("k_hi", [P, 2, T], F32R)
        k_lo = sb("k_lo", [P, 2, T], F32R)
        v_hi = sb("v_hi", [P, NT, D], F32R)
        v_lo = sb("v_lo", [P, NT, D], F32R)
        pT_hi = sb("pT_hi", [P, NT, CH], F32R)
        pT_lo = sb("pT_lo", [P, NT, CH], F32R)
        oT_hi = sb("oT_hi", [P, 2, CH], F32R)
        oT_lo = sb("oT_lo", [P, 2, CH], F32R)
        work = sb("work", [P, 8, CH])
        qb, qs = work[:, 0:4, :], work[:, 4:8, :]
        hf = work[:, 0:4, :].rearrange("p (c k) n -> p k c n", k=KD)
        be2 = work[:, 4:6, :].rearrange("p a (e n) -> p (a e) n", n=D)
        gelu = work[:, 6:8, :]
        prob = rows[:, :, :].rearrange("p (r a) n -> p r (a n)", r=2)

        wqk_st = sb("wqk_st", [P, 2, 2, KD, HD])
        wqk_hi = sb("wqk_hi", [P, 2, 2, KD, HD], F32R)
        wqk_lo = sb("wqk_lo", [P, 2, 2, KD, HD], F32R)
        wv_st = sb("wv_st", [P, KD, 2 * HD])
        wv_hi = sb("wv_hi", [P, KD, 2 * HD], F32R)
        wv_lo = sb("wv_lo", [P, KD, 2 * HD], F32R)
        wo_st = sb("wo_st", [P, 2, D])
        wo_hi = sb("wo_hi", [P, 2, D], F32R)
        wo_lo = sb("wo_lo", [P, 2, D], F32R)
        bqk_st = sb("bqk_st", [P, 2, 2])
        bqk = sb("bqk", [P, 2, 2])
        bv = sb("bv", [P, 1, 2 * HD])

        stats = sb("stats", [P, NT, 6])
        mv = sb("mv", [P, NT, 2])
        var = sb("var", [P, NT])
        rstd = sb("rstd", [P, NT])
        nmax = sb("nmax", [P, 2, NT])
        rsum = sb("rsum", [P, 2, NT])
        rinv = sb("rinv", [P, 2, NT])
        logit = sb("logit", [P, NT, EXPERTS])
        prob4 = sb("prob4", [P, NT, EXPERTS])
        beats = sb("beats", [P, NT, EXPERTS, EXPERTS])
        rank = sb("rank", [P, NT, EXPERTS])
        is1 = sb("is1", [P, NT, EXPERTS])
        is2 = sb("is2", [P, NT, EXPERTS])
        g1 = sb("g1", [P, NT, 1])
        g2 = sb("g2", [P, NT, 1])
        g3 = sb("g3", [P, NT, 1])
        g4 = sb("g4", [P, NT, 1])
        e21 = sb("e21", [P, NT, 1])
        comb = sb("comb", [P, NT, EXPERTS])

        const_ld = sem("const_ld")
        const_done = sem("const_done")
        rope_ld = sem("rope_ld")
        x_ld = counted("x_ld", lead=1, s1=1, post=1, step=16)
        x_twice = counted("x_twice", s1=1)
        norm_step = counted("norm_step", pro=12, post=12)
        norm_rstd = counted("norm_rstd", pro=4, post=4)
        norm_rows = counted("norm_rows", pro=16, post=16)
        x_step = counted("x_step", lead=6, post=6)
        x_rstd = counted("x_rstd", lead=2, post=2)
        x_normed = counted("x_normed", lead=8, post=8)
        norm_T = counted("norm_T", s1=4, pro=4, post=4)
        norm_f = counted("norm_f", s1=4, pro=4, post=4)
        norm_hi = counted("norm_hi", s1=4, pro=4, post=4)
        norm_lo = counted("norm_lo", s1=4, pro=4, post=4)
        added = counted("added", pro=NC, post=1)
        qk_ld = [counted("qkA_ld", lead=2, post=2, pro=4, body=4, step=16),
                 counted("qkB_ld", lead=2, post=2, pro=4, body=4, step=16)]
        v_ld = counted("v_ld", lead=1, post=1, pro=2, body=2, step=16)
        wo_ld = [counted("woA_ld", lead=1, post=1, pro=1, body=1, step=16),
                 counted("woB_ld", lead=1, post=1, body=1, last=1, step=16)]
        qk_w_hi = [counted("qkA_w_hi", s1=1, pro=1, body=1), counted("qkB_w_hi", s1=1, pro=1, body=1)]
        qk_w = [counted("qkA_w", lead=1, s1=1, pro=1, body=1), counted("qkB_w", lead=1, s1=1, pro=1, body=1)]
        v_w_hi = counted("v_w_hi", s1=1, pro=1, body=1)
        v_w = counted("v_w", lead=1, s1=1, pro=1, body=1)
        wo_w_hi = [counted("woA_w_hi", s1=1, pro=1, body=1), counted("woB_w_hi", s1=1, body=1, last=1)]
        wo_w = [counted("woA_w", lead=1, s1=1, pro=1, body=1), counted("woB_w", lead=1, s1=1, body=1, last=1)]
        qk_mm = counted("qk_mm", lead=1, s1=8, pro=6, body=8, last=2)
        s1_hi = counted("s1_hi", s1=8)
        s1_lo = counted("s1_lo", s1=8)
        qb_done = counted("qb_done", pro=6, body=8, last=2)

        def slots(section):
            return [(QK_SLOT0[section] + n) % QK_SLOTS for n in range(len(QK[section]))]

        swapped = [counted(f"swapped_{x}", step=16, **{s.lower(): 2 * slots(s).count(x) for s in QK_SLOT0})
                   for x in range(QK_SLOTS)]
        rot_done = counted("rot_done", pro=6, body=8, last=2)
        cos_done = counted("cos_done", pro=6, body=8, last=2)
        rope_done = counted("rope_done", pro=6, body=8, last=2)
        qk_hi_done = counted("qk_hi_done", pro=6, body=8, last=2)
        qk_lo_done = counted("qk_lo_done", pro=6, body=8, last=2)

        def slot_of(w, n):
            return (QK_SLOT0[w.section] + n) % QK_SLOTS

        def group_of(w, n):
            return QK["BODY" if n < 0 else w.section][n]

        def swap_event(w, n):
            before = sum((QK_SLOT0[w.section] + m) % QK_SLOTS == slot_of(w, n) for m in range(max(n, 0)))
            return 2 * before + 1 if n >= 0 else -1

        v_mm = counted("v_mm", lead=1, s1=4, pro=4, body=4)
        v_staged = counted("v_staged", s1=4, pro=4, body=4)
        v_hi_done = [counted("vA_hi", s1=2, pro=2, body=2), counted("vB_hi", s1=2, body=2, last=2)]
        v_split = [counted("vA_split", s1=2, pro=2, body=2), counted("vB_split", s1=2, body=2, last=2)]
        s_mm = counted("s_mm", s1=8, body=16, last=16)
        max_done = counted("max_done", s1=8, body=16, last=16)
        exp_done = counted("exp_done", s1=8, body=16, last=16)
        t_mm = counted("t_mm", s1=12, body=24, last=24)
        t_hi = counted("t_hi", s1=12, body=24, last=24)
        t_lo = counted("t_lo", s1=12, body=24, last=24)
        pv_mm = counted("pv_mm", lead=1, s1=4, body=4, last=4)
        o_hi = counted("o_hi", s1=4, body=4, last=4)
        o_lo = counted("o_lo", s1=4, body=4, last=4)
        rinv_done = counted("rinv_done", s1=2, body=4, last=4)
        wo_mm = counted("wo_mm", lead=1, s1=4, body=8, last=8)
        acc_done = counted("acc_done", s1=4, body=8, last=8)
        we_ld = counted("we_ld", last=1, post=1, step=16)
        we_hi = counted("we_hi", last=1, post=1)
        we_lo = counted("we_lo", lead=1, last=1, post=1)
        be2_ld = counted("be2_ld", post=2, step=16)
        gate_mm = counted("gate_mm", post=NC)
        gate_in = counted("gate_in", post=2)
        gate_exp = counted("gate_exp", post=2)
        GATE_LINKS = 23
        gate_link = counted("gate_link", post=GATE_LINKS)
        mid_mm = counted("mid_mm", post=16)
        gelu_done = counted("gelu_done", post=16)
        mid_hi = counted("mid_hi", post=16)
        mid_lo = counted("mid_lo", post=16)
        out_mm = counted("out_mm", post=16)
        mixed = counted("mixed", lead=3, post=16)
        bias2 = counted("bias2", post=8)
        stored = counted("stored", lead=NC, post=NC, step=16)

        block = ctx.enter_context(nc.Block())
        SETUP_DMAS = 9

        @block.sync
        def _(sp):
            w_attn = A["L0_attn_qkv"]

            def first_loads():
                with nc.allow_non_contiguous_dma(reason="a few short vectors, once"):
                    for m, name in enumerate(("attn_gamma", "ffn_ln1_w", "ffn_ln2_w")):
                        sp.dma_start(ln_w[:, m, :], A["L0_" + name].rearrange("(k p) -> p k", p=P)).then_inc(const_ld, 16)
                    for m, name in enumerate(("attn_beta", "ffn_ln1_b", "ffn_ln2_b")):
                        sp.dma_start(ln_b[:, m, :], A["L0_" + name].rearrange("(k p) -> p k", p=P)).then_inc(const_ld, 16)
                    sp.dma_start(be1[:, :, :].rearrange("p e i -> p (e i)"),
                                 A["L0_ffn_be1"].rearrange("e (i p) -> p (e i)", p=P)).then_inc(const_ld, 16)
                    sp.dma_start(w_gate[:, :, :], A["L0_ffn_w_gate"].rearrange("(k p) e -> p k e", p=P)).then_inc(const_ld, 16)
                    sp.dma_start(bo[:, 0, :], A["L0_ffn_bo"].partition_broadcast(P)).then_inc(const_ld, 16)
                for dst, src in ((cos_t[:, :], A["rope_cos"]), (sin_t[:, :], A["rope_sin"])):
                    sp.dma_start(dst, src).then_inc(rope_ld, 16)

            def at(offset):
                return offset if isinstance(offset, int) else sp.snap(offset)

            def load_qk(w, h, head):
                cols = bass.ds(at(head * HD), HD)
                sp.wait_ge(qk_w[h].sem, qk_w[h].at(w, -1))
                sp.dma_start(wqk_st[:, h, 0], A["L0_ffn_wq"][:, cols].rearrange("(k p) n -> p k n", p=P)).then_inc(qk_ld[h].sem, 16)
                sp.dma_start(wqk_st[:, h, 1], A["L0_ffn_wk"][:, cols].rearrange("(k p) n -> p k n", p=P)).then_inc(qk_ld[h].sem, 16)
                sp.dma_start(bqk_st[:, h, 0:1], A["L0_ffn_bq"][cols].unsqueeze(1)).then_inc(qk_ld[h].sem, 16)
                sp.dma_start(bqk_st[:, h, 1:2], A["L0_ffn_bk"][cols].unsqueeze(1)).then_inc(qk_ld[h].sem, 16)

            def load_v(w, pair):
                cols = bass.ds(at(pair * 2 * HD), 2 * HD)
                sp.wait_ge(v_staged.sem, v_staged.at(w, -1))
                sp.dma_start(wv_st[:, :, :], A["L0_ffn_wv"][:, cols].rearrange("(k p) n -> p k n", p=P)).then_inc(v_ld.sem, 16)
                sp.dma_start(bv[:, 0, :], A["L0_ffn_bv"][cols].partition_broadcast(P)).then_inc(v_ld.sem, 16)

            def load_wo(w, h, head):
                rows_ = bass.ds(at(head * HD), HD)
                sp.wait_ge(wo_w[h].sem, wo_w[h].at(w, -1))
                sp.dma_start(wo_st[:, h, :], A["L0_ffn_wo"][rows_, :]).then_inc(wo_ld[h].sem, 16)

            def swap(w, n):
                sp.wait_ge(qb_done.sem, qb_done.at(w, n))
                x = slot_of(w, n)
                half = HD // 2
                sp.dma_start(qs[0:half, x, :], qb[half:HD, x, :]).then_inc(swapped[x].sem, 16)
                sp.dma_start(qs[half:HD, x, :], qb[0:half, x, :]).then_inc(swapped[x].sem, 16)

            def x_rows(b):
                return A["L0_attn_x"][bass.ds(b, 1)].rearrange("o (t p) d -> p (o t) d", p=P)

            def load_first_block(w=None):
                for h in range(2):
                    if w:
                        sp.wait_ge(qk_w[h].sem, qk_w[h].at(w, -1))
                    for j in range(2):
                        cols = slice(j * D + h * HD, j * D + (h + 1) * HD)
                        sp.dma_start(wqk_st[:, h, j], w_attn[:, cols].rearrange("(k p) n -> p k n", p=P)).then_inc(qk_ld[h].sem, 16)
                if w:
                    sp.wait_ge(v_w.sem, v_w.at(w, -1))
                sp.dma_start(wv_st[:, :, :], w_attn[:, 2 * D:3 * D].rearrange("(k p) n -> p k n", p=P)).then_inc(v_ld.sem, 16)
                for h in range(2):
                    if w:
                        sp.wait_ge(wo_w[h].sem, wo_w[h].at(w, -1))
                    sp.dma_start(wo_st[:, h, :], A["L0_attn_o_proj"][h * P:(h + 1) * P, :]).then_inc(wo_ld[h].sem, 16)

            sp.dma_start(stage[:, :, :], x_rows(0)).then_inc(x_ld.sem, 16)
            load_first_block()
            first_loads()
            sp.sem_inc(stored.sem, 16 * stored.lead)
            with sp.Fori(0, BATCH) as b:
                w = Where(sp, b, "S1")
                b = sp.snap(b)
                this_x = x_rows(b)
                next_x = x_rows(sp.snap(1 - b))
                out_rows = A["out"][bass.ds(b, 1)].rearrange("o (t p) d -> p (o t) d", p=P)
                sp.wait_ge(v_split[1].sem, v_split[1].at(w, 1))
                sp.dma_start(stage[:, :, :], this_x).then_inc(x_ld.sem, 16)
                w = Where(sp, b, "PRO")
                load_qk(w, 0, 0)
                load_v(w, 0)
                load_wo(w, 0, 0)
                load_qk(w, 1, 1)
                for n in range(6):
                    swap(w, n)

                with sp.Fori(0, PAIRS - 1) as it:
                    w = Where(sp, b, "BODY", it)
                    load_v(w, it + 1)
                    load_qk(w, 0, it * 2 + 2)
                    load_wo(w, 1, it * 2 + 1)
                    for n in range(4):
                        swap(w, n)
                    load_qk(w, 1, it * 2 + 3)
                    load_wo(w, 0, it * 2 + 2)
                    for n in range(4, 8):
                        swap(w, n)

                w = Where(sp, b, "LAST")
                load_wo(w, 1, HEADS - 1)
                swap(w, 0)
                swap(w, 1)
                sp.wait_ge(v_split[1].sem, v_split[1].at(w, 1))
                sp.dma_start(stage[:, :, :].rearrange("p (e k) n -> p e k n", k=KD),
                             A["L0_ffn_we1"].rearrange("e (k p) n -> p e k n", p=P)).then_inc(we_ld.sem, 16)

                w = Where(sp, b, "POST")
                sp.wait_ge(we_lo.sem, we_lo.at(w, -1))
                sp.dma_start(stage[:, :, :].rearrange("p (e k) n -> p e k n", k=KD),
                             A["L0_ffn_we2"].rearrange("e (k p) n -> p e k n", p=P)).then_inc(we_ld.sem, 16)
                sp.wait_ge(rope_done.sem, rope_done.at(w, -1))
                first, rest = slice(0, 1), slice(1, EXPERTS)
                sp.dma_start(be2[:, first, :], A["L0_ffn_be2"][first, :].partition_broadcast(P)).then_inc(be2_ld.sem, 16)
                sp.wait_ge(we_lo.sem, we_lo.at(w, 0))
                sp.dma_start(be2[:, rest, :], A["L0_ffn_be2"][rest, :].partition_broadcast(P)).then_inc(be2_ld.sem, 16)
                sp.dma_start(stage[:, :, :], next_x).then_inc(x_ld.sem, 16)
                load_first_block(w)
                for c in range(NC):
                    tiles = slice(TC * c, TC * (c + 1))
                    sp.wait_ge(norm_rows.sem, norm_rows.at(w, 8 + TC * (c + 1) - 1))
                    sp.dma_start(out_rows[:, tiles, :], rows[:, tiles, :]).then_inc(stored.sem, 16)
            sp.wait_ge(stored.sem, 16 * (stored.lead + NC * BATCH))
            for count in (x_ld, *qk_ld, v_ld, *wo_ld):
                sp.wait_ge(count.sem, count.step * (count.lead + count.batch * BATCH))

        @block.gpsimd
        def _(pool):
            pool.memset(ident[:, :], 0.0)
            pool.memset(mask[:, :], 0.0)
            pool.memset(minus_half[:, :], -0.5)
            pool.memset(ones[:, :, :], 1.0)
            pool.memset(bias_scale[:, 0:1], HEAD_SCALE)
            pool.memset(bias_scale[:, 1:2], 1.0)
            pool.memset(beats[:, :, :, :], 0.0)
            pool.memset(pT_hi[:, NT - 1, 2 * P:3 * P].bitcast(F32), 0.0)
            pool.memset(pT_lo[:, NT - 1, 2 * P:3 * P].bitcast(F32), 0.0).then_inc(const_done, 1)
            pool.wait_ge(const_done, 1)
            pool.affine_select(out=ident[:, :], in_=ident[:, :], compare_op=ALU.not_equal, fill=1.0,
                               base=0, pattern=[[-1, P]], channel_multiplier=1)
            pool.affine_select(out=mask[:, :], in_=mask[:, :], compare_op=ALU.is_ge, fill=MASKED,
                               base=0, pattern=[[-1, P]], channel_multiplier=1).then_inc(const_done, 1)
            pool.wait_ge(const_done, 2)
            pool.tensor_copy(ident_bf[:, :], ident[:, :])
            pool.tensor_copy(mask_bf[:, :], mask[:, :]).then_inc(const_done, 1)

            def norm_power(w, n):
                c = NORM_CHUNKS[w.section][n]
                tiles = slice(TC * c, TC * (c + 1))
                pool.wait_ge(norm_step.sem, norm_step.at(w, 3 * n + 2))
                pool.tensor_tensor(rstd[:, tiles], var[:, tiles], minus_half[:, tiles], ALU.pow).then_inc(norm_rstd.sem, 1)

            def scale_biases(w, h, last_dma):
                pool.wait_ge(qk_ld[h].sem, qk_ld[h].at(w, last_dma))
                pool.tensor_tensor(bqk[:, h, :], bqk_st[:, h, :], bias_scale[:, :], ALU.mult)

            def low_qk_weights(w, h):
                pool.wait_ge(qk_w_hi[h].sem, qk_w_hi[h].at(w, 0))
                flat = "p j k n -> p (j k n)"
                pool.tensor_tensor(wqk_lo[:, h].rearrange(flat), wqk_st[:, h].rearrange(flat),
                                   wqk_hi[:, h].rearrange(flat).bitcast(F32), ALU.subtract).then_inc(qk_w[h].sem, 1)

            def low_v_weights(w):
                pool.wait_ge(v_w_hi.sem, v_w_hi.at(w, 0))
                flat = "p k n -> p (k n)"
                pool.tensor_tensor(wv_lo[:, :, :].rearrange(flat), wv_st[:, :, :].rearrange(flat),
                                   wv_hi[:, :, :].rearrange(flat).bitcast(F32), ALU.subtract).then_inc(v_w.sem, 1)

            def low_wo(w, h):
                pool.wait_ge(wo_w_hi[h].sem, wo_w_hi[h].at(w, 0))
                pool.tensor_tensor(wo_lo[:, h], wo_st[:, h], wo_hi[:, h].bitcast(F32), ALU.subtract).then_inc(wo_w[h].sem, 1)

            def low_values(w, h, chunks=range(NC)):
                for c in chunks:
                    pool.wait_ge(v_hi_done[h].sem, v_hi_done[h].at(w, c))
                    tiles, cols = slice(TC * c, TC * (c + 1)), slice(h * HD, (h + 1) * HD)
                    pool.tensor_tensor(v_lo[:, tiles, cols], stage[:, tiles, cols], v_hi[:, tiles, cols].bitcast(F32),
                                       ALU.subtract).then_inc(v_split[h].sem, 1)

            def rotate(w, n):
                x = slot_of(w, n)
                pool.wait_ge(swapped[x].sem, swapped[x].at(w, swap_event(w, n)))
                c = group_of(w, n)[1] % 2
                pool.tensor_tensor(qs[:, x, :], qs[:, x, :], sin_t[:, c * CH:(c + 1) * CH],
                                   ALU.mult).then_inc(rot_done.sem, 1)

            def low_qk(w, n):
                h, g = group_of(w, n)
                pool.wait_ge(qk_hi_done.sem, qk_hi_done.at(w, n))
                hi, lo = ((q_hi, q_lo), (k_hi, k_lo))[g // 2]
                cols = slice(g % 2 * CH, (g % 2 + 1) * CH)
                pool.tensor_tensor(lo[:, h, cols], qb[:, slot_of(w, n), :], hi[:, h, cols].bitcast(F32),
                                   ALU.subtract).then_inc(qk_lo_done.sem, 1)

            def low_expert(w, n):
                pool.wait_ge(we_hi.sem, we_hi.at(w, 0))
                lo = (q_lo, k_lo)[n]
                hi = (q_hi, k_hi)[n]
                pool.tensor_tensor(lo[:, :, :].rearrange("p h n -> p (h n)"), stage[:, :, :].rearrange("p t n -> p (t n)"),
                                   hi[:, :, :].rearrange("p h n -> p (h n)").bitcast(F32),
                                   ALU.subtract).then_inc(we_lo.sem, 1)

            for count in (*qk_w, v_w, *wo_w, we_lo):
                pool.sem_inc(count.sem, count.lead)

            def x_power(w, c, back=0):
                tiles = slice(TC * c, TC * (c + 1))
                pool.wait_ge(x_step.sem, x_step.at(w, 3 * (c - back) + 2))
                pool.tensor_tensor(rstd[:, tiles], var[:, tiles], minus_half[:, tiles], ALU.pow).then_inc(x_rstd.sem, 1)

            for c in range(NC):
                x_power(Where(pool, 0, "S1"), c, 2)
            pool.wait_ge(rope_ld, 32)
            with pool.Fori(0, BATCH) as b:
                w = Where(pool, b, "S1")
                low_qk_weights(w, 0)
                low_qk_weights(w, 1)
                low_v_weights(w)
                low_wo(w, 0)
                low_wo(w, 1)
                for c in range(NC):
                    for h in range(2):
                        low_values(w, h, (c,))
                pool.wait_ge(x_ld.sem, x_ld.at(w, 0))
                pool.tensor_tensor(stage[:, :, :], stage[:, :, :], stage[:, :, :], ALU.add).then_inc(x_twice.sem, 1)

                w = Where(pool, b, "PRO")
                scale_biases(w, 0, 3)
                low_qk_weights(w, 0)
                low_v_weights(w)
                scale_biases(w, 1, 3)
                low_qk_weights(w, 1)
                for n in range(4):
                    norm_power(w, n)
                low_wo(w, 0)
                rotate(w, 0)
                rotate(w, 1)
                low_qk(w, 0)
                low_qk(w, 1)
                rotate(w, 2)
                rotate(w, 3)
                low_values(w, 0)
                low_qk(w, 2)
                low_qk(w, 3)

                with pool.Fori(0, PAIRS - 1) as it:
                    w = Where(pool, b, "BODY", it)
                    rotate(w, -2)
                    rotate(w, -1)
                    low_values(w, 1)
                    rotate(w, 0)
                    low_qk(w, -2)
                    rotate(w, 1)
                    low_qk(w, -1)
                    low_v_weights(w)
                    low_qk(w, 0)
                    scale_biases(w, 0, 3)
                    low_qk_weights(w, 0)
                    low_wo(w, 1)
                    low_qk(w, 1)
                    rotate(w, 2)
                    rotate(w, 3)
                    rotate(w, 4)
                    low_qk(w, 2)
                    rotate(w, 5)
                    low_qk(w, 3)
                    low_qk(w, 4)
                    scale_biases(w, 1, 3)
                    low_qk_weights(w, 1)
                    low_values(w, 0)
                    low_wo(w, 0)
                    low_qk(w, 5)

                w = Where(pool, b, "LAST")
                rotate(w, -2)
                rotate(w, -1)
                low_values(w, 1)
                rotate(w, 0)
                low_qk(w, -2)
                rotate(w, 1)
                low_qk(w, -1)
                low_qk(w, 0)
                low_wo(w, 1)
                low_qk(w, 1)
                low_expert(w, 0)

                w = Where(pool, b, "POST")
                norm_power(w, 0)
                norm_power(w, 1)
                low_expert(w, 1)
                for n in range(16):
                    pool.wait_ge(mid_hi.sem, mid_hi.at(w, n))
                    pool.tensor_tensor(pT_lo[:, n % 4, :], gelu[:, n % 2, :], pT_hi[:, n % 4, :].bitcast(F32),
                                       ALU.subtract).then_inc(mid_lo.sem, 1)
                    if n == 5:
                        x_power(w, 0)
                    if n == 9:
                        x_power(w, 1)
                    if n == 13:
                        norm_power(w, 2)
                norm_power(w, 3)

        @block.scalar
        def _(act):
            act.wait_ge(const_ld, 16 * SETUP_DMAS)

            def norm_affine(w, m, c):
                for k in range(KD):
                    u = KD * c + k
                    act.wait_ge(norm_T.sem, norm_T.at(w, u))
                    act.activation(hf[:, k, c, :], ps_s[:, u, :], ACT.Identity, bias=ln_b[:, m, k:k + 1],
                                   scale=ln_w[:, m, k:k + 1]).then_inc(norm_f.sem, 1)

            def high_qk_s1(w, n):
                act.wait_ge(qk_mm.sem, qk_mm.at(w, n))
                h, g = group_of(w, n)
                act.activation((q_hi, k_hi)[g // 2][:, h, g % 2 * CH:(g % 2 + 1) * CH], ps_m[:, n % 2, :], ACT.Identity,
                               scale=(S1_SCALE, 1.0)[g // 2]).then_inc(s1_hi.sem, 1)

            def add_bias(w, n):
                h, g = group_of(w, n)
                act.wait_ge(qk_mm.sem, qk_mm.at(w, n))
                if w.section != "PRO" or n >= QK_SLOTS:
                    act.wait_ge(qk_lo_done.sem, qk_lo_done.at(w, n - QK_SLOTS))
                j = g // 2
                act.activation(qb[:, slot_of(w, n), :], ps_m[:, w.place(("qk", h, g)) % 2, :], ACT.Identity,
                               bias=bqk[:, h, j:j + 1], scale=(HEAD_SCALE, 1.0)[j]).then_inc(qb_done.sem, 1)

            def high_qk(w, n):
                h, g = group_of(w, n)
                act.wait_ge(rope_done.sem, rope_done.at(w, n))
                hi = (q_hi, k_hi)[g // 2]
                act.activation(hi[:, h, g % 2 * CH:(g % 2 + 1) * CH], qb[:, slot_of(w, n), :],
                               ACT.Copy).then_inc(qk_hi_done.sem, 1)

            def high_qk_weights(w, h, last_dma, use):
                act.wait_ge(qk_ld[h].sem, qk_ld[h].at(w, last_dma))
                act.wait_ge(qk_mm.sem, qk_mm.at(w, use))
                flat = "p j k n -> p (j k n)"
                act.activation(wqk_hi[:, h].rearrange(flat), wqk_st[:, h].rearrange(flat),
                               ACT.Copy).then_inc(qk_w_hi[h].sem, 1)

            def high_v_weights(w, last_dma):
                act.wait_ge(v_ld.sem, v_ld.at(w, last_dma))
                act.wait_ge(v_mm.sem, v_mm.at(w, -1))
                flat = "p k n -> p (k n)"
                act.activation(wv_hi[:, :, :].rearrange(flat), wv_st[:, :, :].rearrange(flat),
                               ACT.Copy).then_inc(v_w_hi.sem, 1)

            def high_wo(w, h, use):
                act.wait_ge(wo_ld[h].sem, wo_ld[h].at(w, -1 if w.section == "S1" else 0))
                act.wait_ge(wo_mm.sem, wo_mm.at(w, use))
                act.activation(wo_hi[:, h], wo_st[:, h], ACT.Copy).then_inc(wo_w_hi[h].sem, 1)

            def high_values(w, h, c, staged, used):
                act.wait_ge(pv_mm.sem, pv_mm.at(w, used))
                act.wait_ge(v_staged.sem, v_staged.at(w, staged))
                tiles, cols = slice(TC * c, TC * (c + 1)), slice(h * HD, (h + 1) * HD)
                act.activation(v_hi[:, tiles, cols], stage[:, tiles, cols], ACT.Copy).then_inc(v_hi_done[h].sem, 1)

            def exponent(w, n, i, a):
                act.wait_ge(max_done.sem, max_done.at(w, n))
                if i >= 2:
                    act.wait_ge(t_mm.sem, t_mm.at(w, (n - i) // 8 * NTG + TG0[i - 1] - 1))
                elif w.section != "S1":
                    act.wait_ge(t_mm.sem, t_mm.at(w, (n - i) // 8 * NTG - (1 if i else 3)))
                k = (i + 1) * P
                act.activation(prob[:, i % 2, 0:k], ps_s[:, :, :].rearrange("p a n -> p (a n)")[:, i % 2 * T:i % 2 * T + k],
                               ACT.Exp, bias=nmax[:, a, i:i + 1], accum_out=rsum[:, a, i:i + 1]).then_inc(exp_done.sem, 1)

            def high_p(w, t0, i):
                for j, size in enumerate(TG[i]):
                    n = t0 + TG0[i] + j
                    act.wait_ge(t_mm.sem, t_mm.at(w, n))
                    first = 4 * j + (4 if i < 4 else 0)
                    act.activation(pT_hi[:, first:first + size, i % 4 * P:(i % 4 + 1) * P],
                                   ps_t[:, n % 2, 0:size * P].rearrange("p (j q) -> p j q", q=P),
                                   ACT.Copy).then_inc(t_hi.sem, 1)

            def high_o(w, n, h, use):
                act.wait_ge(pv_mm.sem, pv_mm.at(w, n))
                act.activation(oT_hi[:, h, :], ps_m[:, w.place(use) % 2, :], ACT.Copy).then_inc(o_hi.sem, 1)

            def attention(w, a, n0, t0, pv0, outs, others, ends, late, ahead):
                for i in range(NT):
                    if i + 1 < NT:
                        exponent(w, n0 + i + 1, i + 1, a)
                    elif ahead:
                        exponent(w, n0 + NT, 0, 1 - a)
                    if i == TC:
                        for j, (h, use) in enumerate(outs):
                            high_o(w, pv0 + j, h, ("pv", use, 0))
                    high_p(w, t0, i)
                    for other in others.get(i, ()):
                        other()
                for n in ends[:1]:
                    add_bias(w, n)
                if late is not None:
                    high_qk(w, late)
                for j, (h, use) in enumerate(outs):
                    high_o(w, pv0 + len(outs) + j, h, ("pv", use, 1))
                for n in ends[1:]:
                    add_bias(w, n)

            def high_expert(w, n):
                act.wait_ge(we_ld.sem, we_ld.at(w, 0))
                if n == 0:
                    act.wait_ge(s_mm.sem, s_mm.at(w, 15))
                hi = (q_hi, k_hi)[n]
                act.activation(hi[:, :, :].rearrange("p h n -> p (h n)"), stage[:, :, :].rearrange("p t n -> p (t n)"),
                               ACT.Copy).then_inc(we_hi.sem, 1)

            def gelu_mid(w, n):
                act.wait_ge(mid_mm.sem, mid_mm.at(w, n))
                if n >= 2:
                    act.wait_ge(mid_lo.sem, mid_lo.at(w, n - 2))
                act.activation(gelu[:, n % 2, :], ps_m[:, n % 2, :], ACT.Gelu,
                               bias=be1[:, n // 2 % EXPERTS, n % 2:n % 2 + 1]).then_inc(gelu_done.sem, 1)

            def high_mid(w, n):
                act.wait_ge(gelu_done.sem, gelu_done.at(w, n))
                if n >= 4:
                    act.wait_ge(out_mm.sem, out_mm.at(w, 2 * (n // 2 - 2) + 1))
                act.activation(pT_hi[:, n % 4, :], gelu[:, n % 2, :], ACT.Copy).then_inc(mid_hi.sem, 1)

            with act.Fori(0, BATCH) as b:
                w = Where(act, b, "S1")
                high_qk_weights(w, 0, -1, -1)
                high_qk_weights(w, 1, -1, -1)
                high_v_weights(w, -1)
                norm_affine(w, 0, 0)
                norm_affine(w, 0, 1)
                high_wo(w, 0, -1)
                high_wo(w, 1, -1)
                for n in range(8):
                    high_qk_s1(w, n)
                act.wait_ge(stored.sem, stored.at(w, -1))
                exponent(w, 0, 0, 0)
                values = {c: [lambda h=h, c=c: high_values(w, h, c, 2 * c + 1, -1) for h in range(2)] for c in range(NC)}
                pro = Where(act, b, "PRO")
                ahead = {6: [lambda: high_qk_weights(pro, 0, 3, -1), lambda: high_v_weights(pro, 1)],
                         7: [lambda: high_qk_weights(pro, 1, 3, -1)]}
                attention(w, 0, 0, 0, 0, [(0, 0), (1, 1)], {**values, **ahead}, (), None, False)

                w = pro
                norm_affine(w, 1, 0)
                high_wo(w, 0, -1)
                add_bias(w, 0)
                add_bias(w, 1)
                norm_affine(w, 1, 1)
                high_values(w, 0, 0, 1, -1)
                high_qk(w, 0)
                high_qk(w, 1)
                add_bias(w, 2)
                add_bias(w, 3)
                high_values(w, 0, 1, 3, -1)
                exponent(w, 0, 0, 0)
                add_bias(w, 4)
                high_qk(w, 2)
                add_bias(w, 5)
                high_qk(w, 3)

                def beside_a(w, more):
                    steps = {
                        0: [lambda: add_bias(w, 0), lambda: high_values(w, 1, 0, -1, -1)],
                        1: [lambda: add_bias(w, 1), lambda: high_values(w, 1, 1, -1, -1)],
                        2: [lambda: high_qk(w, -2)],
                        3: [lambda: high_qk(w, -1)],
                        4: [lambda: high_qk(w, 0)],
                        6: [lambda: high_wo(w, 1, -1)],
                    }
                    if more:
                        steps[3].append(lambda: high_v_weights(w, 1))
                        steps[5] = [lambda: high_qk_weights(w, 0, 3, -1)]
                    return steps

                def beside_b(w):
                    return {
                        0: [lambda: add_bias(w, 4)],
                        1: [lambda: add_bias(w, 5)],
                        2: [lambda: high_qk(w, 2)],
                        3: [lambda: high_qk(w, 3)],
                        4: [lambda: high_qk(w, 4)],
                        5: [lambda: high_qk_weights(w, 1, 3, 1)],
                        6: [lambda: high_values(w, 0, 0, 1, 1)],
                        7: [lambda: high_values(w, 0, 1, 3, 1), lambda: high_wo(w, 0, 3)],
                    }

                with act.Fori(0, PAIRS - 1) as it:
                    w = Where(act, b, "BODY", it)
                    attention(w, 0, 0, 0, 0, [(0, 0)], beside_a(w, True), (2, 3), 1, True)
                    attention(w, 1, 8, NTG, 2, [(1, 1)], beside_b(w), (6, 7), 5, True)

                w = Where(act, b, "LAST")
                attention(w, 0, 0, 0, 0, [(0, 0)], beside_a(w, False), (), 1, True)
                attention(w, 1, 8, NTG, 2, [(1, 1)], {6: [lambda: high_expert(w, 0)]}, (), None, False)

                w = Where(act, b, "POST")
                norm_affine(w, 2, 0)
                high_expert(w, 1)
                norm_affine(w, 2, 1)
                for half in (gelu_mid, high_mid):
                    half(w, 0)
                    half(w, 1)
                act.wait_ge(gate_in.sem, gate_in.at(w, 0))
                act.activation(prob4[:, :, :], logit[:, :, :], ACT.Exp).then_inc(gate_exp.sem, 1)
                act.wait_ge(gate_in.sem, gate_in.at(w, 1))
                act.activation(e21[:, :, :], g1[:, :, :], ACT.Exp).then_inc(gate_exp.sem, 1)
                for u in range(1, 8):
                    for half in (gelu_mid, high_mid):
                        half(w, 2 * u)
                        half(w, 2 * u + 1)

        @block.vector
        def _(dve):
            dve.wait_ge(const_ld, 16 * SETUP_DMAS)
            dve.wait_ge(const_done, 3)

            def norm_stats(w, n, src):
                c = NORM_CHUNKS[w.section][n]
                tiles = range(TC * c, TC * (c + 1))
                for t in tiles:
                    last = dve.bn_stats(stats[:, t, :], src[:, t, :])
                last.then_inc(norm_step.sem, 1)
                dve.wait_ge(norm_step.sem, norm_step.at(w, 3 * n))
                dve.tensor_copy(held[:, 0:1], minus_half[:, 0:1])
                for t in tiles:
                    last = dve.bn_aggr(mv[:, t, :], stats[:, t, :])
                last.then_inc(norm_step.sem, 1)
                dve.wait_ge(norm_step.sem, norm_step.at(w, 3 * n + 1))
                dve.tensor_scalar(var[:, TC * c:TC * (c + 1)], mv[:, TC * c:TC * (c + 1), 1], EPS, None,
                                  ALU.add).then_inc(norm_step.sem, 1)

            def norm_apply(w, n, src, dst):
                c = NORM_CHUNKS[w.section][n]
                dve.wait_ge(norm_rstd.sem, norm_rstd.at(w, n))
                for t in range(TC * c, TC * (c + 1)):
                    dve.tensor_scalar(dst[:, t, :], src[:, t, :], mv[:, t, 0:1], rstd[:, t:t + 1],
                                      ALU.subtract, ALU.mult).then_inc(norm_rows.sem, 1)

            def x_stats(w, c, back=0):
                tiles = range(TC * c, TC * (c + 1))
                step = 3 * (c - back)
                for t in tiles:
                    last = dve.bn_stats(stats[:, t, :], stage[:, t, :])
                last.then_inc(x_step.sem, 1)
                dve.wait_ge(x_step.sem, x_step.at(w, step))
                dve.tensor_copy(held[:, 0:1], minus_half[:, 0:1])
                for t in tiles:
                    last = dve.bn_aggr(mv[:, t, :], stats[:, t, :])
                last.then_inc(x_step.sem, 1)
                dve.wait_ge(x_step.sem, x_step.at(w, step + 1))
                dve.tensor_scalar(var[:, TC * c:TC * (c + 1)], mv[:, TC * c:TC * (c + 1), 1], EPS, None,
                                  ALU.add).then_inc(x_step.sem, 1)

            def x_apply(w, c, back=0):
                dve.wait_ge(x_rstd.sem, x_rstd.at(w, c - back))
                for t in range(TC * c, TC * (c + 1)):
                    dve.tensor_scalar(stage[:, t, :], stage[:, t, :], mv[:, t, 0:1], rstd[:, t:t + 1],
                                      ALU.subtract, ALU.mult).then_inc(x_normed.sem, 1)

            def norm_between(w, c):
                norm_stats(w, 2 * c, acc)
                norm_apply(w, 2 * c, acc, x1)
                dve.wait_ge(norm_rows.sem, norm_rows.at(w, 8 * c + 3))
                norm_stats(w, 2 * c + 1, x1)
                tiles = slice(TC * c, TC * (c + 1))
                dve.tensor_tensor(acc[:, tiles, :], x1[:, tiles, :], bo[:, :, :].to_broadcast([P, TC, D]),
                                  ALU.add).then_inc(added.sem, 1)
                norm_apply(w, 2 * c + 1, x1, rows)

            def split_norm(w, c):
                for k in range(KD):
                    u = KD * c + k
                    dve.wait_ge(norm_f.sem, norm_f.at(w, u))
                    dve.tensor_copy(hT_hi[:, k, c * CH:(c + 1) * CH], hf[:, k, c, :]).then_inc(norm_hi.sem, 1)
                for k in range(KD):
                    u = KD * c + k
                    dve.wait_ge(norm_hi.sem, norm_hi.at(w, u))
                    dve.tensor_tensor(hT_lo[:, k, c * CH:(c + 1) * CH], hf[:, k, c, :],
                                      hT_hi[:, k, c * CH:(c + 1) * CH].bitcast(F32), ALU.subtract).then_inc(norm_lo.sem, 1)

            def low_qk_s1(w, n):
                dve.wait_ge(s1_hi.sem, s1_hi.at(w, n))
                h, g = group_of(w, n)
                hi, lo = ((q_hi, q_lo), (k_hi, k_lo))[g // 2]
                cols = slice(g % 2 * CH, (g % 2 + 1) * CH)
                dve.scalar_tensor_tensor(lo[:, h, cols], ps_m[:, n % 2, :], (S1_SCALE, 1.0)[g // 2],
                                         hi[:, h, cols].bitcast(F32), ALU.mult,
                                         ALU.subtract).then_inc(s1_lo.sem, 1)

            def stage_values(w, g):
                dve.wait_ge(v_mm.sem, v_mm.at(w, g))
                src = ps_m[:, w.place(("v", g)) % 2, :].rearrange("p (t n) -> p t n", n=D)
                dst = stage[:, 2 * g:2 * g + 2, :]
                if w.section == "S1":
                    dve.tensor_copy(dst, src).then_inc(v_staged.sem, 1)
                else:
                    dve.tensor_tensor(dst, src, bv[:, :, :].to_broadcast([P, 2, D]), ALU.add).then_inc(v_staged.sem, 1)

            def rotate(w, n):
                x, c = slot_of(w, n), group_of(w, n)[1] % 2
                dve.wait_ge(rot_done.sem, rot_done.at(w, n))
                dve.tensor_tensor(qb[:, x, :], qb[:, x, :], cos_t[:, c * CH:(c + 1) * CH],
                                  ALU.mult).then_inc(cos_done.sem, 1)
                dve.wait_ge(cos_done.sem, cos_done.at(w, n))
                dve.tensor_tensor(qb[:, x, :], qb[:, x, :], qs[:, x, :], ALU.add).then_inc(rope_done.sem, 1)

            def row_max(w, n, i, a):
                dve.wait_ge(s_mm.sem, s_mm.at(w, n))
                k = (i + 1) * P
                dve.tensor_reduce(nmax[:, a, i:i + 1], ps_s[:, :, :].rearrange("p a n -> p (a n)")[:, i % 2 * T:i % 2 * T + k],
                                  AX.X, ALU.max, negate=True).then_inc(max_done.sem, 1)

            def low_p(w, t0, i):
                for j, size in enumerate(TG[i]):
                    n = t0 + TG0[i] + j
                    dve.wait_ge(t_hi.sem, t_hi.at(w, n))
                    first = 4 * j + (4 if i < 4 else 0)
                    part = (slice(None), slice(first, first + size), slice(i % 4 * P, (i % 4 + 1) * P))
                    dve.tensor_tensor(pT_lo[part], ps_t[:, n % 2, 0:size * P].rearrange("p (j q) -> p j q", q=P),
                                      pT_hi[part].bitcast(F32), ALU.subtract).then_inc(t_lo.sem, 1)

            def low_o(w, n, h, use):
                dve.wait_ge(o_hi.sem, o_hi.at(w, n))
                dve.tensor_tensor(oT_lo[:, h, :], ps_m[:, w.place(use) % 2, :], oT_hi[:, h, :].bitcast(F32),
                                  ALU.subtract).then_inc(o_lo.sem, 1)

            def invert(w, a, c, r0):
                dve.wait_ge(exp_done.sem, exp_done.at(w, (r0 // 2) * NT + TC * c + TC - 1))
                dve.reciprocal(rinv[:, a, TC * c:TC * (c + 1)], rsum[:, a, TC * c:TC * (c + 1)]).then_inc(rinv_done.sem, 1)
                reciprocals, twice = rinv_done.at(w, r0 + c), x_twice.at(w, 0)
                dve.wait_ge(rinv_done.sem, reciprocals)
                if w.section == "S1":
                    dve.wait_ge(x_twice.sem, twice)

            def accumulate(w, a, c, wo0, r0, use, base, groups=(0, 1)):
                if 0 in groups:
                    invert(w, a, c, r0)
                for g in groups:
                    n = wo0 + 2 * c + g
                    dve.wait_ge(wo_mm.sem, wo_mm.at(w, n))
                    if w.section != "S1":
                        dve.wait_ge(acc_done.sem, acc_done.at(w, n - 4))
                    for t in range(2):
                        tile = TC * c + 2 * g + t
                        last = dve.scalar_tensor_tensor(
                            acc[:, tile, :], ps_m[:, w.place(("wo", use, c, g)) % 2, t * D:(t + 1) * D],
                            rinv[:, a, tile:tile + 1], base[:, tile, :], ALU.mult, ALU.add)
                    last.then_inc(acc_done.sem, 1)

            def attention(w, a, n0, t0, pv0, wo0, r0, outs, use, ropes, values, base, ahead, norms=()):
                for i in range(NT):
                    if i + 2 < NT:
                        row_max(w, n0 + i + 2, i + 2, a)
                    elif ahead:
                        row_max(w, n0 + i + 2, i + 2 - NT, 1 - a)
                    if i == TC:
                        for j, h in enumerate(outs):
                            low_o(w, pv0 + j, h, ("pv", h, 0))
                    if i == TC + 1:
                        accumulate(w, a, 0, wo0, r0, use, base, (0,))
                    low_p(w, t0, i)
                    if i == TC + 1:
                        accumulate(w, a, 0, wo0, r0, use, base, (1,))
                    if i in values:
                        if values[i] == 0:
                            dve.wait_ge(v_split[1].sem, v_split[1].at(w, 1))
                        stage_values(w, values[i])
                    if i in ropes:
                        rotate(w, ropes[i])
                for step in norms[:1]:
                    step()
                for j, h in enumerate(outs):
                    low_o(w, pv0 + len(outs) + j, h, ("pv", h, 1))
                for step in norms[1:]:
                    step()
                accumulate(w, a, 1, wo0, r0, use, base)

            def gating(w):
                links = [0]

                def link(ins):
                    ins.then_inc(gate_link.sem, 1)
                    dve.wait_ge(gate_link.sem, gate_link.at(w, links[0]))
                    links[0] += 1

                wide = [P, NT, EXPERTS]
                link(dve.tensor_copy(logit[:, :, :], ps_t[:, 0, 0:NT * EXPERTS].rearrange("p (t e) -> p t e", e=EXPERTS)))
                link(dve.tensor_reduce(g1[:, :, :], logit[:, :, :], AX.X, ALU.max))
                dve.tensor_tensor(logit[:, :, :], logit[:, :, :], g1[:, :, :].to_broadcast(wide),
                                  ALU.subtract).then_inc(gate_in.sem, 1)
                dve.wait_ge(gate_exp.sem, gate_exp.at(w, 0))
                link(dve.tensor_reduce(g2[:, :, :], prob4[:, :, :], AX.X, ALU.add))
                link(dve.reciprocal(g3[:, :, :], g2[:, :, :]))
                link(dve.tensor_tensor(prob4[:, :, :], prob4[:, :, :], g3[:, :, :].to_broadcast(wide), ALU.mult))
                for a in range(EXPERTS):
                    if a:
                        link(dve.tensor_tensor(beats[:, :, 0:a, a], prob4[:, :, a:a + 1].to_broadcast([P, NT, a]),
                                               prob4[:, :, 0:a], ALU.is_gt))
                    if a + 1 < EXPERTS:
                        link(dve.tensor_tensor(beats[:, :, a + 1:, a], prob4[:, :, a:a + 1].to_broadcast([P, NT, EXPERTS - 1 - a]),
                                               prob4[:, :, a + 1:], ALU.is_ge))
                link(dve.tensor_reduce(rank[:, :, :], beats[:, :, :, :], AX.X, ALU.add))
                link(dve.tensor_scalar(is1[:, :, :], rank[:, :, :], 0.0, None, ALU.is_equal))
                link(dve.tensor_scalar(is2[:, :, :], rank[:, :, :], 1.0, None, ALU.is_equal))
                link(dve.tensor_tensor(rank[:, :, :], prob4[:, :, :], is2[:, :, :], ALU.mult))
                link(dve.tensor_reduce(g4[:, :, :], rank[:, :, :], AX.X, ALU.add))
                link(dve.tensor_reduce(g2[:, :, :], prob4[:, :, :], AX.X, ALU.max))
                dve.tensor_tensor(g1[:, :, :], g4[:, :, :], g2[:, :, :], ALU.subtract).then_inc(gate_in.sem, 1)
                dve.wait_ge(gate_exp.sem, gate_exp.at(w, 1))
                link(dve.tensor_scalar(g2[:, :, :], e21[:, :, :], 1.0, None, ALU.add))
                link(dve.reciprocal(g3[:, :, :], g2[:, :, :]))
                link(dve.tensor_tensor(g4[:, :, :], e21[:, :, :], g3[:, :, :], ALU.mult))
                link(dve.tensor_tensor(is1[:, :, :], is1[:, :, :], g3[:, :, :].to_broadcast(wide), ALU.mult))
                link(dve.tensor_tensor(is2[:, :, :], is2[:, :, :], g4[:, :, :].to_broadcast(wide), ALU.mult))
                link(dve.tensor_tensor(comb[:, :, :], is1[:, :, :], is2[:, :, :], ALU.add))
                assert links[0] == GATE_LINKS, links

            def mix(w, u):
                c, e = u // EXPERTS, u % EXPERTS
                if u:
                    dve.wait_ge(mixed.sem, mixed.at(w, 2 * u - 1))
                for t in range(TC):
                    tile = TC * c + t
                    last = dve.scalar_tensor_tensor(acc[:, tile, :], be2[:, e, :], comb[:, tile, e:e + 1],
                                                    acc[:, tile, :], ALU.mult, ALU.add)
                last.then_inc(bias2.sem, 1)
                for g in range(2):
                    n = 2 * u + g
                    dve.wait_ge(out_mm.sem, out_mm.at(w, n))
                    if g == 0:
                        dve.wait_ge(bias2.sem, bias2.at(w, u))
                    for t in range(2):
                        tile = TC * c + 2 * g + t
                        last = dve.scalar_tensor_tensor(acc[:, tile, :], ps_s[:, n % 4, t * D:(t + 1) * D],
                                                        comb[:, tile, e:e + 1], acc[:, tile, :], ALU.mult, ALU.add)
                    last.then_inc(mixed.sem, 1)

            dve.sem_inc(mixed.sem, mixed.lead)
            start = Where(dve, 0, "S1")
            dve.wait_ge(x_ld.sem, x_ld.at(start, -1))
            for step in (x_stats, x_apply):
                for c in range(NC):
                    step(start, c, 2)
            dve.wait_ge(rope_ld, 32)
            with dve.Fori(0, BATCH) as b:
                w = Where(dve, b, "S1")
                split_norm(w, 0)
                split_norm(w, 1)
                for n in range(8):
                    low_qk_s1(w, n)
                row_max(w, 0, 0, 0)
                row_max(w, 1, 1, 0)
                for g in range(4):
                    stage_values(w, g)
                pro = Where(dve, b, "PRO")

                def first_between():
                    dve.wait_ge(acc_done.sem, acc_done.at(w, 1))
                    norm_between(pro, 0)

                attention(w, 0, 0, 0, 0, 0, 0, (0, 1), None, {}, {}, stage, False,
                          (first_between, lambda: split_norm(pro, 0)))

                w = pro
                dve.wait_ge(acc_done.sem, acc_done.at(w, -1))
                norm_between(w, 1)
                stage_values(w, 0)
                stage_values(w, 1)
                split_norm(w, 1)
                rotate(w, 0)
                rotate(w, 1)
                stage_values(w, 2)
                stage_values(w, 3)
                row_max(w, 0, 0, 0)
                dve.wait_ge(added.sem, added.at(w, 1))
                row_max(w, 1, 1, 0)
                rotate(w, 2)
                rotate(w, 3)

                with dve.Fori(0, PAIRS - 1) as it:
                    w = Where(dve, b, "BODY", it)
                    attention(w, 0, 0, 0, 0, 0, 0, (0,), 0, {1: -2, 2: -1, 3: 0, 7: 1},
                              {i: g for g, i in enumerate(V_STEPS["A"])}, acc, True)
                    attention(w, 1, 8, NTG, 2, 4, 2, (1,), 1, {1: 2, 2: 3, 3: 4, 7: 5},
                              {i: 2 + g for g, i in enumerate(V_STEPS["B"])}, acc, True)

                w = Where(dve, b, "LAST")
                attention(w, 0, 0, 0, 0, 0, 0, (0,), 0, {1: -2, 2: -1, 3: 0, 7: 1}, {}, acc, True)
                post = Where(dve, b, "POST")

                def first_rows():
                    dve.wait_ge(acc_done.sem, acc_done.at(w, 5))
                    norm_stats(post, 0, acc)
                    norm_apply(post, 0, acc, rows)

                attention(w, 1, 8, NTG, 2, 4, 2, (1,), 1, {}, {}, acc, False, (first_rows, lambda: split_norm(post, 0)))

                w = post
                dve.wait_ge(acc_done.sem, acc_done.at(w, -1))
                norm_stats(w, 1, acc)
                norm_apply(w, 1, acc, rows)
                split_norm(w, 1)
                dve.wait_ge(gate_mm.sem, gate_mm.at(w, 1))
                gating(w)
                dve.tensor_tensor(acc[:, :, :], acc[:, :, :], x1[:, :, :], ALU.add).then_inc(added.sem, 1)
                dve.wait_ge(added.sem, added.at(w, 0))
                dve.wait_ge(be2_ld.sem, be2_ld.at(w, 1))
                for u in range(8):
                    mix(w, u)
                    if u == 1:
                        dve.wait_ge(x_ld.sem, x_ld.at(w, 0))
                        x_stats(w, 0)
                    if u == 2:
                        x_apply(w, 0)
                    if u == 3:
                        x_stats(w, 1)
                    if u == 4:
                        x_apply(w, 1)
                    if u == 5:
                        norm_stats(w, 2, acc)
                    if u == 6:
                        norm_apply(w, 2, acc, rows)
                dve.wait_ge(mixed.sem, mixed.at(w, 15))
                norm_stats(w, 3, acc)
                norm_apply(w, 3, acc, rows)

        @block.tensor
        def _(pe):
            pe.wait_ge(const_done, 3)
            pe.wait_ge(const_ld, 16 * SETUP_DMAS)

            def product(out, lhs, rhs, first, last):
                for k, (x, y) in enumerate(((0, 0), (0, 1), (1, 0))):
                    ins = pe.matmul(out, lhs[x], rhs[y], start=first and k == 0, stop=last and k == 2)
                return ins

            def norm_transpose(w, c, n):
                for k in range(KD):
                    pe.wait_ge(norm_rows.sem, norm_rows.at(w, TC * (n + 1) - 1))
                    for t in range(TC):
                        last = pe.transpose(ps_s[:, KD * c + k, t * P:(t + 1) * P],
                                            rows[:, TC * c + t, k * P:(k + 1) * P], ident[:, :])
                    last.then_inc(norm_T.sem, 1)

            def shared_bank(w, use):
                n = w.place(use)
                if n >= 2:
                    read, m = last_reader(w.section, n - 2)
                    pe.wait_ge(read.sem, read.at(w, m))
                elif w.section != "S1":
                    if w.section in ("BODY", "LAST"):
                        pe.wait_ge(qb_done.sem, qb_done.at(w, n - 2))
                    pe.wait_ge(acc_done.sem, acc_done.at(w, n - 2))
                return ps_m[:, n % 2, :]

            def last_reader(section, n):
                kind = SHARED[section][n][0]
                before = sum(u[0] == kind for u in SHARED[section][:n])
                if kind == "qk":
                    return (s1_lo if section == "S1" else qb_done), before
                return {"v": v_staged, "pv": o_lo, "wo": acc_done, "mid": gelu_done}[kind], before

            def project_qk(w, n):
                h, g = group_of(w, n)
                out = shared_bank(w, ("qk", h, g))
                j, c = g // 2, g % 2
                for k in range(KD):
                    last = product(out, (wqk_hi[:, h, j, k, :], wqk_lo[:, h, j, k, :]),
                                   (hT_hi[:, k, c * CH:(c + 1) * CH], hT_lo[:, k, c * CH:(c + 1) * CH]),
                                   k == 0, k == KD - 1)
                last.then_inc(qk_mm.sem, 1)

            def project_v(w, g):
                out = shared_bank(w, ("v", g))
                for t in range(2):
                    rows_ = slice((2 * g + t) * P, (2 * g + t + 1) * P)
                    for k in range(KD):
                        last = product(out[:, t * D:(t + 1) * D], (hT_hi[:, k, rows_], hT_lo[:, k, rows_]),
                                       (wv_hi[:, k, :], wv_lo[:, k, :]), k == 0, k == KD - 1)
                last.then_inc(v_mm.sem, 1)

            def scores(w, n, i, halves):
                if w.section != "S1" or i >= 2:
                    pe.wait_ge(exp_done.sem, exp_done.at(w, n - 2))
                tile = slice(i * P, (i + 1) * P)
                for piece, (k0, width) in enumerate(KEYS[i]):
                    bank = ps_s[:, i % 2 * 2 + piece, :]
                    diagonal = k0 <= i * P < k0 + width
                    for m, h in enumerate(halves):
                        last = product(bank[:, 0:width], (q_hi[:, h, tile], q_lo[:, h, tile]),
                                       (k_hi[:, h, k0:k0 + width], k_lo[:, h, k0:k0 + width]),
                                       m == 0, m == len(halves) - 1 and not diagonal)
                    if diagonal:
                        last = pe.matmul(bank[:, i * P - k0:(i + 1) * P - k0], ident_bf[:, :], mask_bf[:, :],
                                         start=False, stop=True)
                last.then_inc(s_mm.sem, 1)

            def transposes(w, n, t0, i):
                pe.wait_ge(exp_done.sem, exp_done.at(w, n))
                for j, size in enumerate(TG[i]):
                    m = t0 + TG0[i] + j
                    if w.section != "S1" or m >= 2:
                        pe.wait_ge(t_lo.sem, t_lo.at(w, m - 2))
                    for k in range(size):
                        block_ = 4 * j + k
                        last = pe.transpose(ps_t[:, m % 2, k * P:(k + 1) * P],
                                            prob[:, i % 2, block_ * P:(block_ + 1) * P], ident[:, :])
                    last.then_inc(t_mm.sem, 1)

            def outputs(w, c, h, t0):
                out = shared_bank(w, ("pv", h, c))
                pe.wait_ge(t_lo.sem, t_lo.at(w, t0 + (3, NTG - 1)[c]))
                tiles = TC * (c + 1)
                for j in range(tiles):
                    off = min(max(0, j - TC * c), 2) * P
                    slot = j + (4 if c == 0 else 0)
                    vals = slice(h * HD, (h + 1) * HD)
                    last = product(out[:, off:CH], (v_hi[:, j, vals], v_lo[:, j, vals]),
                                   (pT_hi[:, slot, off:CH], pT_lo[:, slot, off:CH]), j == 0, j == tiles - 1)
                last.then_inc(pv_mm.sem, 1)

            def out_project(w, c, halves, use, pv):
                for g in range(2):
                    out = shared_bank(w, ("wo", use, c, g))
                    if g == 0:
                        pe.wait_ge(o_lo.sem, o_lo.at(w, pv))
                    for t in range(2):
                        tile = slice((2 * g + t) * P, (2 * g + t + 1) * P)
                        for m, h in enumerate(halves):
                            last = product(out[:, t * D:(t + 1) * D], (oT_hi[:, h, tile], oT_lo[:, h, tile]),
                                           (wo_hi[:, h, :], wo_lo[:, h, :]), m == 0, m == len(halves) - 1)
                    last.then_inc(wo_mm.sem, 1)

            def attention(w, halves, use, n0, t0, pv0, fill, ends, ahead, rest, v_ready, wo_ready, next_norm=()):
                np_ = len(halves)
                for i in range(NT):
                    if i + 2 == TC and rest is not None:
                        pe.wait_ge(qk_lo_done.sem, qk_lo_done.at(w, rest))
                    if i + 2 < NT:
                        scores(w, n0 + i + 2, i + 2, halves)
                    elif ahead:
                        ahead(i + 2 - NT)
                    if i == TC:
                        v_ready(0)
                        for h in halves:
                            outputs(w, 0, h, t0)
                    if i == TC + 1:
                        wo_ready()
                        out_project(w, 0, halves, use, pv0 + np_ - 1)
                    transposes(w, n0 + i, t0, i)
                    for other in fill.get(i, ()):
                        other()
                for other in ends[:1]:
                    other()
                v_ready(1)
                for h in halves:
                    outputs(w, 1, h, t0)
                for other in (*ends[1:], *next_norm):
                    other()
                out_project(w, 1, halves, use, pv0 + 2 * np_ - 1)

            for count in (v_mm, qk_mm, pv_mm, wo_mm):
                pe.sem_inc(count.sem, count.lead)
            with pe.Fori(0, BATCH) as b:
                w = Where(pe, b, "S1")
                for c in range(NC):
                    pe.wait_ge(mixed.sem, mixed.at(w, 2 * c - 3))
                    for k in range(KD):
                        pe.wait_ge(x_normed.sem, x_normed.at(w, TC * (c + 1) - 9))
                        for t in range(TC):
                            last = pe.transpose(ps_s[:, KD * c + k, t * P:(t + 1) * P],
                                                stage[:, TC * c + t, k * P:(k + 1) * P], ident[:, :])
                        last.then_inc(norm_T.sem, 1)
                for n in range(8):
                    if n % 4 == 0:
                        pe.wait_ge(norm_lo.sem, norm_lo.at(w, 2 * (n // 4) + 1))
                    if n in (0, 2):
                        pe.wait_ge(qk_w[n // 2].sem, qk_w[n // 2].at(w, 0))
                    project_qk(w, n)
                pe.wait_ge(s1_lo.sem, s1_lo.at(w, 3))
                scores(w, 0, 0, (0, 1))
                scores(w, 1, 1, (0, 1))
                pe.wait_ge(s1_lo.sem, s1_lo.at(w, 7))
                pe.wait_ge(v_w.sem, v_w.at(w, 0))
                for g in range(4):
                    project_v(w, g)

                def s1_values(c):
                    for h in range(2):
                        pe.wait_ge(v_split[h].sem, v_split[h].at(w, c))

                def s1_weights():
                    for h in range(2):
                        pe.wait_ge(wo_w[h].sem, wo_w[h].at(w, 0))

                pro = Where(pe, b, "PRO")
                attention(w, (0, 1), None, 0, 0, 0, {}, (), None, None, s1_values, s1_weights,
                          (lambda: norm_transpose(pro, 0, 1),))

                w = pro
                pe.wait_ge(qk_w[0].sem, qk_w[0].at(w, 0))
                pe.wait_ge(v_w.sem, v_w.at(w, 0))
                for c in range(NC):
                    if c:
                        norm_transpose(w, c, 3)
                    pe.wait_ge(norm_lo.sem, norm_lo.at(w, KD * c + 1))
                    project_qk(w, 2 * c)
                    project_qk(w, 2 * c + 1)
                    project_v(w, 2 * c)
                    project_v(w, 2 * c + 1)
                pe.wait_ge(qk_lo_done.sem, qk_lo_done.at(w, 1))
                scores(w, 0, 0, (0,))
                scores(w, 1, 1, (0,))
                pe.wait_ge(qk_w[1].sem, qk_w[1].at(w, 0))
                for n in range(4, 6):
                    project_qk(w, n)

                def pair(w, more, next_norm=()):
                    def project(n, ready=None):
                        if ready:
                            pe.wait_ge(ready.sem, ready.at(w, 0))
                        project_qk(w, n)

                    def values(g, ready=None):
                        if ready:
                            pe.wait_ge(ready.sem, ready.at(w, 0))
                        project_v(w, g)

                    fill_a = {0: [lambda: project(0)], 1: [lambda: project(1)]}
                    fill_b, ends_a, ends_b = {}, (), ()
                    if more:
                        for g, i in enumerate(V_STEPS["A"]):
                            fill_a[i] = [lambda g=g: values(g, None if g else v_w)]
                        ends_a = (lambda: project(2, qk_w[0]), lambda: project(3))
                        fill_b = {0: [lambda: project(4)], 1: [lambda: project(5)]}
                        for g, i in enumerate(V_STEPS["B"]):
                            fill_b[i] = [lambda g=g: values(2 + g)]
                        ends_b = (lambda: project(6, qk_w[1]), lambda: project(7))

                    def scores_b(i):
                        pe.wait_ge(qk_lo_done.sem, qk_lo_done.at(w, -1))
                        scores(w, 8 + i, i, (1,))

                    def scores_next(i):
                        pe.wait_ge(qk_lo_done.sem, qk_lo_done.at(w, 3))
                        scores(w, 16 + i, i, (0,))

                    attention(w, (0,), 0, 0, 0, 0, fill_a, ends_a, scores_b, -3,
                              lambda c: pe.wait_ge(v_split[0].sem, v_split[0].at(w, c - 2)),
                              lambda: pe.wait_ge(wo_w[0].sem, wo_w[0].at(w, -1)))
                    attention(w, (1,), 1, 8, NTG, 2, fill_b, ends_b, scores_next if more else None, 1,
                              lambda c: pe.wait_ge(v_split[1].sem, v_split[1].at(w, c)),
                              lambda: pe.wait_ge(wo_w[1].sem, wo_w[1].at(w, 0)), next_norm)

                with pe.Fori(0, PAIRS - 1) as it:
                    pair(Where(pe, b, "BODY", it), True)
                post = Where(pe, b, "POST")
                pair(Where(pe, b, "LAST"), False, (lambda: norm_transpose(post, 0, 0),))

                w = post

                def gate_logits(c):
                    pe.wait_ge(norm_f.sem, norm_f.at(w, KD * c + 1))
                    for t in range(TC * c, TC * (c + 1)):
                        for k in range(KD):
                            last = pe.matmul(ps_t[:, 0, t * EXPERTS:(t + 1) * EXPERTS],
                                             hf[:, k, c, t % TC * P:(t % TC + 1) * P], w_gate[:, k, :],
                                             start=(k == 0), stop=(k == KD - 1))
                    last.then_inc(gate_mm.sem, 1)

                we1 = [x[:, :, :].rearrange("p h (a n) -> p (h a) n", n=INNER) for x in (q_hi, q_lo)]
                we2 = [x[:, :, :].rearrange("p h (a n) -> p (h a) n", n=D) for x in (k_hi, k_lo)]

                def expert_in(u):
                    c, e = u // EXPERTS, u % EXPERTS
                    for i in range(2):
                        out = shared_bank(w, ("mid", 2 * u + i))
                        for k in range(KD):
                            last = product(out, [x[:, 2 * e + k, i * P:(i + 1) * P] for x in we1],
                                           (hT_hi[:, k, c * CH:(c + 1) * CH], hT_lo[:, k, c * CH:(c + 1) * CH]),
                                           k == 0, k == KD - 1)
                        last.then_inc(mid_mm.sem, 1)

                def expert_out(u):
                    e = u % EXPERTS
                    pe.wait_ge(mid_lo.sem, mid_lo.at(w, 2 * u + 1))
                    for g in range(2):
                        n = 2 * u + g
                        if n >= 4:
                            pe.wait_ge(mixed.sem, mixed.at(w, n - 4))
                        for t in range(2):
                            tile = slice((2 * g + t) * P, (2 * g + t + 1) * P)
                            for i in range(2):
                                slot = (2 * u + i) % 4
                                last = product(ps_s[:, n % 4, t * D:(t + 1) * D],
                                               (pT_hi[:, slot, tile], pT_lo[:, slot, tile]),
                                               [x[:, 2 * e + i, :] for x in we2], i == 0, i == 1)
                        last.then_inc(out_mm.sem, 1)

                gate_logits(0)
                pe.wait_ge(norm_lo.sem, norm_lo.at(w, 1))
                pe.wait_ge(we_lo.sem, we_lo.at(w, -1))
                expert_in(0)
                norm_transpose(w, 1, 1)
                gate_logits(1)
                for u in range(8):
                    if u + 1 == EXPERTS:
                        pe.wait_ge(norm_lo.sem, norm_lo.at(w, 3))
                    if u < 7:
                        expert_in(u + 1)
                    if u == 0:
                        pe.wait_ge(we_lo.sem, we_lo.at(w, 0))
                    expert_out(u)


_INS = ["L0_attn_x", "L0_attn_qkv", "L0_attn_o_proj", "L0_attn_gamma", "L0_attn_beta", "L0_ffn_wq", "L0_ffn_bq",
        "L0_ffn_wk", "L0_ffn_bk", "L0_ffn_wv", "L0_ffn_bv", "L0_ffn_wo", "L0_ffn_bo", "L0_ffn_ln1_w", "L0_ffn_ln1_b",
        "L0_ffn_ln2_w", "L0_ffn_ln2_b", "L0_ffn_w_gate", "L0_ffn_we1", "L0_ffn_be1", "L0_ffn_we2", "L0_ffn_be2"]


def _rope_tables():
    inv = (np.float32(1.0) / np.float32(THETA) ** (np.arange(0, HD, 2, dtype=np.float32) / np.float32(HD))).astype(np.float32)
    angle = np.concatenate([inv, inv])[:, None] * np.arange(T, dtype=np.float32)[None, :]
    sign = np.where(np.arange(HD) < HD // 2, -1.0, 1.0).astype(np.float32)[:, None]
    return np.cos(angle).astype(np.float32), (np.sin(angle) * sign).astype(np.float32)


def kernel(**inputs):
    import concourse.bacc as bacc
    from concourse.bass_utils import run_bass_kernel_spmd

    nc = bacc.Bacc("TRN2", target_bir_lowering=False, num_devices=1, dynamic_dma_scratch_size=1024)
    arrays, dram = {}, {}
    cos, sin = _rope_tables()
    for name, a in [(n, inputs[n]) for n in _INS] + [("rope_cos", cos), ("rope_sin", sin)]:
        a = np.ascontiguousarray(a)
        arrays[f"in_{name}"] = a
        dram[name] = nc.dram_tensor(f"in_{name}", a.shape, mybir.dt.from_np(a.dtype), kind="ExternalInput").ap()
    dram["out"] = nc.dram_tensor("out_rows", (BATCH, T, D), F32, kind="ExternalOutput").ap()
    build(nc, dram)
    r = run_bass_kernel_spmd(nc, [arrays], core_ids=[0])
    return r.results[0]["out_rows"]
```
